# Optimizing a Trainium2 kernel written in Bass

```python
import numpy as np
import jax
import jax.numpy as jnp

def _softmax(x, axis=-1):
    return jax.nn.softmax(x, axis=axis)

def _gelu(x):
    return jax.nn.gelu(x, approximate=True)

def _silu(x):
    return jax.nn.silu(x)

def _sigmoid(x):
    return jax.nn.sigmoid(x)

def _layernorm(x, axis=-1, eps=1e-05):
    m = jnp.mean(x, axis=axis, keepdims=True)
    v = jnp.var(x, axis=axis, keepdims=True)
    return (x - m) / jnp.sqrt(v + eps)

def _scatter_add(tgt, idx, src, axis=0):
    return tgt.at[idx].add(src)

def _segment_sum(src, seg, n):
    return jax.ops.segment_sum(src, seg, n)
kernel_name = 'mk_cond_seq_d4_seqx_r2_28f49e'

def setup_inputs(seed: int=0):
    np.random.seed(seed)
    _w = jnp.asarray

    def _rec_inputs():
        import jax
        import jax.numpy as jnp
        _rk = jax.random.key(seed)
        x = -0.0003929 + 0.9999 * jax.random.normal(jax.random.fold_in(_rk, 1), (8, 512, 512), jnp.float32)
        _lenS = 512 - jax.random.randint(jax.random.fold_in(_rk, 7), (8,), 0, max(1, 512 // 4) + 1, jnp.int32)
        _lenS2 = 512 - jax.random.randint(jax.random.fold_in(_rk, 8), (8,), 0, max(1, 512 // 4) + 1, jnp.int32)
        cond_2048 = 0.00782532 + 1.00527 * jax.random.normal(jax.random.fold_in(_rk, 11), (8, 1024), jnp.float32)
        cond_1024 = 0.00786388 + 1.0143 * jax.random.normal(jax.random.fold_in(_rk, 15), (8, 512), jnp.float32)
        _validS = jnp.arange(512)[None, :] < _lenS[:, None]
        _validS2 = jnp.arange(512)[None, :] < _lenS2[:, None]
        _causal = jnp.tril(jnp.ones((512, 512), dtype=bool))
        mask_BxS_ik0 = jnp.where(jnp.broadcast_to(_validS[:, :], (8, 512)), 0, 1).astype(jnp.int32)
        mask_BxSx1_fk1 = jnp.where(jnp.ones((8, 512, 1), dtype=bool), 1.0, 0.0).astype(jnp.float32)
        mask_BxS_ff1 = jnp.where(jnp.ones((8, 512), dtype=bool), 1.0, 0.0).astype(jnp.float32)
        return (x, cond_2048, cond_1024, mask_BxS_ik0, mask_BxSx1_fk1, mask_BxS_ff1)
    x, cond_2048, cond_1024, mask_BxS_ik0, mask_BxSx1_fk1, mask_BxS_ff1 = _rec_inputs()

    def _L0_cond_setup():
        import jax, jax.numpy as jnp
        import numpy as np
        H = 16
        LN_EPS = 1e-05

        def _layernorm(x, scale, bias):
            mu = jnp.mean(x, axis=-1, keepdims=True)
            var = jnp.var(x, axis=-1, keepdims=True)
            return (x - mu) * jax.lax.rsqrt(var + LN_EPS) * scale + bias
        key = jax.random.key(seed)
        ks = jax.random.split(key, 8)
        B, T, D, E = (4, 2048, 512, 1024)
        s = 0.02
        return {'x': jax.random.normal(ks[0], (B, T, D), jnp.float32), 'emb': jax.random.normal(ks[1], (B, E), jnp.float32), 'src_mask': jax.random.randint(ks[2], (B, T), 0, 2).astype(jnp.int32), 'norm_scale': jnp.ones((D,), jnp.float32), 'norm_bias': jnp.zeros((D,), jnp.float32), 'Wq': jax.random.normal(ks[3], (D, D), jnp.float32) * s, 'bq': jnp.zeros((D,), jnp.float32), 'Wk': jax.random.normal(ks[4], (D, D), jnp.float32) * s, 'bk': jnp.zeros((D,), jnp.float32), 'Wv': jax.random.normal(ks[5], (D, D), jnp.float32) * s, 'bv': jnp.zeros((D,), jnp.float32), 'film_emb_W': jax.random.normal(ks[6], (E, 2 * D), jnp.float32) * s, 'film_emb_b': jnp.zeros((2 * D,), jnp.float32), 'film_norm_scale': jnp.ones((D,), jnp.float32), 'film_norm_bias': jnp.zeros((D,), jnp.float32), 'film_out_W': jax.random.normal(ks[7], (D, D), jnp.float32) * s, 'film_out_b': jnp.zeros((D,), jnp.float32)}
    _L0_cond_all = _L0_cond_setup()
    _L0_cond_in = {k: v for k, v in _L0_cond_all.items() if k in ('norm_scale', 'norm_bias', 'Wq', 'bq', 'Wk', 'bk', 'Wv', 'bv', 'film_emb_W', 'film_emb_b', 'film_norm_scale', 'film_norm_bias', 'film_out_W', 'film_out_b')}
    del _L0_cond_all

    def _L1_cond_setup():
        import jax, jax.numpy as jnp
        import numpy as np
        B, T, D, H, TE = (4, 1024, 512, 8, 1024)
        EPS = 1e-05

        def _ln(x, w, b):
            m = jnp.mean(x, axis=-1, keepdims=True)
            v = jnp.mean((x - m) ** 2, axis=-1, keepdims=True)
            return (x - m) * jax.lax.rsqrt(v + EPS) * w + b
        key = jax.random.key(seed)
        ks = jax.random.split(key, 16)
        s = 0.02
        inp = {'x': jax.random.normal(ks[0], (B, T, D), jnp.float32), 'emb': jax.random.normal(ks[1], (B, TE), jnp.float32), 'src_mask': (jax.random.uniform(ks[2], (B, T, 1)) > 0.2).astype(jnp.float32), 'num_head': H, 'ln_w': jnp.ones((D,), jnp.float32), 'ln_b': jnp.zeros((D,), jnp.float32), 'Wq': jax.random.normal(ks[3], (D, D), jnp.float32) * s, 'bq': jnp.zeros((D,), jnp.float32), 'Wk': jax.random.normal(ks[4], (D, D), jnp.float32) * s, 'bk': jnp.zeros((D,), jnp.float32), 'Wv': jax.random.normal(ks[5], (D, D), jnp.float32) * s, 'bv': jnp.zeros((D,), jnp.float32), 'W_emb': jax.random.normal(ks[6], (TE, 2 * D), jnp.float32) * s, 'b_emb': jnp.zeros((2 * D,), jnp.float32), 'ln2_w': jnp.ones((D,), jnp.float32), 'ln2_b': jnp.zeros((D,), jnp.float32), 'W_out': jax.random.normal(ks[7], (D, D), jnp.float32) * s, 'b_out': jnp.zeros((D,), jnp.float32)}
        return inp
    _L1_cond_all = _L1_cond_setup()
    _L1_cond_in = {k: v for k, v in _L1_cond_all.items() if k in ('ln_w', 'ln_b', 'Wq', 'bq', 'Wk', 'bk', 'Wv', 'bv', 'W_emb', 'b_emb', 'ln2_w', 'ln2_b', 'W_out', 'b_out')}
    del _L1_cond_all

    def _L2_cond_setup():
        import jax, jax.numpy as jnp
        import numpy as np
        B, T, D, H, TE = (8, 512, 512, 16, 1024)
        LN_EPS = 1e-05

        def layer_norm(x, w, b):
            m = jnp.mean(x, axis=-1, keepdims=True)
            v = jnp.var(x, axis=-1, keepdims=True)
            return (x - m) / jnp.sqrt(v + LN_EPS) * w + b
        key = jax.random.key(seed)
        ks = jax.random.split(key, 8)
        s = lambda k, sh: jax.random.normal(k, sh, jnp.float32) * 0.02
        return dict(x=jax.random.normal(ks[0], (B, T, D), jnp.float32), emb=jax.random.normal(ks[1], (B, TE), jnp.float32), src_mask=jnp.ones((B, T), jnp.float32), norm_w=jnp.ones((D,), jnp.float32), norm_b=jnp.zeros((D,), jnp.float32), q_w=s(ks[2], (D, D)), q_b=jnp.zeros((D,), jnp.float32), k_w=s(ks[3], (D, D)), k_b=jnp.zeros((D,), jnp.float32), v_w=s(ks[4], (D, D)), v_b=jnp.zeros((D,), jnp.float32), emb_w=s(ks[5], (TE, 2 * D)), emb_b=jnp.zeros((2 * D,), jnp.float32), sb_norm_w=jnp.ones((D,), jnp.float32), sb_norm_b=jnp.zeros((D,), jnp.float32), out_w=s(ks[6], (D, D)), out_b=jnp.zeros((D,), jnp.float32))
    _L2_cond_all = _L2_cond_setup()
    _L2_cond_in = {k: v for k, v in _L2_cond_all.items() if k in ('norm_w', 'norm_b', 'q_w', 'q_b', 'k_w', 'k_b', 'v_w', 'v_b', 'emb_w', 'emb_b', 'sb_norm_w', 'sb_norm_b', 'out_w', 'out_b')}
    del _L2_cond_all

    def _L3_cond_setup():
        import jax, jax.numpy as jnp
        import numpy as np
        B, S, D, E, N, R = (2, 512, 512, 1024, 16, 64)
        EPS = 1e-05

        def _ln(x, g, b):
            m = jnp.mean(x, -1, keepdims=True)
            v = jnp.mean((x - m) ** 2, -1, keepdims=True)
            return (x - m) * jax.lax.rsqrt(v + EPS) * g + b

        def _ssm(u, Wdbc, Wdt, bdt, Alog, Dp):
            dbc = jnp.einsum('bse,re->bsr', u, Wdbc)
            dlt, Bm, Cm = jnp.split(dbc, [R, R + N], axis=-1)
            delta = jax.nn.softplus(jnp.einsum('bsr,er->bse', dlt, Wdt) + bdt)
            A = -jnp.exp(Alog)
            dA = jnp.exp(delta[..., None] * A)
            dBu = delta[..., None] * Bm[:, :, None, :] * u[..., None]

            def step(h, xs):
                dA_t, dBu_t, C_t = xs
                h = dA_t * h + dBu_t
                y = jnp.einsum('ben,bn->be', h, C_t)
                return (h, y)
            h0 = jnp.zeros((u.shape[0], u.shape[2], N), u.dtype)
            _, ys = jax.lax.scan(step, h0, (dA.swapaxes(0, 1), dBu.swapaxes(0, 1), Cm.swapaxes(0, 1)))
            return ys.swapaxes(0, 1) + u * Dp
        key = jax.random.key(seed)
        ks = jax.random.split(key, 16)
        f = lambda k, sh, s=0.02: jax.random.normal(k, sh, jnp.float32) * s
        Alog = jnp.log(jnp.tile(jnp.arange(1, N + 1, dtype=jnp.float32), (E, 1)))
        return dict(x=f(ks[0], (B, S, D), 1.0), c=f(ks[1], (B, 2 * D), 1.0), w=f(ks[2], (B, D), 1.0), norm1_g=jnp.ones((D,)), norm1_b=jnp.zeros((D,)), norm2_g=jnp.ones((D,)), norm2_b=jnp.zeros((D,)), Wx=f(ks[3], (E, D)), bx=jnp.zeros((E,)), Wz=f(ks[4], (E, D)), bz=jnp.zeros((E,)), Wf=f(ks[5], (D, E)), bf=jnp.zeros((D,)), Wada=f(ks[6], (3 * D, 2 * D)), bada=jnp.zeros((3 * D,)), Wc1=f(ks[7], (E, E)), bc1=jnp.zeros((E,)), Wc2=f(ks[8], (E, E)), bc2=jnp.zeros((E,)), Wdbc1=f(ks[9], (R + 2 * N, E)), Wdt1=f(ks[10], (E, R)), bdt1=jnp.zeros((E,)), Alog1=Alog, Dp1=jnp.ones((E,)), Wdbc2=f(ks[11], (R + 2 * N, E)), Wdt2=f(ks[12], (E, R)), bdt2=jnp.zeros((E,)), Alog2=Alog, Dp2=jnp.ones((E,)))
    _L3_cond_all = _L3_cond_setup()
    _L3_cond_in = {k: v for k, v in _L3_cond_all.items() if k in ('norm1_g', 'norm1_b', 'norm2_g', 'norm2_b', 'Wx', 'bx', 'Wz', 'bz', 'Wf', 'bf', 'Wada', 'bada', 'Wc1', 'bc1', 'Wc2', 'bc2', 'Wdbc1', 'Wdt1', 'bdt1', 'Alog1', 'Dp1', 'Wdbc2', 'Wdt2', 'bdt2', 'Alog2', 'Dp2')}
    del _L3_cond_all
    return {'x': x, 'cond_2048': cond_2048, 'cond_1024': cond_1024, 'mask_BxS_ik0': mask_BxS_ik0, 'mask_BxSx1_fk1': mask_BxSx1_fk1, 'mask_BxS_ff1': mask_BxS_ff1, 'L0_cond_norm_scale': _L0_cond_in['norm_scale'], 'L0_cond_norm_bias': _L0_cond_in['norm_bias'], 'L0_cond_Wq': _L0_cond_in['Wq'], 'L0_cond_bq': _L0_cond_in['bq'], 'L0_cond_Wk': _L0_cond_in['Wk'], 'L0_cond_bk': _L0_cond_in['bk'], 'L0_cond_Wv': _L0_cond_in['Wv'], 'L0_cond_bv': _L0_cond_in['bv'], 'L0_cond_film_emb_W': _L0_cond_in['film_emb_W'], 'L0_cond_film_emb_b': _L0_cond_in['film_emb_b'], 'L0_cond_film_norm_scale': _L0_cond_in['film_norm_scale'], 'L0_cond_film_norm_bias': _L0_cond_in['film_norm_bias'], 'L0_cond_film_out_W': _L0_cond_in['film_out_W'], 'L0_cond_film_out_b': _L0_cond_in['film_out_b'], 'L1_cond_ln_w': _L1_cond_in['ln_w'], 'L1_cond_ln_b': _L1_cond_in['ln_b'], 'L1_cond_Wq': _L1_cond_in['Wq'], 'L1_cond_bq': _L1_cond_in['bq'], 'L1_cond_Wk': _L1_cond_in['Wk'], 'L1_cond_bk': _L1_cond_in['bk'], 'L1_cond_Wv': _L1_cond_in['Wv'], 'L1_cond_bv': _L1_cond_in['bv'], 'L1_cond_W_emb': _L1_cond_in['W_emb'], 'L1_cond_b_emb': _L1_cond_in['b_emb'], 'L1_cond_ln2_w': _L1_cond_in['ln2_w'], 'L1_cond_ln2_b': _L1_cond_in['ln2_b'], 'L1_cond_W_out': _L1_cond_in['W_out'], 'L1_cond_b_out': _L1_cond_in['b_out'], 'L2_cond_norm_w': _L2_cond_in['norm_w'], 'L2_cond_norm_b': _L2_cond_in['norm_b'], 'L2_cond_q_w': _L2_cond_in['q_w'], 'L2_cond_q_b': _L2_cond_in['q_b'], 'L2_cond_k_w': _L2_cond_in['k_w'], 'L2_cond_k_b': _L2_cond_in['k_b'], 'L2_cond_v_w': _L2_cond_in['v_w'], 'L2_cond_v_b': _L2_cond_in['v_b'], 'L2_cond_emb_w': _L2_cond_in['emb_w'], 'L2_cond_emb_b': _L2_cond_in['emb_b'], 'L2_cond_sb_norm_w': _L2_cond_in['sb_norm_w'], 'L2_cond_sb_norm_b': _L2_cond_in['sb_norm_b'], 'L2_cond_out_w': _L2_cond_in['out_w'], 'L2_cond_out_b': _L2_cond_in['out_b'], 'L3_cond_norm1_g': _L3_cond_in['norm1_g'], 'L3_cond_norm1_b': _L3_cond_in['norm1_b'], 'L3_cond_norm2_g': _L3_cond_in['norm2_g'], 'L3_cond_norm2_b': _L3_cond_in['norm2_b'], 'L3_cond_Wx': _L3_cond_in['Wx'], 'L3_cond_bx': _L3_cond_in['bx'], 'L3_cond_Wz': _L3_cond_in['Wz'], 'L3_cond_bz': _L3_cond_in['bz'], 'L3_cond_Wf': _L3_cond_in['Wf'], 'L3_cond_bf': _L3_cond_in['bf'], 'L3_cond_Wada': _L3_cond_in['Wada'], 'L3_cond_bada': _L3_cond_in['bada'], 'L3_cond_Wc1': _L3_cond_in['Wc1'], 'L3_cond_bc1': _L3_cond_in['bc1'], 'L3_cond_Wc2': _L3_cond_in['Wc2'], 'L3_cond_bc2': _L3_cond_in['bc2'], 'L3_cond_Wdbc1': _L3_cond_in['Wdbc1'], 'L3_cond_Wdt1': _L3_cond_in['Wdt1'], 'L3_cond_bdt1': _L3_cond_in['bdt1'], 'L3_cond_Alog1': _L3_cond_in['Alog1'], 'L3_cond_Dp1': _L3_cond_in['Dp1'], 'L3_cond_Wdbc2': _L3_cond_in['Wdbc2'], 'L3_cond_Wdt2': _L3_cond_in['Wdt2'], 'L3_cond_bdt2': _L3_cond_in['bdt2'], 'L3_cond_Alog2': _L3_cond_in['Alog2'], 'L3_cond_Dp2': _L3_cond_in['Dp2']}

def reference(x, cond_2048, cond_1024, mask_BxS_ik0, mask_BxSx1_fk1, mask_BxS_ff1, L0_cond_norm_scale, L0_cond_norm_bias, L0_cond_Wq, L0_cond_bq, L0_cond_Wk, L0_cond_bk, L0_cond_Wv, L0_cond_bv, L0_cond_film_emb_W, L0_cond_film_emb_b, L0_cond_film_norm_scale, L0_cond_film_norm_bias, L0_cond_film_out_W, L0_cond_film_out_b, L1_cond_ln_w, L1_cond_ln_b, L1_cond_Wq, L1_cond_bq, L1_cond_Wk, L1_cond_bk, L1_cond_Wv, L1_cond_bv, L1_cond_W_emb, L1_cond_b_emb, L1_cond_ln2_w, L1_cond_ln2_b, L1_cond_W_out, L1_cond_b_out, L2_cond_norm_w, L2_cond_norm_b, L2_cond_q_w, L2_cond_q_b, L2_cond_k_w, L2_cond_k_b, L2_cond_v_w, L2_cond_v_b, L2_cond_emb_w, L2_cond_emb_b, L2_cond_sb_norm_w, L2_cond_sb_norm_b, L2_cond_out_w, L2_cond_out_b, L3_cond_norm1_g, L3_cond_norm1_b, L3_cond_norm2_g, L3_cond_norm2_b, L3_cond_Wx, L3_cond_bx, L3_cond_Wz, L3_cond_bz, L3_cond_Wf, L3_cond_bf, L3_cond_Wada, L3_cond_bada, L3_cond_Wc1, L3_cond_bc1, L3_cond_Wc2, L3_cond_bc2, L3_cond_Wdbc1, L3_cond_Wdt1, L3_cond_bdt1, L3_cond_Alog1, L3_cond_Dp1, L3_cond_Wdbc2, L3_cond_Wdt2, L3_cond_bdt2, L3_cond_Alog2, L3_cond_Dp2):
    import jax
    import jax.numpy as jnp

    def _L0_cond_ref(x, emb, src_mask, norm_scale, norm_bias, Wq, bq, Wk, bk, Wv, bv, film_emb_W, film_emb_b, film_norm_scale, film_norm_bias, film_out_W, film_out_b):
        import jax, jax.numpy as jnp
        import numpy as np
        H = 16
        LN_EPS = 1e-05

        def _layernorm(x, scale, bias):
            mu = jnp.mean(x, axis=-1, keepdims=True)
            var = jnp.var(x, axis=-1, keepdims=True)
            return (x - mu) * jax.lax.rsqrt(var + LN_EPS) * scale + bias
        B, T, D = x.shape
        dh = D // H
        xn = _layernorm(x, norm_scale, norm_bias)
        q = xn @ Wq + bq
        k = xn @ Wk + bk
        v = xn @ Wv + bv
        mask = (src_mask == 1)[:, :, None]
        k = jnp.where(mask, -jnp.inf, k)
        v = jnp.where(mask, 0.0, v)
        q = q.reshape(B, T, H, dh).transpose(0, 2, 1, 3)
        k = k.reshape(B, T, H, dh).transpose(0, 2, 1, 3)
        v = v.reshape(B, T, H, dh).transpose(0, 2, 1, 3)
        q = jax.nn.softmax(q, axis=-1)
        k = jax.nn.softmax(k, axis=2)
        attn = jnp.einsum('bhse,bhsd->bhed', k, v)
        y = jnp.einsum('bhtd,bhed->bhte', q, attn)
        y = y.transpose(0, 2, 1, 3).reshape(B, T, D)
        emb_out = jax.nn.silu(emb) @ film_emb_W + film_emb_b
        scale, shift = jnp.split(emb_out, 2, axis=-1)
        h = _layernorm(y, film_norm_scale, film_norm_bias) * (1.0 + scale[:, None, :]) + shift[:, None, :]
        h = jax.nn.silu(h) @ film_out_W + film_out_b
        return x + h

    def _L1_cond_ref(x, emb, src_mask, num_head, ln_w, ln_b, Wq, bq, Wk, bk, Wv, bv, W_emb, b_emb, ln2_w, ln2_b, W_out, b_out):
        import jax, jax.numpy as jnp
        import numpy as np
        B, T, D, H, TE = (4, 1024, 512, 8, 1024)
        EPS = 1e-05

        def _ln(x, w, b):
            m = jnp.mean(x, axis=-1, keepdims=True)
            v = jnp.mean((x - m) ** 2, axis=-1, keepdims=True)
            return (x - m) * jax.lax.rsqrt(v + EPS) * w + b
        b, t, d = x.shape
        h = num_head
        dh = d // h
        xn = _ln(x, ln_w, ln_b)
        q = xn @ Wq + bq
        k = xn @ Wk + bk + (1.0 - src_mask) * -1000000.0
        q = jax.nn.softmax(q.reshape(b, t, h, dh), axis=-1)
        k = jax.nn.softmax(k.reshape(b, t, h, dh), axis=1)
        v = ((xn @ Wv + bv) * src_mask).reshape(b, t, h, dh)
        att = jnp.einsum('bnhd,bnhl->bhdl', k, v)
        y = jnp.einsum('bnhd,bhdl->bnhl', q, att).reshape(b, t, d)
        emb_out = (jax.nn.silu(emb) @ W_emb + b_emb)[:, None, :]
        scale, shift = jnp.split(emb_out, 2, axis=2)
        hh = _ln(y, ln2_w, ln2_b) * (1.0 + scale) + shift
        hh = jax.nn.silu(hh) @ W_out + b_out
        return x + hh

    def _L2_cond_ref(x, emb, src_mask, norm_w, norm_b, q_w, q_b, k_w, k_b, v_w, v_b, emb_w, emb_b, sb_norm_w, sb_norm_b, out_w, out_b):
        import jax, jax.numpy as jnp
        import numpy as np
        B, T, D, H, TE = (8, 512, 512, 16, 1024)
        LN_EPS = 1e-05

        def layer_norm(x, w, b):
            m = jnp.mean(x, axis=-1, keepdims=True)
            v = jnp.var(x, axis=-1, keepdims=True)
            return (x - m) / jnp.sqrt(v + LN_EPS) * w + b
        Bx, Tx, Dx = x.shape
        xn = layer_norm(x, norm_w, norm_b)
        q = (xn @ q_w + q_b).reshape(Bx, Tx, H, -1)
        k = (xn @ k_w + k_b).reshape(Bx, Tx, H, -1)
        att = jnp.einsum('bnhl,bmhl->bnmh', q, k)
        mask = src_mask.reshape(Bx, 1, Tx, 1)
        att = att + (1.0 - mask) * -1000000.0
        att = jax.nn.softmax(att, axis=2)
        v = ((xn @ v_w + v_b) * src_mask[:, :, None]).reshape(Bx, Tx, H, -1)
        y = jnp.einsum('bnmh,bmhl->bnhl', att, v).reshape(Bx, Tx, Dx)
        e = jax.nn.silu(emb) @ emb_w + emb_b
        scale, shift = jnp.split(e[:, None, :], 2, axis=2)
        h = layer_norm(y, sb_norm_w, sb_norm_b) * (1.0 + scale) + shift
        h = jax.nn.silu(h) @ out_w + out_b
        return x + h

    def _L3_cond_ref(x, c, w, norm1_g, norm1_b, norm2_g, norm2_b, Wx, bx, Wz, bz, Wf, bf, Wada, bada, Wc1, bc1, Wc2, bc2, Wdbc1, Wdt1, bdt1, Alog1, Dp1, Wdbc2, Wdt2, bdt2, Alog2, Dp2):
        import jax, jax.numpy as jnp
        import numpy as np
        B, S, D, E, N, R = (2, 512, 512, 1024, 16, 64)
        EPS = 1e-05

        def _ln(x, g, b):
            m = jnp.mean(x, -1, keepdims=True)
            v = jnp.mean((x - m) ** 2, -1, keepdims=True)
            return (x - m) * jax.lax.rsqrt(v + EPS) * g + b

        def _ssm(u, Wdbc, Wdt, bdt, Alog, Dp):
            dbc = jnp.einsum('bse,re->bsr', u, Wdbc)
            dlt, Bm, Cm = jnp.split(dbc, [R, R + N], axis=-1)
            delta = jax.nn.softplus(jnp.einsum('bsr,er->bse', dlt, Wdt) + bdt)
            A = -jnp.exp(Alog)
            dA = jnp.exp(delta[..., None] * A)
            dBu = delta[..., None] * Bm[:, :, None, :] * u[..., None]

            def step(h, xs):
                dA_t, dBu_t, C_t = xs
                h = dA_t * h + dBu_t
                y = jnp.einsum('ben,bn->be', h, C_t)
                return (h, y)
            h0 = jnp.zeros((u.shape[0], u.shape[2], N), u.dtype)
            _, ys = jax.lax.scan(step, h0, (dA.swapaxes(0, 1), dBu.swapaxes(0, 1), Cm.swapaxes(0, 1)))
            return ys.swapaxes(0, 1) + u * Dp
        ada = jax.nn.silu(c) @ Wada.T + bada
        shift, scale, gate = jnp.split(ada, 3, axis=1)
        x_ssm = _ln(x, norm1_g, norm1_b)
        x_ssm = x_ssm * (1.0 + scale[:, None, :]) + shift[:, None, :]
        skip = x_ssm
        x_ssm = _ln(x_ssm, norm2_g, norm2_b)
        mz = jnp.einsum('bsd,ed->bse', x_ssm, Wz) + bz
        mx = jnp.einsum('bsd,ed->bse', x_ssm, Wx) + bx
        act_mx = jax.nn.silu(mx)
        z1 = jnp.einsum('bse,fe->bsf', mz, Wc1) + bc1
        z1 = _ssm(z1, Wdbc1, Wdt1, bdt1, Alog1, Dp1)
        y1 = act_mx * z1
        z2 = jnp.einsum('bse,fe->bsf', mz, Wc2) + bc2
        z2 = jnp.flip(z2, axis=1)
        z2 = _ssm(z2, Wdbc2, Wdt2, bdt2, Alog2, Dp2)
        z2 = jnp.flip(z2, axis=1)
        y2 = act_mx * z2
        out = jnp.einsum('bse,de->bsd', y1 + y2, Wf) + bf + skip
        return x + gate[:, None, :] * out
    x = _L0_cond_ref(x, cond_2048, mask_BxS_ik0, L0_cond_norm_scale, L0_cond_norm_bias, L0_cond_Wq, L0_cond_bq, L0_cond_Wk, L0_cond_bk, L0_cond_Wv, L0_cond_bv, L0_cond_film_emb_W, L0_cond_film_emb_b, L0_cond_film_norm_scale, L0_cond_film_norm_bias, L0_cond_film_out_W, L0_cond_film_out_b)
    x = _L1_cond_ref(x, cond_2048, mask_BxSx1_fk1, 8, L1_cond_ln_w, L1_cond_ln_b, L1_cond_Wq, L1_cond_bq, L1_cond_Wk, L1_cond_bk, L1_cond_Wv, L1_cond_bv, L1_cond_W_emb, L1_cond_b_emb, L1_cond_ln2_w, L1_cond_ln2_b, L1_cond_W_out, L1_cond_b_out)
    x = _L2_cond_ref(x, cond_2048, mask_BxS_ff1, L2_cond_norm_w, L2_cond_norm_b, L2_cond_q_w, L2_cond_q_b, L2_cond_k_w, L2_cond_k_b, L2_cond_v_w, L2_cond_v_b, L2_cond_emb_w, L2_cond_emb_b, L2_cond_sb_norm_w, L2_cond_sb_norm_b, L2_cond_out_w, L2_cond_out_b)
    x = _L3_cond_ref(x, cond_2048, cond_1024, L3_cond_norm1_g, L3_cond_norm1_b, L3_cond_norm2_g, L3_cond_norm2_b, L3_cond_Wx, L3_cond_bx, L3_cond_Wz, L3_cond_bz, L3_cond_Wf, L3_cond_bf, L3_cond_Wada, L3_cond_bada, L3_cond_Wc1, L3_cond_bc1, L3_cond_Wc2, L3_cond_bc2, L3_cond_Wdbc1, L3_cond_Wdt1, L3_cond_bdt1, L3_cond_Alog1, L3_cond_Dp1, L3_cond_Wdbc2, L3_cond_Wdt2, L3_cond_bdt2, L3_cond_Alog2, L3_cond_Dp2)
    return x

_drawn_inputs = setup_inputs


def setup_inputs(seed=0):
    import zlib

    import numpy as np

    out = dict(_drawn_inputs(seed))
    spreads = {'L0_cond_norm_scale': (1.0, 0.2),
     'L0_cond_norm_bias': (0.0, 0.1),
     'L0_cond_bq': (0.0, 0.1),
     'L0_cond_bk': (0.0, 0.1),
     'L0_cond_bv': (0.0, 0.1),
     'L0_cond_film_emb_b': (0.0, 0.1),
     'L0_cond_film_norm_scale': (1.0, 0.2),
     'L0_cond_film_norm_bias': (0.0, 0.1),
     'L0_cond_film_out_b': (0.0, 0.1),
     'L1_cond_ln_w': (1.0, 0.2),
     'L1_cond_ln_b': (0.0, 0.1),
     'L1_cond_bq': (0.0, 0.1),
     'L1_cond_bk': (0.0, 0.1),
     'L1_cond_bv': (0.0, 0.1),
     'L1_cond_b_emb': (0.0, 0.1),
     'L1_cond_ln2_w': (1.0, 0.2),
     'L1_cond_ln2_b': (0.0, 0.1),
     'L1_cond_b_out': (0.0, 0.1),
     'L2_cond_norm_w': (1.0, 0.2),
     'L2_cond_norm_b': (0.0, 0.1),
     'L2_cond_q_b': (0.0, 0.1),
     'L2_cond_k_b': (0.0, 0.1),
     'L2_cond_v_b': (0.0, 0.1),
     'L2_cond_emb_b': (0.0, 0.1),
     'L2_cond_sb_norm_w': (1.0, 0.2),
     'L2_cond_sb_norm_b': (0.0, 0.1),
     'L2_cond_out_b': (0.0, 0.1),
     'L3_cond_norm1_g': (1.0, 0.2),
     'L3_cond_norm1_b': (0.0, 0.1),
     'L3_cond_norm2_g': (1.0, 0.2),
     'L3_cond_norm2_b': (0.0, 0.1),
     'L3_cond_bx': (0.0, 0.1),
     'L3_cond_bz': (0.0, 0.1),
     'L3_cond_bf': (0.0, 0.1),
     'L3_cond_bada': (0.0, 0.1),
     'L3_cond_bc1': (0.0, 0.1),
     'L3_cond_bc2': (0.0, 0.1),
     'L3_cond_bdt1': (0.0, 0.1),
     'L3_cond_Dp1': (1.0, 0.2),
     'L3_cond_bdt2': (0.0, 0.1),
     'L3_cond_Dp2': (1.0, 0.2)}
    factors = {}
    for name, (base, spread) in spreads.items():
        noise = np.random.default_rng([zlib.crc32(name.encode()), seed]).standard_normal(out[name].shape)
        drawn = base * np.exp(spread * noise) if base else spread * noise
        out[name] = jnp.asarray(drawn.astype(out[name].dtype))
    for name, factor in factors.items():
        out[name] = (out[name] * factor).astype(out[name].dtype)
    return out
```

```python
import concourse.bass as bass
from concourse import mybir
from contextlib import ExitStack

F32 = mybir.dt.float32
I32 = mybir.dt.int32
ALU = mybir.AluOpType
ACT = mybir.ActivationFunctionType
AX = mybir.AxisListType

P = 128
B = 8
T = 512
D = 512
E = 1024
N = 16
R = 64
TT = T // P
DT = D // P
ET = E // P
EPS = 1e-5
NEG = -1.0e30
SP_CAP = 40.0

NW, NB, BQ, BK, FS, FH, N2W, N2B = range(8)
G2, B2, BX, BC, BZ, BDT, DPC = 0, 4, 8, 16, 32, 40, 56


class Stages:

    def __init__(self, plan):
        self.first, self.by, self.per = {}, [], {}
        for name, n, engine in plan:
            self.first[name] = len(self.by)
            self.by += [engine] * n
        for engine in set(self.by):
            self.per[engine] = self.by.count(engine)
        self.n = len(self.by)

    def full(self, b, name, k=0):
        return (b + 1) * self.n + self.first[name] + k + 1

    def drained(self, b, name, k=0):
        at = self.first[name] + k
        engine = self.by[at]
        return engine, (b + 1) * self.per[engine] + self.by[: at + 1].count(engine)

    def before(self, b, name, k, ring):
        at = self.first[name] + k - ring
        if at >= 0:
            engine = self.by[at]
            return engine, (b + 1) * self.per[engine] + self.by[: at + 1].count(engine)
        engine = self.by[at + self.n]
        return engine, b * self.per[engine] + self.by[: at + self.n + 1].count(engine)


class LayerSemaphores:

    def __init__(self, nc):
        self.nc, self.held = nc, []

    def take(self, name):
        self.held.append(self.nc.alloc_semaphore(name=name))
        return self.held[-1]

    def clear(self):
        self.nc.clear_and_free_semaphores(self.held)
        self.held = []
        self.nc.all_engine_barrier()


def prologue(nc, sems, d, mod_all, banks):
    with ExitStack() as ctx:
        sb = lambda n, s, t=F32: ctx.enter_context(nc.sbuf_tensor("pro_" + n, s, t))
        sem = lambda n: sems.take("pro_" + n)
        cond = sb("cond", [B, E])
        ident = sb("ident", [P, P])
        silu_t = sb("silu_t", [P, ET, B])
        w_mod = [sb(f"w_mod{i}", [P, ET, 512]) for i in range(2)]
        cols = sb("cols", [P, 3, 8 * DT])
        raw = sb("raw", [P, 2 * DT, B])
        ada_bias = sb("ada_bias", [B, 5, D])
        ada = sb("ada", [B, 3, D])
        wz = sb("wz", [P, ET, D])
        wc = sb("wc", [P, ET, E])
        fused = [sb(f"fused{i}", [P, D]) for i in range(2)]

        loaded, stored = sem("loaded"), [sem(f"stored{i}") for i in range(2)]
        w_loaded = [sem(f"w_loaded{i}") for i in range(2)]
        wc_loaded, silu_ready, silu_t_full, silu_t_ready = sem("wc"), sem("silu"), sem("silu_t_full"), sem("silu_t")
        full, drained, mod_step, ada_ready = sem("full"), sem("drained"), sem("mod_step"), sem("ada_ready")
        fused_full, fused_ready = sem("fused_full"), sem("fused_ready")
        pieces = [(d["mod_w"][l], 512 * h) for l in range(3) for h in range(2)]
        pieces += [(d["ada_wT"], 512 * h) for h in range(3)]
        with nc.Block() as block:

            @block.sync
            def _(sp):
                sp.dma_start(cond[:, :], d["cond"]).then_inc(loaded, 16)
                sp.dma_start(ident[:, :], d["ident"]).then_inc(loaded, 16)
                sp.dma_start(cols[:, :, :], d["att_cols"]).then_inc(loaded, 16)
                sp.dma_start(ada_bias[:, :, :].rearrange("b r n -> b (r n)"),
                             d["ada_rows"].broadcast_to([B, 5 * D])).then_inc(loaded, 16)
                sp.dma_start(wz[:, :, :], d["wz"].rearrange("(k p) n -> p k n", p=P)).then_inc(loaded, 16)
                for i, (w, c0) in enumerate(pieces):
                    if i >= 2:
                        sp.wait_ge(full, i - 1)
                    sp.dma_start(w_mod[i % 2][:, :, :], w[:, c0:c0 + 512].rearrange("(k p) n -> p k n", p=P)
                                 ).then_inc(w_loaded[i % 2], 16)
                sp.dma_start(wc[:, :, :], d["wcT"][0].rearrange("(k p) n -> p k n", p=P)).then_inc(wc_loaded, 16)
                for s in range(2):
                    for m in range(DT * 2):
                        i = s * 8 + m
                        sp.wait_ge(fused_ready, i + 1)
                        sp.dma_start(d["wzc"][s, (m // 2) * P:(m // 2 + 1) * P, (m % 2) * 512:(m % 2 + 1) * 512],
                                     fused[i % 2][:, :]).then_inc(stored[i % 2], 16)
                    if s == 0:
                        sp.wait_ge(fused_full, 9)
                        sp.dma_start(wc[:, :, :], d["wcT"][1].rearrange("(k p) n -> p k n", p=P)
                                     ).then_inc(wc_loaded, 16)
                sp.wait_ge(ada_ready, 1)
                sp.dma_start(d["ada_d"], ada[:, :, :].rearrange("b r n -> b (r n)")).then_inc(loaded, 16)
                sp.wait_ge(loaded, 96)
                for i in range(2):
                    sp.wait_ge(stored[i], 128)

            @block.scalar
            def _(act):
                act.wait_ge(loaded, 80)
                act.activation(cond[:, :], cond[:, :], ACT.Silu).then_inc(silu_ready, 1)

            @block.tensor
            def _(pe):
                pe.wait_ge(silu_ready, 1)
                for k in range(ET):
                    last = pe.transpose(banks[0][:, k * B:(k + 1) * B], cond[:, k * P:(k + 1) * P], ident[0:B, 0:B])
                last.then_inc(silu_t_full, 1)
                pe.wait_ge(silu_t_ready, 1)
                for i in range(9):
                    pe.wait_ge(w_loaded[i % 2], 16 * (i // 2 + 1))
                    if i >= 2:
                        pe.wait_ge(drained, i - 1)
                    bank = banks[1 + i % 2]
                    if i < 6:
                        for m in range(4):
                            for k in range(ET):
                                last = pe.matmul(bank[:, m * B:(m + 1) * B], w_mod[i % 2][:, k, m * P:(m + 1) * P],
                                                 silu_t[:, k, :], start=(k == 0), stop=(k == ET - 1))
                    else:
                        for k in range(ET):
                            last = pe.matmul(bank[0:B, :], silu_t[:, k, :], w_mod[i % 2][:, k, :],
                                             start=(k == 0), stop=(k == ET - 1))
                    last.then_inc(full, 1)
                for s in range(2):
                    pe.wait_ge(wc_loaded, 16 * (s + 1))
                    for m in range(8):
                        i = s * 8 + m
                        if i >= 2:
                            pe.wait_ge(fused_ready, i - 1)
                        for k in range(ET):
                            last = pe.matmul(banks[3 + i % 2][:, :], wz[:, k, (m // 2) * P:(m // 2 + 1) * P],
                                             wc[:, k, (m % 2) * 512:(m % 2 + 1) * 512],
                                             start=(k == 0), stop=(k == ET - 1))
                        last.then_inc(fused_full, 1)
                    for m in range(ET):
                        for k in range(ET):
                            last = pe.matmul(banks[5][:, s * 8 + m:s * 8 + m + 1], wc[:, k, m * P:(m + 1) * P],
                                             mod_all["ssm_cols"][:, BZ + k:BZ + k + 1],
                                             start=(k == 0), stop=(k == ET - 1))
                    last.then_inc(fused_full, 1)

            @block.vector
            def _(dve):
                steps = [0]

                def step(ins):
                    ins.then_inc(mod_step, 1)
                    steps[0] += 1
                    dve.wait_ge(mod_step, steps[0])

                dve.wait_ge(silu_t_full, 1)
                dve.tensor_copy(silu_t[:, :, :].rearrange("p k b -> p (k b)"), banks[0][:, 0:ET * B]
                                ).then_inc(silu_t_ready, 1)
                dve.wait_ge(loaded, 80)
                col = lambda l, v: cols[:, l, v * DT:(v + 1) * DT].unsqueeze(2).broadcast_to([P, DT, B])
                for l in range(3):
                    for h, v in ((0, FS), (1, FH)):
                        i = 2 * l + h
                        dve.wait_ge(full, i + 1)
                        ins = dve.tensor_tensor(raw[:, h * DT:(h + 1) * DT, :],
                                                banks[1 + i % 2][:, 0:DT * B].rearrange("p (m b) -> p m b", b=B),
                                                col(l, v), ALU.add)
                        ins.then_inc(drained, 1)
                        dve.wait_ge(drained, i + 1)
                    gain, shift = mod_all["gain"][:, l, :, :], mod_all["shift"][:, l, :, :]
                    step(dve.tensor_scalar(raw[:, 0:DT, :], raw[:, 0:DT, :], 1.0, None, ALU.add))
                    step(dve.tensor_tensor(gain, raw[:, 0:DT, :], col(l, N2W), ALU.mult))
                    step(dve.tensor_tensor(shift, raw[:, 0:DT, :], col(l, N2B), ALU.mult))
                    step(dve.tensor_tensor(shift, shift, raw[:, DT:2 * DT, :], ALU.add))
                for h in range(3):
                    dve.wait_ge(full, 7 + h)
                    dve.tensor_tensor(ada[:, h, :], banks[1 + (6 + h) % 2][0:B, :], ada_bias[:, 2 + h, :], ALU.add
                                      ).then_inc(drained, 1)
                dve.wait_ge(drained, 9)
                step(dve.tensor_scalar(ada[:, 1, :], ada[:, 1, :], 1.0, None, ALU.add))
                step(dve.tensor_tensor(ada_bias[:, 1, :], ada_bias[:, 1, :], ada[:, 1, :], ALU.mult))
                step(dve.tensor_tensor(ada_bias[:, 1, :], ada_bias[:, 1, :], ada[:, 0, :], ALU.add))
                step(dve.tensor_tensor(ada[:, 0, :], ada[:, 1, :], ada_bias[:, 0, :], ALU.mult))
                step(dve.tensor_copy(ada[:, 1, :], ada_bias[:, 1, :]))
                dve.sem_inc(ada_ready, 1)
                for s in range(2):
                    for m in range(8):
                        i = s * 8 + m
                        dve.wait_ge(fused_full, s * 9 + m + 1)
                        if i >= 2:
                            dve.wait_ge(stored[i % 2], 16 * (i // 2))
                        dve.tensor_copy(fused[i % 2][:, :], banks[3 + i % 2][:, :]).then_inc(fused_ready, 1)
                dve.wait_ge(fused_full, 18)
                dve.tensor_tensor(mod_all["bzc"][:, :], banks[5][:, 0:16], mod_all["ssm_cols"][:, BC:BC + 16], ALU.add)


def attention_layer(nc, sems, d, mod_all, banks, layer, x_in, x_out):
    H = (16, 8, 16)[layer]
    dh = D // H
    linear = layer < 2
    if linear:
        plan = [("T", 4, "act"), ("K", 4, "dve"), ("Q", 4, "dve"), ("V", 4, "dve"), ("TK", 4, "act"),
                ("A", 4, "dve"), ("TQ", 4, "act"), ("Y", 4, "dve"), ("TY", 4, "act"), ("O", 4, "dve")]
    else:
        plan = [("T", 4, "act"), ("K", 4, "act"), ("Q", 4, "act"), ("V", 4, "dve"),
                ("YT", 4, "dve"), ("TY", 4, "act"), ("O", 4, "dve")]
    st = Stages(plan)
    bank_of = lambda name, k: banks[(st.first[name] + k) % 8]
    pre = f"l{layer}_"
    HG = 4
    NG = H // HG
    UNITS = TT * H

    with ExitStack() as ctx:
        sb = lambda n, s, t=F32: ctx.enter_context(nc.sbuf_tensor(pre + n, s, t))
        sem = lambda n: sems.take(pre + n)
        w = [sb(f"w{i}", [P, DT, D]) for i in range(4)]
        cols = sb("cols", [P, 8 * DT])
        rows = sb("rows", [P, 3, D])
        ident = sb("ident", [P, P])
        block_mask = sb("block_mask", [P, P])
        minus_half = sb("minus_half", [P, TT])
        keep_in = sb("keep_in", [P, B * TT], I32 if layer == 0 else F32)
        keep = sb("keep", [P, B * TT])
        mask_in = [sb(f"mask_in{j}", [P, T], I32 if layer == 0 else F32) for j in range(2)]
        mask_add = sb("mask_add", [P, T])
        x = [sb(f"x{j}", [P, TT, D]) for j in range(2)]
        xn = sb("xn", [P, TT, D])
        xn_t = sb("xn_t", [P, DT, T])
        k_t = sb("k_t", [P, DT, T])
        v_tm = sb("v_tm", [P, TT, D])
        q_t = sb("q_t", [P, DT, T])
        attn = sb("attn", [P, DT, P])
        stats = sb("stats", [P, TT, 6])
        mv = sb("mv", [P, TT, 2])
        rstd = sb("rstd", [P, TT])
        y_stats = sb("y_stats", [P, TT, 6])
        y_mv = sb("y_mv", [P, TT, 2])
        y_rstd = sb("y_rstd", [P, TT])
        k_max = sb("k_max", [P, DT])
        k_sum = sb("k_sum", [P, DT])
        q_max = sb("q_max", [P, TT, H])
        q_sum = sb("q_sum", [P, TT, H])
        if linear:
            k_tm, q_tm, y = (sb(n, [P, TT, D]) for n in ("k_tm", "q_tm", "y"))
            h_t = sb("h_t", [P, DT, T])
        else:
            prob = sb("prob", [P, 2 * HG, T])
            prob_t = sb("prob_t", [P, 2, HG, TT, T])
            y_t = sb("y_t", [P, DT, T])
            y, h_t = xn, xn_t
            s_max = sb("s_max", [P, TT * H])

        w_loaded, const_ready, passed = sem("w_loaded"), sem("const_ready"), sem("passed")
        half_ready = sem("half_ready")
        x_loaded = [sem(f"x_loaded{j}") for j in range(2)]
        mask_loaded = [sem(f"mask_loaded{j}") for j in range(2)]
        x_stored = [sem(f"x_stored{j}") for j in range(2)]
        psum_full = sem("psum_full")
        drained = {"act": sem("act_drained"), "dve": sem("dve_drained")}
        mask_ready, stats_ready, mv_ready = sem("mask_ready"), sem("stats_ready"), sem("mv_ready")
        var_ready, rstd_ready, xn_ready, xb_ready = sem("var_ready"), sem("rstd_ready"), sem("xn_ready"), sem("xb_ready")
        k_max_ready, k_exp_ready, rk_ready = sem("k_max_ready"), sem("k_exp_ready"), sem("rk_ready")
        k_norm_ready = sem("k_norm_ready")
        q_max_ready, q_sub_ready, q_exp_ready = sem("q_max_ready"), sem("q_sub_ready"), sem("q_exp_ready")
        q_sum_ready, v_ready, out_ready = sem("q_sum_ready"), sem("v_ready"), sem("out_ready")
        y_stats_ready, y_mv_ready, y_var_ready = sem("y_stats_ready"), sem("y_mv_ready"), sem("y_var_ready")
        y_rstd_ready, yn_ready = sem("y_rstd_ready"), sem("yn_ready")
        s_full, s_drained, p_ready = sem("s_full"), sem("s_drained"), sem("p_ready")
        pt_full, pt_ready, pv_done, y_drained = sem("pt_full"), sem("pt_ready"), sem("pv_done"), sem("y_drained")

        def wait_bank(pe, b, name, k):
            if linear:
                engine, count = st.before(b, name, k, 8)
                pe.wait_ge(drained[engine], count)
            elif name == "T":
                engine, count = st.drained(b - 1, "O", k)
                pe.wait_ge(drained[engine], count)
            elif name == "K":
                engine, count = st.drained(b - 1, "TY", k)
                pe.wait_ge(drained[engine], count)
            elif name in ("Q", "V", "O"):
                engine, count = st.drained(b, {"Q": "T", "V": "K", "O": "YT"}[name], k)
                pe.wait_ge(drained[engine], count)

        def batches(eng, body):
            with eng.Fori(0, B // 2) as pair:
                for j in range(2):
                    body(pair * 2 + j, pair, j)

        def wait_drained(b, name, k):
            engine, count = st.drained(b, name, k)
            return drained[engine], count

        def transposes(pe, b, name, src):
            for k in range(4):
                wait_bank(pe, b, name, k)
                for i in range(4):
                    last = pe.transpose(bank_of(name, k)[:, i * P:(i + 1) * P], src[:, i, k * P:(k + 1) * P],
                                        ident[:, :])
                last.then_inc(psum_full, 1)

        def project_t(pe, b, name, weight):
            for m in range(DT):
                wait_bank(pe, b, name, m)
                for k in range(DT):
                    last = pe.matmul(bank_of(name, m)[:, :], weight[:, k, m * P:(m + 1) * P], xn_t[:, k, :],
                                     start=(k == 0), stop=(k == DT - 1))
                last.then_inc(psum_full, 1)

        def project(pe, b, name, src_t, weight):
            for t in range(TT):
                wait_bank(pe, b, name, t)
                for k in range(DT):
                    last = pe.matmul(bank_of(name, t)[:, :], src_t[:, k, t * P:(t + 1) * P], weight[:, k, :],
                                     start=(k == 0), stop=(k == DT - 1))
                last.then_inc(psum_full, 1)

        def attention_pe(pe, b):
            pe.wait_ge(*wait_drained(b, "Q", DT - 1))

            def scores(g):
                quad, t = g // TT, g % TT
                for i in range(HG):
                    if g > 0:
                        pe.wait_ge(s_drained, b * UNITS + g * HG + i - HG + 1)
                    head = slice(dh * i, dh * (i + 1))
                    pe.matmul(banks[i][:, :], q_t[head, quad, t * P:(t + 1) * P], k_t[head, quad, :],
                              start=True, stop=True).then_inc(s_full, 1)

            def transpose_p(u):
                pe.wait_ge(p_ready, b * UNITS + u + 1)
                if u >= 2:
                    pe.wait_ge(pt_ready, b * UNITS + u - 1)
                for m in range(TT):
                    last = pe.transpose(banks[4 + u % 2][:, m * P:(m + 1) * P],
                                        prob[:, u % (2 * HG), m * P:(m + 1) * P], ident[:, :])
                last.then_inc(pt_full, 1)

            def values(quad):
                pe.wait_ge(pt_ready, b * UNITS + (quad + 1) * TT * HG)
                if quad >= 2:
                    pe.wait_ge(y_drained, b * DT + quad - 1)
                for m in range(TT):
                    for i in range(HG):
                        h = quad * HG + i
                        last = pe.matmul(banks[6 + quad % 2][dh * i:dh * (i + 1), :], v_tm[:, m, h * dh:(h + 1) * dh],
                                         prob_t[:, quad % 2, i, m, :], start=(m == 0), stop=(m == TT - 1))
                last.then_inc(pv_done, 1)

            scores(0)
            pe.wait_ge(v_ready, (b + 1) * TT)
            for g in range(TT * NG):
                if g + 1 < TT * NG:
                    scores(g + 1)
                for i in range(HG):
                    transpose_p(g * HG + i)
                if g % TT == 0 and g > 0:
                    values(g // TT - 1)
            values(NG - 1)
            pe.wait_ge(s_drained, (b + 1) * UNITS)
            pe.wait_ge(y_drained, (b + 1) * DT)
            transposes(pe, b, "YT", y_t)

        def attention_act(act, b):
            def exps(g):
                for i in range(HG):
                    u = g * HG + i
                    act.wait_ge(s_drained, b * UNITS + u + 1)
                    h = (g // TT) * HG + i
                    act.activation(prob[:, u % (2 * HG), :], prob[:, u % (2 * HG), :], ACT.Exp, scale=-1.0,
                                   bias=s_max[:, u:u + 1],
                                   accum_out=q_sum[:, g % TT, h:h + 1]).then_inc(p_ready, 1)

            for g in range(TT * NG):
                exps(g)

        def attention_dve(dve, b):
            def scores(g):
                for i in range(HG):
                    u = g * HG + i
                    dve.wait_ge(s_full, b * UNITS + u + 1)
                    if u >= 2 * HG:
                        dve.wait_ge(pt_full, b * UNITS + u - 2 * HG + 1)
                    dve.sem_inc(passed, 1)
                    dve.tensor_tensor_reduce(out=prob[:, u % (2 * HG), :], in0=banks[i][:, :],
                                             in1=mask_add[:, :], op0=ALU.add, op1=ALU.min, scale=-1.0,
                                             scalar=3.0e38, accum_out=s_max[:, u:u + 1]).then_inc(s_drained, 1)

            def y_copy(quad):
                dve.wait_ge(pv_done, b * NG + quad + 1)
                dve.tensor_copy(y_t[:, quad, :], banks[6 + quad % 2][:, :]).then_inc(y_drained, 1)

            scores(0)
            for g in range(TT * NG):
                if g + 1 < TT * NG:
                    scores(g + 1)
                for i in range(HG):
                    u = g * HG + i
                    dve.wait_ge(pt_full, b * UNITS + u + 1)
                    if g >= 2 * TT and g % TT == 0 and i == 0:
                        dve.wait_ge(pv_done, b * NG + g // TT - 1)
                    dve.tensor_copy(prob_t[:, (g // TT) % 2, i, :, (g % TT) * P:(g % TT + 1) * P],
                                    banks[4 + u % 2][:, :].rearrange("p (m n) -> p m n", m=TT)).then_inc(pt_ready, 1)
                if g % TT == 1 and g > TT:
                    y_copy(g // TT - 1)
            y_copy(NG - 1)
            dve.wait_ge(p_ready, (b + 1) * UNITS)
            dve.reciprocal(q_sum[:, :, :], q_sum[:, :, :]).then_inc(q_sum_ready, 1)
            dve.wait_ge(q_sum_ready, b + 1)
            for t in range(TT):
                dve.wait_ge(psum_full, st.full(b, "YT", t))
                dve.tensor_tensor(y[:, t, :].rearrange("p (h e) -> p h e", e=dh),
                                  bank_of("YT", t)[:, :].rearrange("p (h e) -> p h e", e=dh),
                                  q_sum[:, t, :].unsqueeze(2).broadcast_to([P, H, dh]), ALU.mult
                                  ).then_inc(drained["dve"], 1)
            dve.wait_ge(*wait_drained(b, "YT", TT - 1))

        with nc.Block() as block:

            @block.sync
            def _(sp):
                for j in range(2):
                    sp.sem_inc(x_stored[j], 16)
                for i in range(4):
                    sp.dma_start(w[i][:, :, :], d["att_w"][layer, i].rearrange("(k p) n -> p k n", p=P)
                                 ).then_inc(w_loaded, 16)
                sp.dma_start(cols[:, :], d["att_cols"][:, layer, :]).then_inc(w_loaded, 16)
                sp.dma_start(rows[:, :, :].rearrange("p r n -> p (r n)"),
                             d["att_rows"][layer:layer + 1, :].broadcast_to([P, 3 * D])).then_inc(w_loaded, 16)
                sp.dma_start(ident[:, :], d["ident"]).then_inc(w_loaded, 16)
                sp.dma_start(block_mask[:, :], d["block_masks"][:, 1 if dh == 64 else 0, :]).then_inc(w_loaded, 16)
                sp.dma_start(keep_in[:, :], d[f"mask{layer}_t"]).then_inc(w_loaded, 16)

                def load(b, j):
                    sp.dma_start(x[j][:, :, :], x_in[b].rearrange("(t p) n -> p t n", p=P)).then_inc(x_loaded[j], 16)
                    sp.dma_start(mask_in[j][:, :], d[f"mask{layer}"][b].broadcast_to([P, T])).then_inc(mask_loaded[j], 16)

                load(0, 0)

                with sp.Fori(0, B // 2 - 1) as pair:
                    for j in range(2):
                        b = pair * 2 + j
                        if j == 0:
                            sp.wait_ge(x_stored[1], pair * 16 + 16)
                            sp.sem_inc(passed, 1)
                            sp.wait_ge(mask_ready, b + 1)
                            sp.sem_inc(passed, 1)
                            load(b + 1, 1)
                        sp.wait_ge(out_ready, (b + 1) * TT)
                        sp.sem_inc(passed, 1)
                        sp.dma_start(x_out[b].rearrange("(t p) n -> p t n", p=P), x[j][:, :, :]
                                     ).then_inc(x_stored[j], 16)
                        if j == 0:
                            sp.wait_ge(x_stored[0], pair * 16 + 32)
                            sp.sem_inc(passed, 1)
                            sp.wait_ge(mask_ready, b + 2)
                            sp.sem_inc(passed, 1)
                            load(b + 2, 0)
                b = B - 2
                sp.wait_ge(x_stored[1], B // 2 * 16)
                sp.wait_ge(mask_ready, b + 1)
                sp.sem_inc(passed, 1)
                load(b + 1, 1)
                for j in range(2):
                    sp.wait_ge(out_ready, (b + j + 1) * TT)
                    sp.sem_inc(passed, 1)
                    sp.dma_start(x_out[b + j].rearrange("(t p) n -> p t n", p=P), x[j][:, :, :]
                                 ).then_inc(x_stored[j], 16)
                for j in range(2):
                    sp.wait_ge(x_stored[j], B // 2 * 16 + 16)

            @block.gpsimd
            def _(pool):
                pool.memset(minus_half[:, :], -0.5).then_inc(half_ready, 1)
                pool.wait_ge(half_ready, 1)
                pool.wait_ge(w_loaded, 9 * 16)

                def body(b, pair, j):
                    pool.wait_ge(mv_ready, (b + 1) * TT)
                    pool.sem_inc(passed, 1)
                    pool.tensor_scalar(rstd[:, :], mv[:, :, 1], EPS, 0.0, ALU.add, ALU.add).then_inc(var_ready, 1)
                    pool.wait_ge(var_ready, b + 1)
                    pool.tensor_tensor(rstd[:, :], rstd[:, :], minus_half[:, :], ALU.pow).then_inc(rstd_ready, 1)
                    pool.wait_ge(xn_ready, (b + 1) * TT)
                    pool.tensor_tensor(x[j][:, :, :], x[j][:, :, :],
                                       rows[:, 2, :].unsqueeze(1).broadcast_to([P, TT, D]), ALU.add
                                       ).then_inc(xb_ready, 1)
                    pool.wait_ge(y_mv_ready, (b + 1) * TT)
                    pool.sem_inc(passed, 1)
                    pool.tensor_scalar(y_rstd[:, :], y_mv[:, :, 1], EPS, 0.0, ALU.add, ALU.add).then_inc(y_var_ready, 1)
                    pool.wait_ge(y_var_ready, b + 1)
                    pool.tensor_tensor(y_rstd[:, :], y_rstd[:, :], minus_half[:, :], ALU.pow).then_inc(y_rstd_ready, 1)

                batches(pool, body)

            @block.scalar
            def _(act):
                act.sem_inc(drained["act"], st.per["act"])
                act.wait_ge(w_loaded, 9 * 16)
                col = lambda v, k: cols[:, v * DT + k:v * DT + k + 1]

                def drain(b, name, k, out, func, **kw):
                    act.wait_ge(psum_full, st.full(b, name, k))
                    act.activation(out, bank_of(name, k)[:, :], func, **kw).then_inc(drained["act"], 1)

                def body(b, pair, j):
                    for k in range(DT):
                        drain(b, "T", k, xn_t[:, k, :], ACT.Identity, scale=col(NW, k), bias=col(NB, k))
                    if linear:
                        act.wait_ge(k_max_ready, 2 * (b + 1))
                        for k in range(DT):
                            act.activation(k_t[:, k, :], k_t[:, k, :], ACT.Exp, bias=k_max[:, k:k + 1],
                                           accum_out=k_sum[:, k:k + 1]).then_inc(k_exp_ready, 1)
                        for t in range(TT):
                            act.wait_ge(q_sub_ready, b * TT + t + 1)
                            act.activation(q_tm[:, t, :], q_tm[:, t, :], ACT.Exp).then_inc(q_exp_ready, 1)
                        for t in range(TT):
                            drain(b, "TK", t, k_tm[:, t, :], ACT.Copy)
                        for k in range(DT):
                            drain(b, "TQ", k, q_t[:, k, :], ACT.Copy)
                    else:
                        for k in range(DT):
                            drain(b, "K", k, k_t[:, k, :], ACT.Identity, bias=col(BK, k))
                        for k in range(DT):
                            drain(b, "Q", k, q_t[:, k, :], ACT.Identity, bias=col(BQ, k))
                        attention_act(act, b)
                    for k in range(DT):
                        drain(b, "TY", k, h_t[:, k, :], ACT.Silu,
                              scale=mod_all["gain"][:, layer, k, bass.ds(b, 1)],
                              bias=mod_all["shift"][:, layer, k, bass.ds(b, 1)])

                batches(act, body)

            @block.tensor
            def _(pe):
                pe.sem_inc(psum_full, st.n)
                pe.wait_ge(w_loaded, 9 * 16)
                wq, wk, wv, wo = w

                def body(b, pair, j):
                    pe.wait_ge(xn_ready, (b + 1) * TT)
                    transposes(pe, b, "T", xn)
                    pe.wait_ge(*wait_drained(b, "T", DT - 1))
                    project_t(pe, b, "K", wk)
                    if linear:
                        project(pe, b, "Q", xn_t, wq)
                        project(pe, b, "V", xn_t, wv)
                        pe.wait_ge(k_norm_ready if layer == 0 else k_exp_ready, (b + 1) * DT)
                        transposes(pe, b, "TK", k_t)
                        pe.wait_ge(v_ready, (b + 1) * TT)
                        pe.wait_ge(*wait_drained(b, "TK", TT - 1))
                        for g in range(DT):
                            wait_bank(pe, b, "A", g)
                            for t in range(TT):
                                k_part, v_part = (i[:, t, g * P:(g + 1) * P] for i in (k_tm, v_tm))
                                lhs_t, rhs = (v_part, k_part) if layer == 0 else (k_part, v_part)
                                last = pe.matmul(bank_of("A", g)[:, 0:P], lhs_t, rhs, start=(t == 0),
                                                 stop=(t == TT - 1))
                            last.then_inc(psum_full, 1)
                        pe.wait_ge(q_exp_ready, (b + 1) * TT)
                        transposes(pe, b, "TQ", q_tm)
                        pe.wait_ge(*wait_drained(b, "A", DT - 1))
                        pe.wait_ge(*wait_drained(b, "TQ", DT - 1))
                        for t in range(TT):
                            wait_bank(pe, b, "Y", t)
                            for g in range(DT):
                                last = pe.matmul(bank_of("Y", t)[:, g * P:(g + 1) * P], q_t[:, g, t * P:(t + 1) * P],
                                                 attn[:, g, :], start=True, stop=True)
                            last.then_inc(psum_full, 1)
                    else:
                        project_t(pe, b, "Q", wq)
                        project(pe, b, "V", xn_t, wv)
                        attention_pe(pe, b)
                    pe.wait_ge(yn_ready, (b + 1) * TT)
                    transposes(pe, b, "TY", y)
                    pe.wait_ge(*wait_drained(b, "TY", DT - 1))
                    project(pe, b, "O", h_t, wo)

                batches(pe, body)

            @block.vector
            def _(dve):
                dve.sem_inc(drained["dve"], st.per["dve"])
                dve.sem_inc(mask_ready, 1)
                dve.wait_ge(w_loaded, 9 * 16)
                if layer == 0:
                    dve.tensor_scalar(keep[:, :], keep_in[:, :], 1.0, None, ALU.not_equal).then_inc(const_ready, 1)
                else:
                    dve.tensor_copy(keep[:, :], keep_in[:, :]).then_inc(const_ready, 1)
                dve.wait_ge(const_ready, 1)
                col = lambda v, k: cols[:, v * DT + k:v * DT + k + 1]

                def norm_stats(b, src, out, agg, stats_sem, agg_sem):
                    for t in range(TT):
                        dve.bn_stats(out[:, t, :], src[:, t, :]).then_inc(stats_sem, 1)
                    for t in range(TT):
                        dve.wait_ge(stats_sem, b * TT + t + 1)
                        dve.sem_inc(passed, 1)
                        dve.bn_aggr(agg[:, t, :], out[:, t, :]).then_inc(agg_sem, 1)

                def body(b, pair, j):
                    dve.wait_ge(mask_loaded[j], pair * 16 + 16)
                    if layer == 0:
                        dve.tensor_scalar(mask_add[:, :], mask_in[j][:, :], 1.0, NEG, ALU.is_equal, ALU.mult
                                          ).then_inc(mask_ready, 1)
                    else:
                        dve.tensor_scalar(mask_add[:, :], mask_in[j][:, :], 1.0, 1.0e6, ALU.subtract, ALU.mult
                                          ).then_inc(mask_ready, 1)
                    dve.wait_ge(x_loaded[j], pair * 16 + 16)
                    norm_stats(b, x[j], stats, mv, stats_ready, mv_ready)
                    dve.wait_ge(rstd_ready, b + 1)
                    for t in range(TT):
                        dve.tensor_scalar(xn[:, t, :], x[j][:, t, :], mv[:, t, 0:1], rstd[:, t:t + 1],
                                          ALU.subtract, ALU.mult).then_inc(xn_ready, 1)
                    dve.wait_ge(mask_ready, b + 2)
                    if linear:
                        for k in range(DT):
                            dve.wait_ge(psum_full, st.full(b, "K", k))
                            dve.scalar_tensor_tensor(k_t[:, k, :], bank_of("K", k)[:, :], col(BK, k), mask_add[:, :],
                                                     ALU.add, ALU.add).then_inc(drained["dve"], 1)
                            dve.wait_ge(*wait_drained(b, "K", k))
                            last = dve.reduce_max(k_max[:, k:k + 1], k_t[:, k, :], AX.X)
                        last.then_inc(k_max_ready, 1)
                        dve.wait_ge(k_max_ready, 2 * b + 1)
                        dve.tensor_scalar(k_max[:, :], k_max[:, :], -1.0, None, ALU.mult).then_inc(k_max_ready, 1)
                        for t in range(TT):
                            dve.wait_ge(psum_full, st.full(b, "Q", t))
                            dve.tensor_tensor(q_tm[:, t, :], bank_of("Q", t)[:, :], rows[:, 0, :], ALU.add
                                              ).then_inc(drained["dve"], 1)
                            dve.wait_ge(*wait_drained(b, "Q", t))
                            heads = q_tm[:, t, :].rearrange("p (h e) -> p h e", e=dh)
                            dve.tensor_reduce(q_max[:, t, :], heads, AX.X, ALU.max).then_inc(q_max_ready, 1)
                            dve.wait_ge(q_max_ready, b * TT + t + 1)
                            dve.tensor_tensor(heads, heads, q_max[:, t, :].unsqueeze(2).broadcast_to([P, H, dh]),
                                              ALU.subtract).then_inc(q_sub_ready, 1)
                    if linear:
                        dve.wait_ge(k_exp_ready, (b + 1) * DT)
                        dve.reciprocal(k_sum[:, :], k_sum[:, :]).then_inc(rk_ready, 1)
                        dve.wait_ge(rk_ready, b + 1)
                        if layer == 0:
                            for k in range(DT):
                                dve.tensor_scalar(k_t[:, k, :], k_t[:, k, :], k_sum[:, k:k + 1], None, ALU.mult
                                                  ).then_inc(k_norm_ready, 1)
                    for t in range(TT):
                        dve.wait_ge(psum_full, st.full(b, "V", t))
                        dve.tensor_tensor(v_tm[:, t, :], bank_of("V", t)[:, :], rows[:, 1, :], ALU.add
                                          ).then_inc(drained["dve"], 1)
                        dve.wait_ge(*wait_drained(b, "V", t))
                        dve.tensor_scalar(v_tm[:, t, :], v_tm[:, t, :], keep[:, bass.ds(b * TT + t, 1)], None, ALU.mult
                                          ).then_inc(v_ready, 1)
                    if linear:
                        for t in range(TT):
                            dve.wait_ge(q_exp_ready, b * TT + t + 1)
                            last = dve.reduce_sum(q_sum[:, t, :], q_tm[:, t, :].rearrange("p (h e) -> p h e", e=dh), AX.X)
                        last.then_inc(q_sum_ready, 1)
                        dve.wait_ge(q_sum_ready, 2 * b + 1)
                        dve.reciprocal(q_sum[:, :, :], q_sum[:, :, :]).then_inc(q_sum_ready, 1)
                        for g in range(DT):
                            dve.wait_ge(psum_full, st.full(b, "A", g))
                            if layer == 0:
                                ins = dve.tensor_tensor(attn[:, g, :], bank_of("A", g)[:, 0:P], block_mask[:, :],
                                                        ALU.mult)
                            else:
                                ins = dve.scalar_tensor_tensor(attn[:, g, :], bank_of("A", g)[:, 0:P],
                                                               k_sum[:, g:g + 1], block_mask[:, :], ALU.mult, ALU.mult)
                            ins.then_inc(drained["dve"], 1)
                        dve.wait_ge(q_sum_ready, 2 * b + 2)
                        for t in range(TT):
                            dve.wait_ge(psum_full, st.full(b, "Y", t))
                            dve.tensor_tensor(y[:, t, :].rearrange("p (h e) -> p h e", e=dh),
                                              bank_of("Y", t)[:, :].rearrange("p (h e) -> p h e", e=dh),
                                              q_sum[:, t, :].unsqueeze(2).broadcast_to([P, H, dh]), ALU.mult
                                              ).then_inc(drained["dve"], 1)
                        dve.wait_ge(*wait_drained(b, "Y", TT - 1))
                    else:
                        attention_dve(dve, b)
                    norm_stats(b, y, y_stats, y_mv, y_stats_ready, y_mv_ready)
                    dve.wait_ge(y_rstd_ready, b + 1)
                    for t in range(TT):
                        dve.tensor_scalar(y[:, t, :], y[:, t, :], y_mv[:, t, 0:1], y_rstd[:, t:t + 1],
                                          ALU.subtract, ALU.mult).then_inc(yn_ready, 1)
                    dve.wait_ge(xb_ready, b + 1)
                    for t in range(TT):
                        dve.wait_ge(psum_full, st.full(b, "O", t))
                        ins = dve.tensor_tensor(x[j][:, t, :], bank_of("O", t)[:, :], x[j][:, t, :], ALU.add)
                        ins.then_inc(drained["dve"], 1)
                    dve.wait_ge(*wait_drained(b, "O", TT - 1))
                    dve.sem_inc(out_ready, TT)

                batches(dve, body)



def ssm_layer(nc, sems, d, mod_all, banks, x_in, x_out):
    plan = [("T", 4, "act")]
    for s in range(2):
        plan += [(f"Z{s}", ET, "act"), (f"DBC{s}", 1, "dve"), (f"TC{s}", 1, "dve"), (f"DL{s}", ET, "dve"),
                 (f"Y{s}0", 4, "dve"), (f"Y{s}1", 4, "dve")]
    plan += [("MX", ET, "act"), ("O", TT, "dve")]
    st = Stages(plan)
    RING = 2
    bank_of = lambda name, k: banks[6 + (st.first[name] + k) % RING]
    GE = 4
    UNITS = 4
    STEPS = UNITS * N
    CH = 4
    with ExitStack() as ctx:
        sb = lambda n, s, t=F32: ctx.enter_context(nc.sbuf_tensor("ssm_" + n, s, t))
        sem = lambda n: sems.take("ssm_" + n)
        ident = sb("ident", [P, P])
        w_a = sb("w_a", [P, DT, E])
        w_b = sb("w_b", [P, DT * E])
        w_b_in = w_b[:, :].rearrange("p (k n) -> p k n", n=E)
        w_b_out = w_b[:, :].rearrange("p (k n) -> p k n", n=D)
        w_dbc = sb("w_dbc", [P, 2, ET, R + 2 * N])
        w_dt = sb("w_dt", [R, 2, E])
        neg_a = sb("neg_a", [P, 2, ET, N])
        bf_row = sb("bf_row", [P, D])
        ada = sb("ada", [P, 3, D])
        minus_half = sb("minus_half", [P, TT])
        work = sb("work", [P, 4, 4, 512])
        d_bu = [work[:, i] for i in range(2)]
        state = [work[:, 2 + i] for i in range(2)]
        x, xs, xn = work[:, 0], work[:, 1], work[:, 2]
        resid = sb("resid", [P, TT, D])
        xn_t = sb("xn_t", [P, DT, T])
        z = sb("z", [P, ET, T])
        delta = sb("delta", [P, ET, T])
        soft = sb("soft", [P, 2, T])
        y_sum = sb("y_sum", [P, ET, T])
        acc = sb("acc", [P, TT, GE * P])
        b_rows = sb("b_rows", [P, 2, CH, T])
        dbc_t = sb("dbc_t", [R + 2 * N, T])
        dbc_tm = sb("dbc_tm", [P, TT, R + 2 * N])
        stats = sb("stats", [P, TT, 6])
        mv = sb("mv", [P, TT, 2])
        rstd = sb("rstd", [P, TT])
        stats2 = sb("stats2", [P, TT, 6])
        mv2 = sb("mv2", [P, TT, 2])
        rstd2 = sb("rstd2", [P, TT])
        cols = mod_all["ssm_cols"]
        bzc = mod_all["bzc"]

        w_loaded, const_ready, passed = sem("w_loaded"), sem("const_ready"), sem("passed")
        half_ready = sem("half_ready")
        x_loaded, x_stored, ada_loaded = sem("x_loaded"), sem("x_stored"), sem("ada_loaded")
        wa_loaded, wb_loaded = sem("wa_loaded"), sem("wb_loaded")
        full = sem("full")
        drained = {"act": sem("act_drained"), "dve": sem("dve_drained")}
        stats_ready, mv_ready, var_ready, rstd_ready = sem("stats_ready"), sem("mv_ready"), sem("var_ready"), sem("rstd_ready")
        stats2_ready, mv2_ready, var2_ready, rstd2_ready = sem("stats2_ready"), sem("mv2_ready"), sem("var2_ready"), sem("rstd2_ready")
        xn_ready, xs_ready, xn2_ready, resid_ready = sem("xn_ready"), sem("xs_ready"), sem("xn2_ready"), sem("resid_ready")
        soft_in, soft_out, delta_ready, u_used, du_ready = sem("soft_in"), sem("soft_out"), sem("delta_ready"), sem("u_used"), sem("du_ready")
        b_stored = sem("b_stored")
        b_loaded = [sem(f"b_loaded{i}") for i in range(2)]
        da_ready, dbu_ready, scanned, turned, added = sem("da_ready"), sem("dbu_ready"), sem("scanned"), sem("turned"), sem("added")
        gated, scaled, out_ready = sem("gated"), sem("scaled"), sem("out_ready")

        def wait_drained(b, name, k):
            engine, count = st.drained(b, name, k)
            return drained[engine], count

        with nc.Block() as block:

            @block.sync
            def _(sp):
                sp.sem_inc(x_stored, 16)
                sp.sem_inc(b_stored, 16)
                sp.dma_start(ident[:, :], d["ident"]).then_inc(w_loaded, 16)
                sp.dma_start(w_dbc[:, :, :, :], d["wdbcT"].rearrange("s (k p) n -> p s k n", p=P)).then_inc(w_loaded, 16)
                sp.dma_start(w_dt[:, :, :], d["wdtT"].rearrange("s r n -> r s n")).then_inc(w_loaded, 16)
                sp.dma_start(neg_a[:, :, :, :].rearrange("p s k n -> p (s k n)"), d["alog"]).then_inc(w_loaded, 16)
                sp.dma_start(bf_row[:, :], d["bf_row"].broadcast_to([P, D])).then_inc(w_loaded, 16)
                with sp.Fori(0, B) as b:
                    sp.wait_ge(full, b * st.n + st.first["MX"] + ET)
                    sp.sem_inc(passed, 1)
                    sp.dma_start(w_a[:, :, :], d["wzc"][0].rearrange("(k p) n -> p k n", p=P)).then_inc(wa_loaded, 16)
                    sp.wait_ge(turned, 1 + b * STEPS * TT)
                    sp.sem_inc(passed, 1)
                    sp.wait_ge(out_ready, 1 + b * TT)
                    sp.sem_inc(passed, 1)
                    sp.dma_start(x, x_in[b].rearrange("(t p) n -> p t n", p=P)).then_inc(x_loaded, 16)
                    sp.dma_start(ada[:, :, :].rearrange("p r n -> p (r n)"), d["ada_d"][bass.ds(b, 1), :].broadcast_to([P, 3 * D])
                                 ).then_inc(ada_loaded, 16)
                    sp.dma_start(w_b_in, d["wzc"][1].rearrange("(k p) n -> p k n", p=P)).then_inc(wb_loaded, 16)
                    for s in range(2):
                        sp.wait_ge(*wait_drained(b, f"DBC{s}", 0))
                        sp.sem_inc(passed, 1)
                        sp.dma_start(d["b_d"][s], dbc_t[R:R + N, :]).then_inc(b_stored, 16)
                        if s == 0:
                            sp.wait_ge(full, st.full(b, "Z0", ET - 1))
                            sp.sem_inc(passed, 1)
                            sp.dma_start(w_a[:, :, :], d["wxT"].rearrange("(k p) n -> p k n", p=P)
                                         ).then_inc(wa_loaded, 16)
                        else:
                            sp.wait_ge(full, st.full(b, "Z1", ET - 1))
                            sp.sem_inc(passed, 1)
                            sp.dma_start(w_b_out, d["wfT"].rearrange("(k p) n -> p k n", p=P)
                                         ).then_inc(wb_loaded, 16)
                        sp.wait_ge(b_stored, 16 + b * 32 + s * 16 + 16)
                        sp.sem_inc(passed, 1)
                        for g in range(2):
                            for c in range(N // CH):
                                i = (s * 2 + g) * (N // CH) + c
                                if i >= 2:
                                    sp.wait_ge(dbu_ready, 1 + b * STEPS + (i - 1) * CH)
                                    sp.sem_inc(passed, 1)
                                else:
                                    sp.wait_ge(dbu_ready, 1 + b * STEPS)
                                    sp.sem_inc(passed, 1)
                                sp.dma_start(b_rows[:, i % 2, :, :].rearrange("p c n -> p (c n)"),
                                             d["b_flat"][s:s + 1, c * CH * T:(c + 1) * CH * T].broadcast_to([P, CH * T])
                                             ).then_inc(b_loaded[i % 2], 16)
                    sp.wait_ge(out_ready, 1 + (b + 1) * TT)
                    sp.sem_inc(passed, 1)
                    sp.dma_start(x_out[b].rearrange("(t p) n -> p t n", p=P), resid[:, :, :]).then_inc(x_stored, 16)
                sp.wait_ge(x_stored, 16 + B * 16)

            @block.gpsimd
            def _(pool):
                pool.sem_inc(dbu_ready, 1)
                pool.memset(minus_half[:, :], -0.5).then_inc(half_ready, 1)
                pool.wait_ge(half_ready, 1)
                pool.wait_ge(w_loaded, 5 * 16)

                def rsqrt(b, agg, out, agg_sem, var_sem, out_sem):
                    pool.wait_ge(agg_sem, (b + 1) * TT)
                    pool.sem_inc(passed, 1)
                    pool.tensor_scalar(out[:, :], agg[:, :, 1], EPS, 0.0, ALU.add, ALU.add).then_inc(var_sem, 1)
                    pool.wait_ge(var_sem, b + 1)
                    pool.tensor_tensor(out[:, :], out[:, :], minus_half[:, :], ALU.pow).then_inc(out_sem, 1)

                with pool.Fori(0, B) as b:
                    rsqrt(b, mv, rstd, mv_ready, var_ready, rstd_ready)
                    rsqrt(b, mv2, rstd2, mv2_ready, var2_ready, rstd2_ready)
                    pool.wait_ge(x_stored, 16 + b * 16)
                    for i in range(3):
                        if i:
                            pool.wait_ge(resid_ready, b * 3 + i)
                        if i == 0:
                            ins = pool.tensor_tensor(resid[:, :, :], xs, bf_row[:, :].unsqueeze(1).broadcast_to([P, TT, D]), ALU.add)
                        elif i == 1:
                            ins = pool.tensor_tensor(resid[:, :, :], resid[:, :, :], ada[:, 2, :].unsqueeze(1).broadcast_to([P, TT, D]), ALU.mult)
                        else:
                            ins = pool.tensor_tensor(resid[:, :, :], resid[:, :, :], x, ALU.add)
                        ins.then_inc(resid_ready, 1)
                    for s in range(2):
                        for m in range(ET):
                            pool.wait_ge(delta_ready, (b * 2 + s) * ET + m + 1)
                            pool.wait_ge(u_used, (b * 2 + s) * ET + m + 1)
                            pool.tensor_tensor(z[:, m, :], z[:, m, :], delta[:, m, :], ALU.mult).then_inc(du_ready, 1)
                        pool.wait_ge(du_ready, (b * 2 + s + 1) * ET)
                        pool.wait_ge(resid_ready, b * 3 + 3)
                        pool.wait_ge(full, st.full(b, "T", 3))
                        for g in range(2):
                            for c in range(N // CH):
                                i = (s * 2 + g) * (N // CH) + c
                                pool.wait_ge(b_loaded[i % 2], (b * UNITS * N // CH // 2 + i // 2 + 1) * 16)
                                for k in range(CH):
                                    at = i * CH + k
                                    if at >= 2:
                                        pool.wait_ge(scanned, 2 + (b * STEPS + at - 1) * GE)
                                    else:
                                        pool.wait_ge(scanned, 2 + b * STEPS * GE)
                                    pool.tensor_tensor(d_bu[at % 2], z[:, g * GE:(g + 1) * GE, :],
                                                       b_rows[:, i % 2, k, :].unsqueeze(1).broadcast_to([P, GE, T]),
                                                       ALU.mult).then_inc(dbu_ready, 1)

            @block.scalar
            def _(act):
                act.sem_inc(drained["act"], st.per["act"])
                act.wait_ge(w_loaded, 5 * 16)
                flat = neg_a[:, :, :, :].rearrange("p s k n -> p (s k n)")
                act.activation(flat, flat, ACT.Exp).then_inc(const_ready, 1)
                act.wait_ge(const_ready, 1)
                act.activation(flat, flat, ACT.Copy, scale=-1.0).then_inc(const_ready, 1)
                act.wait_ge(const_ready, 2)

                def drain(b, name, k, out, func, **kw):
                    act.wait_ge(full, st.full(b, name, k))
                    act.activation(out, bank_of(name, k)[:, :], func, **kw).then_inc(drained["act"], 1)

                with act.Fori(0, B) as b:
                    for k in range(DT):
                        drain(b, "T", k, xn_t[:, k, :], ACT.Identity, scale=cols[:, G2 + k:G2 + k + 1],
                              bias=cols[:, B2 + k:B2 + k + 1])
                    for s in range(2):
                        if s == 1:
                            act.wait_ge(dbu_ready, 1 + b * STEPS + STEPS // 2)
                        else:
                            act.wait_ge(dbu_ready, 1 + b * STEPS)
                        for m in range(ET):
                            drain(b, f"Z{s}", m, z[:, m, :], ACT.Identity, bias=bzc[:, s * ET + m:s * ET + m + 1])
                        act.preload_act_table_set("natural_log_exp_and_others")
                        for m in range(ET):
                            i = (b * 2 + s) * ET + m
                            act.wait_ge(soft_in, i + 1)
                            act.activation(soft[:, m % 2, :], soft[:, m % 2, :], ACT.Exp).then_inc(soft_out, 1)
                            act.wait_ge(soft_out, 2 * i + 1)
                            act.activation(soft[:, m % 2, :], soft[:, m % 2, :], ACT.Ln, bias=1.0).then_inc(soft_out, 1)
                        act.wait_ge(delta_ready, (b * 2 + s + 1) * ET)
                        for g in range(2):
                            u = s * 2 + g
                            with act.Fori(0, N) as n:
                                for e in range(GE):
                                    at = (b * STEPS + u * N + n) * GE + e
                                    act.wait_ge(scanned, at + 1)
                                    act.activation(banks[e % 2][:, :], delta[:, g * GE + e, :], ACT.Exp,
                                                   scale=neg_a[:, s, g * GE + e, bass.ds(n, 1)]).then_inc(da_ready, 1)
                    for m in range(ET):
                        if m == 0:
                            act.wait_ge(da_ready, (b + 1) * STEPS * GE)
                        drain(b, "MX", m, delta[:, m, :], ACT.Silu, bias=cols[:, BX + m:BX + m + 1])

            @block.tensor
            def _(pe):
                pe.sem_inc(full, st.n)
                pe.sem_inc(turned, 1)
                pe.wait_ge(w_loaded, 5 * 16)

                def wait_bank(b, name, k):
                    engine, count = st.before(b, name, k, RING)
                    pe.wait_ge(drained[engine], count)

                def products(b, name, k, pairs, rows_out=P):
                    wait_bank(b, name, k)
                    for i, (lhs_t, rhs) in enumerate(pairs):
                        last = pe.matmul(bank_of(name, k)[0:rows_out, :], lhs_t, rhs, start=(i == 0),
                                         stop=(i == len(pairs) - 1))
                    last.then_inc(full, 1)

                with pe.Fori(0, B) as b:
                    pe.wait_ge(xn2_ready, (b + 1) * TT)
                    for k in range(DT):
                        wait_bank(b, "T", k)
                        for t in range(TT):
                            last = pe.transpose(bank_of("T", k)[:, t * P:(t + 1) * P], xn[:, t, k * P:(k + 1) * P], ident[:, :])
                        last.then_inc(full, 1)
                    pe.wait_ge(*wait_drained(b, "T", DT - 1))
                    for s in range(2):
                        weight = w_a if s == 0 else w_b_in
                        pe.wait_ge(wa_loaded if s == 0 else wb_loaded, b * 32 + 16)
                        for m in range(ET):
                            products(b, f"Z{s}", m, [(weight[:, k, m * P:(m + 1) * P], xn_t[:, k, :]) for k in range(DT)])
                        pe.wait_ge(*wait_drained(b, f"Z{s}", ET - 1))
                        products(b, f"DBC{s}", 0, [(w_dbc[:, s, k, :], z[:, k, :]) for k in range(ET)], R + 2 * N)
                        pe.wait_ge(*wait_drained(b, f"DBC{s}", 0))
                        wait_bank(b, f"TC{s}", 0)
                        for t in range(TT):
                            last = pe.transpose(bank_of(f"TC{s}", 0)[:, t * 96:(t + 1) * 96],
                                                dbc_t[:, t * P:(t + 1) * P], ident[0:96, 0:96])
                        last.then_inc(full, 1)
                        for m in range(ET):
                            products(b, f"DL{s}", m, [(w_dt[:, s, m * P:(m + 1) * P], dbc_t[0:R, :])])
                        for g in range(2):
                            u = s * 2 + g
                            with pe.Fori(0, N // 2) as pair:
                                for j in range(2):
                                    step = b * STEPS + u * N + pair * 2 + j
                                    pe.wait_ge(scanned, 2 + (step + 1) * GE)
                                    for t in range(TT):
                                        pe.wait_ge(added, step * TT + t + 1)
                                        for e in range(GE):
                                            last = pe.transpose(banks[2 + t][:, e * P:(e + 1) * P],
                                                                state[j][:, e, t * P:(t + 1) * P], ident[:, :])
                                        last.then_inc(turned, 1)
                            pe.wait_ge(added, (b * STEPS + (u + 1) * N) * TT + TT)
                            for e in range(GE):
                                wait_bank(b, f"Y{s}{g}", e)
                                for t in range(TT):
                                    last = pe.transpose(bank_of(f"Y{s}{g}", e)[:, t * P:(t + 1) * P],
                                                        acc[:, t, e * P:(e + 1) * P], ident[:, :])
                                last.then_inc(full, 1)
                    pe.wait_ge(wa_loaded, b * 32 + 32)
                    for m in range(ET):
                        products(b, "MX", m, [(w_a[:, k, m * P:(m + 1) * P], xn_t[:, k, :]) for k in range(DT)])
                    pe.wait_ge(wb_loaded, b * 32 + 32)
                    pe.wait_ge(gated, (b + 1) * ET)
                    for t in range(TT):
                        products(b, "O", t, [(y_sum[:, k, t * P:(t + 1) * P], w_b_out[:, k, :]) for k in range(ET)])

            @block.vector
            def _(dve):
                dve.sem_inc(drained["dve"], st.per["dve"])
                dve.sem_inc(added, TT)
                dve.sem_inc(scanned, 2)
                dve.sem_inc(out_ready, 1)
                dve.wait_ge(w_loaded, 5 * 16)
                dve.wait_ge(const_ready, 2)

                with dve.Fori(0, B) as b:
                    dve.wait_ge(x_loaded, b * 16 + 16)
                    dve.wait_ge(ada_loaded, b * 16 + 16)
                    for t in range(TT):
                        dve.bn_stats(stats[:, t, :], x[:, t, :]).then_inc(stats_ready, 1)
                    for t in range(TT):
                        dve.wait_ge(stats_ready, b * TT + t + 1)
                        dve.sem_inc(passed, 1)
                        dve.bn_aggr(mv[:, t, :], stats[:, t, :]).then_inc(mv_ready, 1)
                    dve.wait_ge(rstd_ready, b + 1)
                    for t in range(TT):
                        dve.tensor_scalar(xs[:, t, :], x[:, t, :], mv[:, t, 0:1], rstd[:, t:t + 1],
                                          ALU.subtract, ALU.mult).then_inc(xn_ready, 1)
                    for t in range(TT):
                        dve.wait_ge(xn_ready, b * TT + t + 1)
                        dve.tensor_tensor(xs[:, t, :], xs[:, t, :], ada[:, 0, :], ALU.mult).then_inc(xs_ready, 1)
                    for t in range(TT):
                        dve.wait_ge(xs_ready, b * 2 * TT + t + 1)
                        dve.tensor_tensor(xs[:, t, :], xs[:, t, :], ada[:, 1, :], ALU.add).then_inc(xs_ready, 1)
                    for t in range(TT):
                        dve.wait_ge(xs_ready, b * 2 * TT + TT + t + 1)
                        dve.bn_stats(stats2[:, t, :], xs[:, t, :]).then_inc(stats2_ready, 1)
                    for t in range(TT):
                        dve.wait_ge(stats2_ready, b * TT + t + 1)
                        dve.sem_inc(passed, 1)
                        dve.bn_aggr(mv2[:, t, :], stats2[:, t, :]).then_inc(mv2_ready, 1)
                    dve.wait_ge(rstd2_ready, b + 1)
                    for t in range(TT):
                        dve.tensor_scalar(xn[:, t, :], xs[:, t, :], mv2[:, t, 0:1], rstd2[:, t:t + 1],
                                          ALU.subtract, ALU.mult).then_inc(xn2_ready, 1)
                    for s in range(2):
                        for m in range(ET):
                            dve.wait_ge(*wait_drained(b, f"Z{s}", m))
                            dp = cols[:, DPC + s * ET + m:DPC + s * ET + m + 1]
                            if s == 0:
                                ins = dve.tensor_scalar(y_sum[:, m, :], z[:, m, :], dp, None, ALU.mult)
                            else:
                                ins = dve.scalar_tensor_tensor(y_sum[:, m, :], z[:, m, :], dp, y_sum[:, m, :],
                                                               ALU.mult, ALU.add)
                            ins.then_inc(u_used, 1)
                        dve.wait_ge(full, st.full(b, f"DBC{s}", 0))
                        dve.wait_ge(b_stored, 16 + b * 32 + s * 16)
                        dve.tensor_copy(dbc_t[:, :], bank_of(f"DBC{s}", 0)[0:96, :]).then_inc(drained["dve"], 1)
                        dve.wait_ge(full, st.full(b, f"TC{s}", 0))
                        dve.tensor_copy(dbc_tm[:, :, :].rearrange("p t n -> p (t n)"),
                                        bank_of(f"TC{s}", 0)[:, 0:TT * 96]).then_inc(drained["dve"], 1)

                        def finish(m):
                            i = (b * 2 + s) * ET + m
                            dve.wait_ge(soft_out, 2 * i + 2)
                            dve.tensor_tensor(delta[:, m, :], delta[:, m, :], soft[:, m % 2, :], ALU.max
                                              ).then_inc(delta_ready, 1)

                        for m in range(ET):
                            dve.wait_ge(full, st.full(b, f"DL{s}", m))
                            bias = cols[:, BDT + s * ET + m:BDT + s * ET + m + 1]
                            dve.tensor_scalar(delta[:, m, :], bank_of(f"DL{s}", m)[:, :], bias, None, ALU.add
                                              ).then_inc(drained["dve"], 1)
                            if m >= 2:
                                finish(m - 2)
                            dve.wait_ge(*wait_drained(b, f"DL{s}", m))
                            if m >= 2:
                                dve.wait_ge(delta_ready, (b * 2 + s) * ET + m - 1)
                            dve.tensor_scalar(soft[:, m % 2, :], delta[:, m, :], SP_CAP, None, ALU.min
                                              ).then_inc(soft_in, 1)
                        finish(ET - 2)
                        finish(ET - 1)
                        dve.wait_ge(*wait_drained(b, f"TC{s}", 0))
                        for g in range(2):
                            u = s * 2 + g
                            order = slice(None, None, -1 if s else 1)

                            def scan(step, j):
                                dve.wait_ge(dbu_ready, 1 + step + 1)
                                for e in range(GE):
                                    dve.wait_ge(da_ready, step * GE + e + 1)
                                    dve.tensor_tensor_scan(state[j][:, e, order], banks[e % 2][:, order],
                                                           d_bu[j][:, e, order], 0.0, ALU.mult, ALU.add
                                                           ).then_inc(scanned, 1)

                            def add(step, n, first=False):
                                for t in range(TT):
                                    dve.wait_ge(turned, 1 + step * TT + t + 1)
                                    c = dbc_tm[:, t, R + N:R + N + 1] if first else dbc_tm[:, t, bass.ds(n + (R + N), 1)]
                                    if first:
                                        ins = dve.tensor_scalar(acc[:, t, :], banks[2 + t][:, :], c, None, ALU.mult)
                                    else:
                                        dve.wait_ge(added, step * TT + t + 1)
                                        ins = dve.scalar_tensor_tensor(acc[:, t, :], banks[2 + t][:, :], c, acc[:, t, :],
                                                                       ALU.mult, ALU.add)
                                    ins.then_inc(added, 1)

                            base = b * STEPS + u * N
                            scan(base, 0)
                            scan(base + 1, 1)
                            add(base, 0, first=True)
                            with dve.Fori(1, N // 2) as pair:
                                n = pair * 2
                                scan(base + n, 0)
                                add(base + n - 1, n - 1)
                                scan(base + n + 1, 1)
                                add(base + n, n)
                            add(base + N - 1, N - 1)
                            for e in range(GE):
                                dve.wait_ge(full, st.full(b, f"Y{s}{g}", e))
                                dve.tensor_tensor(y_sum[:, g * GE + e, :], bank_of(f"Y{s}{g}", e)[:, :],
                                                  y_sum[:, g * GE + e, :], ALU.add).then_inc(drained["dve"], 1)
                    dve.wait_ge(*wait_drained(b, "Y11", GE - 1))
                    for m in range(ET):
                        dve.wait_ge(*wait_drained(b, "MX", m))
                        dve.tensor_tensor(y_sum[:, m, :], y_sum[:, m, :], delta[:, m, :], ALU.mult).then_inc(gated, 1)
                    dve.wait_ge(resid_ready, b * 3 + 3)
                    for t in range(TT):
                        dve.wait_ge(full, st.full(b, "O", t))
                        dve.tensor_tensor(xn_t[:, t, :], bank_of("O", t)[:, :], ada[:, 2, :], ALU.mult
                                          ).then_inc(drained["dve"], 1)
                        dve.wait_ge(*wait_drained(b, "O", t))
                        dve.tensor_tensor(resid[:, t, :], resid[:, t, :], xn_t[:, t, :], ALU.add).then_inc(out_ready, 1)


def program(nc, d, out):
    with ExitStack() as ctx:
        banks = [ctx.enter_context(nc.psum_tensor(f"bank{i}", [P, 512], F32)) for i in range(8)]
        sb = lambda n, s: ctx.enter_context(nc.sbuf_tensor(n, s, F32))
        mod_all = {"gain": sb("gain", [P, 3, DT, B]), "shift": sb("shift", [P, 3, DT, B]),
                   "ssm_cols": sb("ssm_cols", [P, 72]), "bzc": sb("bzc", [P, 16])}
        d = dict(d)
        for name, shape in (("wzc", [2, D, E]), ("ada_d", [B, 3 * D]), ("b_d", [2, N, T]),
                            ("x1", [B, T, D]), ("x2", [B, T, D]), ("x3", [B, T, D])):
            d[name] = nc.dram_tensor(name, shape, F32, kind="Internal").ap()
        d["b_flat"] = d["b_d"].rearrange("s n t -> s (n t)")
        cols_loaded = ctx.enter_context(nc.semaphore("cols_loaded"))
        with nc.Block() as block:

            @block.sync
            def _(sp):
                sp.dma_start(mod_all["ssm_cols"][:, :], d["ssm_cols"]).then_inc(cols_loaded, 16)
                sp.wait_ge(cols_loaded, 16)

        sems = LayerSemaphores(nc)
        prologue(nc, sems, d, mod_all, banks)
        sems.clear()
        attention_layer(nc, sems, d, mod_all, banks, 0, d["x"], d["x1"])
        sems.clear()
        attention_layer(nc, sems, d, mod_all, banks, 1, d["x1"], d["x2"])
        sems.clear()
        attention_layer(nc, sems, d, mod_all, banks, 2, d["x2"], d["x3"])
        sems.clear()
        ssm_layer(nc, sems, d, mod_all, banks, d["x3"], out)


def kernel(**inputs):
    import numpy as np
    import concourse.bacc as bacc
    from concourse.bass_utils import run_bass_kernel_spmd

    v = {k: np.asarray(a) for k, a in inputs.items()}
    col = lambda a: a.reshape(-1, P).T
    layers = [
        dict(n="L0_cond_", nw="norm_scale", nb="norm_bias", wq="Wq", wk="Wk", wv="Wv", wo="film_out_W", bq="bq",
             bk="bk", bv="bv", bo="film_out_b", mw="film_emb_W", mb="film_emb_b", n2w="film_norm_scale",
             n2b="film_norm_bias"),
        dict(n="L1_cond_", nw="ln_w", nb="ln_b", wq="Wq", wk="Wk", wv="Wv", wo="W_out", bq="bq", bk="bk", bv="bv",
             bo="b_out", mw="W_emb", mb="b_emb", n2w="ln2_w", n2b="ln2_b"),
        dict(n="L2_cond_", nw="norm_w", nb="norm_b", wq="q_w", wk="k_w", wv="v_w", wo="out_w", bq="q_b", bk="k_b",
             bv="v_b", bo="out_b", mw="emb_w", mb="emb_b", n2w="sb_norm_w", n2b="sb_norm_b"),
    ]
    g = lambda l, key: v[l["n"] + l[key]]
    s = lambda key: v["L3_cond_" + key]
    arrays = {
        "x": v["x"],
        "cond": v["cond_2048"],
        "ident": np.eye(P, dtype=np.float32),
        "block_masks": np.stack([np.kron(np.eye(P // w), np.ones((w, w))) for w in (32, 64)], 1).astype(np.float32),
        "att_w": np.stack([np.stack([g(l, k) for k in ("wq", "wk", "wv", "wo")]) for l in layers]),
        "mod_w": np.stack([g(l, "mw") for l in layers]),
        "att_cols": np.stack([np.concatenate([col(a) for a in (g(l, "nw"), g(l, "nb"), g(l, "bq"), g(l, "bk"),
                                                               g(l, "mb")[:D], g(l, "mb")[D:], g(l, "n2w"),
                                                               g(l, "n2b"))], 1) for l in layers], 1),
        "att_rows": np.stack([np.concatenate([g(l, "bq"), g(l, "bv"), g(l, "bo")]) for l in layers]),
        "ada_wT": s("Wada").T,
        "ada_rows": np.concatenate([s("norm1_g"), s("norm1_b"), s("bada")])[None],
        "wz": s("Wz"),
        "wcT": np.stack([s("Wc1").T, s("Wc2").T]),
        "wxT": s("Wx").T,
        "wfT": s("Wf").T,
        "wdbcT": np.stack([s("Wdbc1").T, s("Wdbc2").T]),
        "wdtT": np.stack([s("Wdt1").T, s("Wdt2").T]),
        "alog": np.stack([s("Alog1"), s("Alog2")]).reshape(2, ET, P, N).transpose(2, 0, 1, 3).reshape(P, -1),
        "ssm_cols": np.concatenate([col(s(k)) for k in ("norm2_g", "norm2_b", "bx", "bc1", "bc2", "bz", "bdt1",
                                                        "bdt2", "Dp1", "Dp2")], 1),
        "bf_row": s("bf")[None],
    }
    for i, key in enumerate(("mask_BxS_ik0", "mask_BxSx1_fk1", "mask_BxS_ff1")):
        m = v[key].reshape(B, T)
        arrays[f"mask{i}"] = m[:, None]
        arrays[f"mask{i}_t"] = m.reshape(B * TT, P).T
    nc = bacc.Bacc("TRN2", target_bir_lowering=False, num_devices=1)
    maps, d = {}, {}
    for name, a in arrays.items():
        a = np.ascontiguousarray(a)
        maps["in_" + name] = a
        d[name] = nc.dram_tensor("in_" + name, a.shape, mybir.dt.from_np(a.dtype), kind="ExternalInput").ap()
    out = nc.dram_tensor("out_0", (B, T, D), F32, kind="ExternalOutput").ap()
    program(nc, d, out)
    r = run_bass_kernel_spmd(nc, [maps], core_ids=[0])
    return r.results[0]["out_0"]
```

```python
import concourse.bass as bass
from concourse import mybir
from contextlib import ExitStack

F32 = mybir.dt.float32
I32 = mybir.dt.int32
ALU = mybir.AluOpType
ACT = mybir.ActivationFunctionType
AX = mybir.AxisListType

P = 128
B = 8
T = 512
D = 512
E = 1024
N = 16
R = 64
TT = T // P
DT = D // P
ET = E // P
EPS = 1e-5
NEG = -1.0e30
SP_CAP = 40.0

NW, NB, BQ, BK, FS, FH, N2W, N2B = range(8)
G2, B2, BX, BC, BZ, BDT, DPC = 0, 4, 8, 16, 32, 40, 56


class Stages:

    def __init__(self, plan):
        self.first, self.by, self.per = {}, [], {}
        for name, n, engine in plan:
            self.first[name] = len(self.by)
            self.by += [engine] * n
        for engine in set(self.by):
            self.per[engine] = self.by.count(engine)
        self.n = len(self.by)

    def full(self, b, name, k=0):
        return (b + 1) * self.n + self.first[name] + k + 1

    def drained(self, b, name, k=0):
        at = self.first[name] + k
        engine = self.by[at]
        return engine, (b + 1) * self.per[engine] + self.by[: at + 1].count(engine)

    def before(self, b, name, k, ring):
        at = self.first[name] + k - ring
        if at >= 0:
            engine = self.by[at]
            return engine, (b + 1) * self.per[engine] + self.by[: at + 1].count(engine)
        engine = self.by[at + self.n]
        return engine, b * self.per[engine] + self.by[: at + self.n + 1].count(engine)


class LayerSemaphores:

    def __init__(self, nc):
        self.nc, self.held = nc, []

    def take(self, name):
        self.held.append(self.nc.alloc_semaphore(name=name))
        return self.held[-1]

    def clear(self):
        self.nc.clear_and_free_semaphores(self.held)
        self.held = []
        self.nc.all_engine_barrier()


def prologue(nc, sems, d, mod_all, banks):
    with ExitStack() as ctx:
        sb = lambda n, s, t=F32: ctx.enter_context(nc.sbuf_tensor("pro_" + n, s, t))
        sem = lambda n: sems.take("pro_" + n)
        cond = sb("cond", [B, E])
        ident = sb("ident", [P, P])
        silu_t = sb("silu_t", [P, ET, B])
        w_mod = [sb(f"w_mod{i}", [P, ET, 512]) for i in range(2)]
        cols = sb("cols", [P, 3, 8 * DT])
        raw = sb("raw", [P, 2 * DT, B])
        ada_bias = sb("ada_bias", [B, 5, D])
        ada = sb("ada", [B, 3, D])
        wz = sb("wz", [P, ET, D])
        wc = sb("wc", [P, ET, E])
        fused = [sb(f"fused{i}", [P, D]) for i in range(2)]

        loaded, stored = sem("loaded"), [sem(f"stored{i}") for i in range(2)]
        w_loaded = [sem(f"w_loaded{i}") for i in range(2)]
        wc_loaded, silu_ready, silu_t_full, silu_t_ready = sem("wc"), sem("silu"), sem("silu_t_full"), sem("silu_t")
        full, drained, mod_step, ada_ready = sem("full"), sem("drained"), sem("mod_step"), sem("ada_ready")
        fused_full, fused_ready = sem("fused_full"), sem("fused_ready")
        pieces = [(d["mod_w"][l], 512 * h) for l in range(3) for h in range(2)]
        pieces += [(d["ada_wT"], 512 * h) for h in range(3)]
        with nc.Block() as block:

            @block.sync
            def _(sp):
                sp.dma_start(cond[:, :], d["cond"]).then_inc(loaded, 16)
                sp.dma_start(ident[:, :], d["ident"]).then_inc(loaded, 16)
                sp.dma_start(cols[:, :, :], d["att_cols"]).then_inc(loaded, 16)
                sp.dma_start(ada_bias[:, :, :].rearrange("b r n -> b (r n)"),
                             d["ada_rows"].broadcast_to([B, 5 * D])).then_inc(loaded, 16)
                sp.dma_start(wz[:, :, :], d["wz"].rearrange("(k p) n -> p k n", p=P)).then_inc(loaded, 16)
                for i, (w, c0) in enumerate(pieces):
                    if i >= 2:
                        sp.wait_ge(full, i - 1)
                    sp.dma_start(w_mod[i % 2][:, :, :], w[:, c0:c0 + 512].rearrange("(k p) n -> p k n", p=P)
                                 ).then_inc(w_loaded[i % 2], 16)
                sp.dma_start(wc[:, :, :], d["wcT"][0].rearrange("(k p) n -> p k n", p=P)).then_inc(wc_loaded, 16)
                for s in range(2):
                    for m in range(DT * 2):
                        i = s * 8 + m
                        sp.wait_ge(fused_ready, i + 1)
                        sp.dma_start(d["wzc"][s, (m // 2) * P:(m // 2 + 1) * P, (m % 2) * 512:(m % 2 + 1) * 512],
                                     fused[i % 2][:, :]).then_inc(stored[i % 2], 16)
                    if s == 0:
                        sp.wait_ge(fused_full, 9)
                        sp.dma_start(wc[:, :, :], d["wcT"][1].rearrange("(k p) n -> p k n", p=P)
                                     ).then_inc(wc_loaded, 16)
                sp.wait_ge(ada_ready, 1)
                sp.dma_start(d["ada_d"], ada[:, :, :].rearrange("b r n -> b (r n)")).then_inc(loaded, 16)
                sp.wait_ge(loaded, 96)
                for i in range(2):
                    sp.wait_ge(stored[i], 128)

            @block.scalar
            def _(act):
                act.wait_ge(loaded, 80)
                act.activation(cond[:, :], cond[:, :], ACT.Silu).then_inc(silu_ready, 1)

            @block.tensor
            def _(pe):
                pe.wait_ge(silu_ready, 1)
                for k in range(ET):
                    last = pe.transpose(banks[0][:, k * B:(k + 1) * B], cond[:, k * P:(k + 1) * P], ident[0:B, 0:B])
                last.then_inc(silu_t_full, 1)
                pe.wait_ge(silu_t_ready, 1)
                for i in range(9):
                    pe.wait_ge(w_loaded[i % 2], 16 * (i // 2 + 1))
                    if i >= 2:
                        pe.wait_ge(drained, i - 1)
                    bank = banks[1 + i % 2]
                    if i < 6:
                        for m in range(4):
                            for k in range(ET):
                                last = pe.matmul(bank[:, m * B:(m + 1) * B], w_mod[i % 2][:, k, m * P:(m + 1) * P],
                                                 silu_t[:, k, :], start=(k == 0), stop=(k == ET - 1))
                    else:
                        for k in range(ET):
                            last = pe.matmul(bank[0:B, :], silu_t[:, k, :], w_mod[i % 2][:, k, :],
                                             start=(k == 0), stop=(k == ET - 1))
                    last.then_inc(full, 1)
                for s in range(2):
                    pe.wait_ge(wc_loaded, 16 * (s + 1))
                    for m in range(8):
                        i = s * 8 + m
                        if i >= 2:
                            pe.wait_ge(fused_ready, i - 1)
                        for k in range(ET):
                            last = pe.matmul(banks[3 + i % 2][:, :], wz[:, k, (m // 2) * P:(m // 2 + 1) * P],
                                             wc[:, k, (m % 2) * 512:(m % 2 + 1) * 512],
                                             start=(k == 0), stop=(k == ET - 1))
                        last.then_inc(fused_full, 1)
                    for m in range(ET):
                        for k in range(ET):
                            last = pe.matmul(banks[5][:, s * 8 + m:s * 8 + m + 1], wc[:, k, m * P:(m + 1) * P],
                                             mod_all["ssm_cols"][:, BZ + k:BZ + k + 1],
                                             start=(k == 0), stop=(k == ET - 1))
                    last.then_inc(fused_full, 1)

            @block.vector
            def _(dve):
                steps = [0]

                def step(ins):
                    ins.then_inc(mod_step, 1)
                    steps[0] += 1
                    dve.wait_ge(mod_step, steps[0])

                dve.wait_ge(silu_t_full, 1)
                dve.tensor_copy(silu_t[:, :, :].rearrange("p k b -> p (k b)"), banks[0][:, 0:ET * B]
                                ).then_inc(silu_t_ready, 1)
                dve.wait_ge(loaded, 80)
                col = lambda l, v: cols[:, l, v * DT:(v + 1) * DT].unsqueeze(2).broadcast_to([P, DT, B])
                for l in range(3):
                    for h, v in ((0, FS), (1, FH)):
                        i = 2 * l + h
                        dve.wait_ge(full, i + 1)
                        ins = dve.tensor_tensor(raw[:, h * DT:(h + 1) * DT, :],
                                                banks[1 + i % 2][:, 0:DT * B].rearrange("p (m b) -> p m b", b=B),
                                                col(l, v), ALU.add)
                        ins.then_inc(drained, 1)
                        dve.wait_ge(drained, i + 1)
                    gain, shift = mod_all["gain"][:, l, :, :], mod_all["shift"][:, l, :, :]
                    step(dve.tensor_scalar(raw[:, 0:DT, :], raw[:, 0:DT, :], 1.0, None, ALU.add))
                    step(dve.tensor_tensor(gain, raw[:, 0:DT, :], col(l, N2W), ALU.mult))
                    step(dve.tensor_tensor(shift, raw[:, 0:DT, :], col(l, N2B), ALU.mult))
                    step(dve.tensor_tensor(shift, shift, raw[:, DT:2 * DT, :], ALU.add))
                for h in range(3):
                    dve.wait_ge(full, 7 + h)
                    dve.tensor_tensor(ada[:, h, :], banks[1 + (6 + h) % 2][0:B, :], ada_bias[:, 2 + h, :], ALU.add
                                      ).then_inc(drained, 1)
                dve.wait_ge(drained, 9)
                step(dve.tensor_scalar(ada[:, 1, :], ada[:, 1, :], 1.0, None, ALU.add))
                step(dve.tensor_tensor(ada_bias[:, 1, :], ada_bias[:, 1, :], ada[:, 1, :], ALU.mult))
                step(dve.tensor_tensor(ada_bias[:, 1, :], ada_bias[:, 1, :], ada[:, 0, :], ALU.add))
                step(dve.tensor_tensor(ada[:, 0, :], ada[:, 1, :], ada_bias[:, 0, :], ALU.mult))
                step(dve.tensor_copy(ada[:, 1, :], ada_bias[:, 1, :]))
                dve.sem_inc(ada_ready, 1)
                for s in range(2):
                    for m in range(8):
                        i = s * 8 + m
                        dve.wait_ge(fused_full, s * 9 + m + 1)
                        if i >= 2:
                            dve.wait_ge(stored[i % 2], 16 * (i // 2))
                        dve.tensor_copy(fused[i % 2][:, :], banks[3 + i % 2][:, :]).then_inc(fused_ready, 1)
                dve.wait_ge(fused_full, 18)
                dve.tensor_tensor(mod_all["bzc"][:, :], banks[5][:, 0:16], mod_all["ssm_cols"][:, BC:BC + 16], ALU.add)


def attention_layer(nc, sems, d, mod_all, banks, layer, x_in, x_out):
    H = (16, 8, 16)[layer]
    dh = D // H
    linear = layer < 2
    if linear:
        plan = [("T", 4, "act"), ("K", 4, "dve"), ("Q", 4, "dve"), ("V", 4, "dve"), ("TK", 4, "act"),
                ("A", 4, "dve"), ("TQ", 4, "act"), ("Y", 4, "dve"), ("TY", 4, "act"), ("O", 4, "dve")]
    else:
        plan = [("T", 4, "act"), ("K", 4, "act"), ("Q", 4, "act"), ("V", 4, "dve"),
                ("YT", 4, "dve"), ("TY", 4, "act"), ("O", 4, "dve")]
    st = Stages(plan)
    bank_of = lambda name, k: banks[(st.first[name] + k) % 8]
    pre = f"l{layer}_"
    HG = 4
    NG = H // HG
    UNITS = TT * H

    with ExitStack() as ctx:
        sb = lambda n, s, t=F32: ctx.enter_context(nc.sbuf_tensor(pre + n, s, t))
        sem = lambda n: sems.take(pre + n)
        w = [sb(f"w{i}", [P, DT, D]) for i in range(4)]
        cols = sb("cols", [P, 8 * DT])
        rows = sb("rows", [P, 3, D])
        ident = sb("ident", [P, P])
        block_mask = sb("block_mask", [P, P])
        minus_half = sb("minus_half", [P, TT])
        keep_in = sb("keep_in", [P, B * TT], I32 if layer == 0 else F32)
        keep = sb("keep", [P, B * TT])
        mask_in = [sb(f"mask_in{j}", [P, T], I32 if layer == 0 else F32) for j in range(2)]
        mask_add = sb("mask_add", [P, T])
        x = [sb(f"x{j}", [P, TT, D]) for j in range(2)]
        xn = sb("xn", [P, TT, D])
        xn_t = sb("xn_t", [P, DT, T])
        k_t = sb("k_t", [P, DT, T])
        v_tm = sb("v_tm", [P, TT, D])
        q_t = sb("q_t", [P, DT, T])
        attn = sb("attn", [P, DT, P])
        stats = sb("stats", [P, TT, 6])
        mv = sb("mv", [P, TT, 2])
        rstd = sb("rstd", [P, TT])
        y_stats = sb("y_stats", [P, TT, 6])
        y_mv = sb("y_mv", [P, TT, 2])
        y_rstd = sb("y_rstd", [P, TT])
        k_max = sb("k_max", [P, DT])
        k_sum = sb("k_sum", [P, DT])
        q_max = sb("q_max", [P, TT, H])
        q_sum = sb("q_sum", [P, TT, H])
        if linear:
            k_tm, q_tm, y = (sb(n, [P, TT, D]) for n in ("k_tm", "q_tm", "y"))
            h_t = sb("h_t", [P, DT, T])
        else:
            prob = sb("prob", [P, 2 * HG, T])
            prob_t = sb("prob_t", [P, 2, HG, TT, T])
            y_t = sb("y_t", [P, DT, T])
            y, h_t = xn, xn_t
            s_max = sb("s_max", [P, TT * H])

        w_loaded, const_ready, passed = sem("w_loaded"), sem("const_ready"), sem("passed")
        half_ready = sem("half_ready")
        x_loaded = [sem(f"x_loaded{j}") for j in range(2)]
        mask_loaded = [sem(f"mask_loaded{j}") for j in range(2)]
        x_stored = [sem(f"x_stored{j}") for j in range(2)]
        psum_full = sem("psum_full")
        drained = {"act": sem("act_drained"), "dve": sem("dve_drained")}
        mask_ready, stats_ready, mv_ready = sem("mask_ready"), sem("stats_ready"), sem("mv_ready")
        var_ready, rstd_ready, xn_ready, xb_ready = sem("var_ready"), sem("rstd_ready"), sem("xn_ready"), sem("xb_ready")
        k_max_ready, k_exp_ready, rk_ready = sem("k_max_ready"), sem("k_exp_ready"), sem("rk_ready")
        k_norm_ready = sem("k_norm_ready")
        q_max_ready, q_sub_ready, q_exp_ready = sem("q_max_ready"), sem("q_sub_ready"), sem("q_exp_ready")
        q_sum_ready, v_ready, out_ready = sem("q_sum_ready"), sem("v_ready"), sem("out_ready")
        y_stats_ready, y_mv_ready, y_var_ready = sem("y_stats_ready"), sem("y_mv_ready"), sem("y_var_ready")
        y_rstd_ready, yn_ready = sem("y_rstd_ready"), sem("yn_ready")
        s_full, s_drained, p_ready = sem("s_full"), sem("s_drained"), sem("p_ready")
        pt_full, pt_ready, pv_done, y_drained = sem("pt_full"), sem("pt_ready"), sem("pv_done"), sem("y_drained")

        def wait_bank(pe, b, name, k):
            if linear:
                engine, count = st.before(b, name, k, 8)
                pe.wait_ge(drained[engine], count)
            elif name == "T":
                engine, count = st.drained(b - 1, "O", k)
                pe.wait_ge(drained[engine], count)
            elif name == "K":
                engine, count = st.drained(b - 1, "TY", k)
                pe.wait_ge(drained[engine], count)
            elif name in ("Q", "V", "O"):
                engine, count = st.drained(b, {"Q": "T", "V": "K", "O": "YT"}[name], k)
                pe.wait_ge(drained[engine], count)

        def batches(eng, body):
            with eng.Fori(0, B // 2) as pair:
                for j in range(2):
                    body(pair * 2 + j, pair, j)

        def wait_drained(b, name, k):
            engine, count = st.drained(b, name, k)
            return drained[engine], count

        def transposes(pe, b, name, src):
            for k in range(4):
                wait_bank(pe, b, name, k)
                for i in range(4):
                    last = pe.transpose(bank_of(name, k)[:, i * P:(i + 1) * P], src[:, i, k * P:(k + 1) * P],
                                        ident[:, :])
                last.then_inc(psum_full, 1)

        def project_t(pe, b, name, weight):
            for m in range(DT):
                wait_bank(pe, b, name, m)
                for k in range(DT):
                    last = pe.matmul(bank_of(name, m)[:, :], weight[:, k, m * P:(m + 1) * P], xn_t[:, k, :],
                                     start=(k == 0), stop=(k == DT - 1))
                last.then_inc(psum_full, 1)

        def project(pe, b, name, src_t, weight):
            for t in range(TT):
                wait_bank(pe, b, name, t)
                for k in range(DT):
                    last = pe.matmul(bank_of(name, t)[:, :], src_t[:, k, t * P:(t + 1) * P], weight[:, k, :],
                                     start=(k == 0), stop=(k == DT - 1))
                last.then_inc(psum_full, 1)

        def attention_pe(pe, b):
            pe.wait_ge(*wait_drained(b, "Q", DT - 1))

            def scores(g):
                quad, t = g // TT, g % TT
                for i in range(HG):
                    if g > 0:
                        pe.wait_ge(s_drained, b * UNITS + g * HG + i - HG + 1)
                    head = slice(dh * i, dh * (i + 1))
                    pe.matmul(banks[i][:, :], q_t[head, quad, t * P:(t + 1) * P], k_t[head, quad, :],
                              start=True, stop=True).then_inc(s_full, 1)

            def transpose_p(u):
                pe.wait_ge(p_ready, b * UNITS + u + 1)
                if u >= 2:
                    pe.wait_ge(pt_ready, b * UNITS + u - 1)
                for m in range(TT):
                    last = pe.transpose(banks[4 + u % 2][:, m * P:(m + 1) * P],
                                        prob[:, u % (2 * HG), m * P:(m + 1) * P], ident[:, :])
                last.then_inc(pt_full, 1)

            def values(quad):
                pe.wait_ge(pt_ready, b * UNITS + (quad + 1) * TT * HG)
                if quad >= 2:
                    pe.wait_ge(y_drained, b * DT + quad - 1)
                for m in range(TT):
                    for i in range(HG):
                        h = quad * HG + i
                        last = pe.matmul(banks[6 + quad % 2][dh * i:dh * (i + 1), :], v_tm[:, m, h * dh:(h + 1) * dh],
                                         prob_t[:, quad % 2, i, m, :], start=(m == 0), stop=(m == TT - 1))
                last.then_inc(pv_done, 1)

            scores(0)
            pe.wait_ge(v_ready, (b + 1) * TT)
            for g in range(TT * NG):
                if g + 1 < TT * NG:
                    scores(g + 1)
                for i in range(HG):
                    transpose_p(g * HG + i)
                if g % TT == 0 and g > 0:
                    values(g // TT - 1)
            values(NG - 1)
            pe.wait_ge(s_drained, (b + 1) * UNITS)
            pe.wait_ge(y_drained, (b + 1) * DT)
            transposes(pe, b, "YT", y_t)

        def attention_act(act, b):
            def exps(g):
                for i in range(HG):
                    u = g * HG + i
                    act.wait_ge(s_drained, b * UNITS + u + 1)
                    h = (g // TT) * HG + i
                    act.activation(prob[:, u % (2 * HG), :], prob[:, u % (2 * HG), :], ACT.Exp, scale=-1.0,
                                   bias=s_max[:, u:u + 1],
                                   accum_out=q_sum[:, g % TT, h:h + 1]).then_inc(p_ready, 1)

            for g in range(TT * NG):
                exps(g)

        def attention_dve(dve, b):
            def scores(g):
                for i in range(HG):
                    u = g * HG + i
                    dve.wait_ge(s_full, b * UNITS + u + 1)
                    if u >= 2 * HG:
                        dve.wait_ge(pt_full, b * UNITS + u - 2 * HG + 1)
                    dve.sem_inc(passed, 1)
                    dve.tensor_tensor_reduce(out=prob[:, u % (2 * HG), :], in0=banks[i][:, :],
                                             in1=mask_add[:, :], op0=ALU.add, op1=ALU.min, scale=-1.0,
                                             scalar=3.0e38, accum_out=s_max[:, u:u + 1]).then_inc(s_drained, 1)

            def y_copy(quad):
                dve.wait_ge(pv_done, b * NG + quad + 1)
                dve.tensor_copy(y_t[:, quad, :], banks[6 + quad % 2][:, :]).then_inc(y_drained, 1)

            scores(0)
            for g in range(TT * NG):
                if g + 1 < TT * NG:
                    scores(g + 1)
                for i in range(HG):
                    u = g * HG + i
                    dve.wait_ge(pt_full, b * UNITS + u + 1)
                    if g >= 2 * TT and g % TT == 0 and i == 0:
                        dve.wait_ge(pv_done, b * NG + g // TT - 1)
                    dve.tensor_copy(prob_t[:, (g // TT) % 2, i, :, (g % TT) * P:(g % TT + 1) * P],
                                    banks[4 + u % 2][:, :].rearrange("p (m n) -> p m n", m=TT)).then_inc(pt_ready, 1)
                if g % TT == 1 and g > TT:
                    y_copy(g // TT - 1)
            y_copy(NG - 1)
            dve.wait_ge(p_ready, (b + 1) * UNITS)
            dve.reciprocal(q_sum[:, :, :], q_sum[:, :, :]).then_inc(q_sum_ready, 1)
            dve.wait_ge(q_sum_ready, b + 1)
            for t in range(TT):
                dve.wait_ge(psum_full, st.full(b, "YT", t))
                dve.tensor_tensor(y[:, t, :].rearrange("p (h e) -> p h e", e=dh),
                                  bank_of("YT", t)[:, :].rearrange("p (h e) -> p h e", e=dh),
                                  q_sum[:, t, :].unsqueeze(2).broadcast_to([P, H, dh]), ALU.mult
                                  ).then_inc(drained["dve"], 1)
            dve.wait_ge(*wait_drained(b, "YT", TT - 1))

        with nc.Block() as block:

            @block.sync
            def _(sp):
                for j in range(2):
                    sp.sem_inc(x_stored[j], 16)
                for i in range(4):
                    sp.dma_start(w[i][:, :, :], d["att_w"][layer, i].rearrange("(k p) n -> p k n", p=P)
                                 ).then_inc(w_loaded, 16)
                sp.dma_start(cols[:, :], d["att_cols"][:, layer, :]).then_inc(w_loaded, 16)
                sp.dma_start(rows[:, :, :].rearrange("p r n -> p (r n)"),
                             d["att_rows"][layer:layer + 1, :].broadcast_to([P, 3 * D])).then_inc(w_loaded, 16)
                sp.dma_start(ident[:, :], d["ident"]).then_inc(w_loaded, 16)
                sp.dma_start(block_mask[:, :], d["block_masks"][:, 1 if dh == 64 else 0, :]).then_inc(w_loaded, 16)
                sp.dma_start(keep_in[:, :], d[f"mask{layer}_t"]).then_inc(w_loaded, 16)

                def load(b, j):
                    sp.dma_start(x[j][:, :, :], x_in[b].rearrange("(t p) n -> p t n", p=P)).then_inc(x_loaded[j], 16)
                    sp.dma_start(mask_in[j][:, :], d[f"mask{layer}"][b].broadcast_to([P, T])).then_inc(mask_loaded[j], 16)

                load(0, 0)

                with sp.Fori(0, B // 2 - 1) as pair:
                    for j in range(2):
                        b = pair * 2 + j
                        if j == 0:
                            sp.wait_ge(x_stored[1], pair * 16 + 16)
                            sp.sem_inc(passed, 1)
                            sp.wait_ge(mask_ready, b + 1)
                            sp.sem_inc(passed, 1)
                            load(b + 1, 1)
                        sp.wait_ge(out_ready, (b + 1) * TT)
                        sp.sem_inc(passed, 1)
                        sp.dma_start(x_out[b].rearrange("(t p) n -> p t n", p=P), x[j][:, :, :]
                                     ).then_inc(x_stored[j], 16)
                        if j == 0:
                            sp.wait_ge(x_stored[0], pair * 16 + 32)
                            sp.sem_inc(passed, 1)
                            sp.wait_ge(mask_ready, b + 2)
                            sp.sem_inc(passed, 1)
                            load(b + 2, 0)
                b = B - 2
                sp.wait_ge(x_stored[1], B // 2 * 16)
                sp.wait_ge(mask_ready, b + 1)
                sp.sem_inc(passed, 1)
                load(b + 1, 1)
                for j in range(2):
                    sp.wait_ge(out_ready, (b + j + 1) * TT)
                    sp.sem_inc(passed, 1)
                    sp.dma_start(x_out[b + j].rearrange("(t p) n -> p t n", p=P), x[j][:, :, :]
                                 ).then_inc(x_stored[j], 16)
                for j in range(2):
                    sp.wait_ge(x_stored[j], B // 2 * 16 + 16)

            @block.gpsimd
            def _(pool):
                pool.memset(minus_half[:, :], -0.5).then_inc(half_ready, 1)
                pool.wait_ge(half_ready, 1)
                pool.wait_ge(w_loaded, 9 * 16)

                def body(b, pair, j):
                    pool.wait_ge(mv_ready, (b + 1) * TT)
                    pool.sem_inc(passed, 1)
                    pool.tensor_scalar(rstd[:, :], mv[:, :, 1], EPS, 0.0, ALU.add, ALU.add).then_inc(var_ready, 1)
                    pool.wait_ge(var_ready, b + 1)
                    pool.tensor_tensor(rstd[:, :], rstd[:, :], minus_half[:, :], ALU.pow).then_inc(rstd_ready, 1)
                    pool.wait_ge(xn_ready, (b + 1) * TT)
                    pool.tensor_tensor(x[j][:, :, :], x[j][:, :, :],
                                       rows[:, 2, :].unsqueeze(1).broadcast_to([P, TT, D]), ALU.add
                                       ).then_inc(xb_ready, 1)
                    pool.wait_ge(y_mv_ready, (b + 1) * TT)
                    pool.sem_inc(passed, 1)
                    pool.tensor_scalar(y_rstd[:, :], y_mv[:, :, 1], EPS, 0.0, ALU.add, ALU.add).then_inc(y_var_ready, 1)
                    pool.wait_ge(y_var_ready, b + 1)
                    pool.tensor_tensor(y_rstd[:, :], y_rstd[:, :], minus_half[:, :], ALU.pow).then_inc(y_rstd_ready, 1)

                batches(pool, body)

            @block.scalar
            def _(act):
                act.sem_inc(drained["act"], st.per["act"])
                act.wait_ge(w_loaded, 9 * 16)
                col = lambda v, k: cols[:, v * DT + k:v * DT + k + 1]

                def drain(b, name, k, out, func, **kw):
                    act.wait_ge(psum_full, st.full(b, name, k))
                    act.activation(out, bank_of(name, k)[:, :], func, **kw).then_inc(drained["act"], 1)

                def body(b, pair, j):
                    for k in range(DT):
                        drain(b, "T", k, xn_t[:, k, :], ACT.Identity, scale=col(NW, k), bias=col(NB, k))
                    if linear:
                        act.wait_ge(k_max_ready, 2 * (b + 1))
                        for k in range(DT):
                            act.activation(k_t[:, k, :], k_t[:, k, :], ACT.Exp, bias=k_max[:, k:k + 1],
                                           accum_out=k_sum[:, k:k + 1]).then_inc(k_exp_ready, 1)
                        for t in range(TT):
                            act.wait_ge(q_sub_ready, b * TT + t + 1)
                            act.activation(q_tm[:, t, :], q_tm[:, t, :], ACT.Exp).then_inc(q_exp_ready, 1)
                        for t in range(TT):
                            drain(b, "TK", t, k_tm[:, t, :], ACT.Copy)
                        for k in range(DT):
                            drain(b, "TQ", k, q_t[:, k, :], ACT.Copy)
                    else:
                        for k in range(DT):
                            drain(b, "K", k, k_t[:, k, :], ACT.Identity, bias=col(BK, k))
                        for k in range(DT):
                            drain(b, "Q", k, q_t[:, k, :], ACT.Identity, bias=col(BQ, k))
                        attention_act(act, b)
                    for k in range(DT):
                        drain(b, "TY", k, h_t[:, k, :], ACT.Silu,
                              scale=mod_all["gain"][:, layer, k, bass.ds(b, 1)],
                              bias=mod_all["shift"][:, layer, k, bass.ds(b, 1)])

                batches(act, body)

            @block.tensor
            def _(pe):
                pe.sem_inc(psum_full, st.n)
                pe.wait_ge(w_loaded, 9 * 16)
                wq, wk, wv, wo = w

                def body(b, pair, j):
                    pe.wait_ge(xn_ready, (b + 1) * TT)
                    transposes(pe, b, "T", xn)
                    pe.wait_ge(*wait_drained(b, "T", DT - 1))
                    project_t(pe, b, "K", wk)
                    if linear:
                        project(pe, b, "Q", xn_t, wq)
                        project(pe, b, "V", xn_t, wv)
                        pe.wait_ge(k_norm_ready if layer == 0 else k_exp_ready, (b + 1) * DT)
                        transposes(pe, b, "TK", k_t)
                        pe.wait_ge(v_ready, (b + 1) * TT)
                        pe.wait_ge(*wait_drained(b, "TK", TT - 1))
                        for g in range(DT):
                            wait_bank(pe, b, "A", g)
                            for t in range(TT):
                                k_part, v_part = (i[:, t, g * P:(g + 1) * P] for i in (k_tm, v_tm))
                                lhs_t, rhs = (v_part, k_part) if layer == 0 else (k_part, v_part)
                                last = pe.matmul(bank_of("A", g)[:, 0:P], lhs_t, rhs, start=(t == 0),
                                                 stop=(t == TT - 1))
                            last.then_inc(psum_full, 1)
                        pe.wait_ge(q_exp_ready, (b + 1) * TT)
                        transposes(pe, b, "TQ", q_tm)
                        pe.wait_ge(*wait_drained(b, "A", DT - 1))
                        pe.wait_ge(*wait_drained(b, "TQ", DT - 1))
                        for t in range(TT):
                            wait_bank(pe, b, "Y", t)
                            for g in range(DT):
                                last = pe.matmul(bank_of("Y", t)[:, g * P:(g + 1) * P], q_t[:, g, t * P:(t + 1) * P],
                                                 attn[:, g, :], start=True, stop=True)
                            last.then_inc(psum_full, 1)
                    else:
                        project_t(pe, b, "Q", wq)
                        project(pe, b, "V", xn_t, wv)
                        attention_pe(pe, b)
                    pe.wait_ge(yn_ready, (b + 1) * TT)
                    transposes(pe, b, "TY", y)
                    pe.wait_ge(*wait_drained(b, "TY", DT - 1))
                    project(pe, b, "O", h_t, wo)

                batches(pe, body)

            @block.vector
            def _(dve):
                dve.sem_inc(drained["dve"], st.per["dve"])
                dve.sem_inc(mask_ready, 1)
                dve.wait_ge(w_loaded, 9 * 16)
                if layer == 0:
                    dve.tensor_scalar(keep[:, :], keep_in[:, :], 1.0, None, ALU.not_equal).then_inc(const_ready, 1)
                else:
                    dve.tensor_copy(keep[:, :], keep_in[:, :]).then_inc(const_ready, 1)
                dve.wait_ge(const_ready, 1)
                col = lambda v, k: cols[:, v * DT + k:v * DT + k + 1]

                def norm_stats(b, src, out, agg, stats_sem, agg_sem):
                    for t in range(TT):
                        dve.bn_stats(out[:, t, :], src[:, t, :]).then_inc(stats_sem, 1)
                    for t in range(TT):
                        dve.wait_ge(stats_sem, b * TT + t + 1)
                        dve.sem_inc(passed, 1)
                        dve.bn_aggr(agg[:, t, :], out[:, t, :]).then_inc(agg_sem, 1)

                def body(b, pair, j):
                    dve.wait_ge(mask_loaded[j], pair * 16 + 16)
                    if layer == 0:
                        dve.tensor_scalar(mask_add[:, :], mask_in[j][:, :], 1.0, NEG, ALU.is_equal, ALU.mult
                                          ).then_inc(mask_ready, 1)
                    else:
                        dve.tensor_scalar(mask_add[:, :], mask_in[j][:, :], 1.0, 1.0e6, ALU.subtract, ALU.mult
                                          ).then_inc(mask_ready, 1)
                    dve.wait_ge(x_loaded[j], pair * 16 + 16)
                    norm_stats(b, x[j], stats, mv, stats_ready, mv_ready)
                    dve.wait_ge(rstd_ready, b + 1)
                    for t in range(TT):
                        dve.tensor_scalar(xn[:, t, :], x[j][:, t, :], mv[:, t, 0:1], rstd[:, t:t + 1],
                                          ALU.subtract, ALU.mult).then_inc(xn_ready, 1)
                    dve.wait_ge(mask_ready, b + 2)
                    if linear:
                        for k in range(DT):
                            dve.wait_ge(psum_full, st.full(b, "K", k))
                            dve.scalar_tensor_tensor(k_t[:, k, :], bank_of("K", k)[:, :], col(BK, k), mask_add[:, :],
                                                     ALU.add, ALU.add).then_inc(drained["dve"], 1)
                            dve.wait_ge(*wait_drained(b, "K", k))
                            last = dve.reduce_max(k_max[:, k:k + 1], k_t[:, k, :], AX.X)
                        last.then_inc(k_max_ready, 1)
                        dve.wait_ge(k_max_ready, 2 * b + 1)
                        dve.tensor_scalar(k_max[:, :], k_max[:, :], -1.0, None, ALU.mult).then_inc(k_max_ready, 1)
                        for t in range(TT):
                            dve.wait_ge(psum_full, st.full(b, "Q", t))
                            dve.tensor_tensor(q_tm[:, t, :], bank_of("Q", t)[:, :], rows[:, 0, :], ALU.add
                                              ).then_inc(drained["dve"], 1)
                            dve.wait_ge(*wait_drained(b, "Q", t))
                            heads = q_tm[:, t, :].rearrange("p (h e) -> p h e", e=dh)
                            dve.tensor_reduce(q_max[:, t, :], heads, AX.X, ALU.max).then_inc(q_max_ready, 1)
                            dve.wait_ge(q_max_ready, b * TT + t + 1)
                            dve.tensor_tensor(heads, heads, q_max[:, t, :].unsqueeze(2).broadcast_to([P, H, dh]),
                                              ALU.subtract).then_inc(q_sub_ready, 1)
                    if linear:
                        dve.wait_ge(k_exp_ready, (b + 1) * DT)
                        dve.reciprocal(k_sum[:, :], k_sum[:, :]).then_inc(rk_ready, 1)
                        dve.wait_ge(rk_ready, b + 1)
                        if layer == 0:
                            for k in range(DT):
                                dve.tensor_scalar(k_t[:, k, :], k_t[:, k, :], k_sum[:, k:k + 1], None, ALU.mult
                                                  ).then_inc(k_norm_ready, 1)
                    for t in range(TT):
                        dve.wait_ge(psum_full, st.full(b, "V", t))
                        dve.tensor_tensor(v_tm[:, t, :], bank_of("V", t)[:, :], rows[:, 1, :], ALU.add
                                          ).then_inc(drained["dve"], 1)
                        dve.wait_ge(*wait_drained(b, "V", t))
                        dve.tensor_scalar(v_tm[:, t, :], v_tm[:, t, :], keep[:, bass.ds(b * TT + t, 1)], None, ALU.mult
                                          ).then_inc(v_ready, 1)
                    if linear:
                        for t in range(TT):
                            dve.wait_ge(q_exp_ready, b * TT + t + 1)
                            last = dve.reduce_sum(q_sum[:, t, :], q_tm[:, t, :].rearrange("p (h e) -> p h e", e=dh), AX.X)
                        last.then_inc(q_sum_ready, 1)
                        dve.wait_ge(q_sum_ready, 2 * b + 1)
                        dve.reciprocal(q_sum[:, :, :], q_sum[:, :, :]).then_inc(q_sum_ready, 1)
                        for g in range(DT):
                            dve.wait_ge(psum_full, st.full(b, "A", g))
                            if layer == 0:
                                ins = dve.tensor_tensor(attn[:, g, :], bank_of("A", g)[:, 0:P], block_mask[:, :],
                                                        ALU.mult)
                            else:
                                ins = dve.scalar_tensor_tensor(attn[:, g, :], bank_of("A", g)[:, 0:P],
                                                               k_sum[:, g:g + 1], block_mask[:, :], ALU.mult, ALU.mult)
                            ins.then_inc(drained["dve"], 1)
                        dve.wait_ge(q_sum_ready, 2 * b + 2)
                        for t in range(TT):
                            dve.wait_ge(psum_full, st.full(b, "Y", t))
                            dve.tensor_tensor(y[:, t, :].rearrange("p (h e) -> p h e", e=dh),
                                              bank_of("Y", t)[:, :].rearrange("p (h e) -> p h e", e=dh),
                                              q_sum[:, t, :].unsqueeze(2).broadcast_to([P, H, dh]), ALU.mult
                                              ).then_inc(drained["dve"], 1)
                        dve.wait_ge(*wait_drained(b, "Y", TT - 1))
                    else:
                        attention_dve(dve, b)
                    norm_stats(b, y, y_stats, y_mv, y_stats_ready, y_mv_ready)
                    dve.wait_ge(y_rstd_ready, b + 1)
                    for t in range(TT):
                        dve.tensor_scalar(y[:, t, :], y[:, t, :], y_mv[:, t, 0:1], y_rstd[:, t:t + 1],
                                          ALU.subtract, ALU.mult).then_inc(yn_ready, 1)
                    dve.wait_ge(xb_ready, b + 1)
                    for t in range(TT):
                        dve.wait_ge(psum_full, st.full(b, "O", t))
                        ins = dve.tensor_tensor(x[j][:, t, :], bank_of("O", t)[:, :], x[j][:, t, :], ALU.add)
                        ins.then_inc(drained["dve"], 1)
                    dve.wait_ge(*wait_drained(b, "O", TT - 1))
                    dve.sem_inc(out_ready, TT)

                batches(dve, body)



def ssm_layer(nc, sems, d, mod_all, banks, x_in, x_out):
    PARTS = 4
    plan = []
    for p in range(PARTS):
        plan += [(f"Z1{p}", 2, "act"), (f"O{p}", 1, "dve")]
    plan += [("Y00", 4, "dve"), ("MX", ET, "act"), ("DBC1", 1, "dve"), ("Y01", 4, "dve"), ("TC1", 1, "dve"),
             ("T", DT, "act"), ("DL1", ET, "dve"), ("Y10", 4, "dve"), ("Z0", ET, "act"),
             ("DBC0", 1, "dve"), ("Y11", 4, "dve"), ("TC0", 1, "dve"), ("DL0", ET, "dve")]
    st = Stages(plan)
    RING = 2

    def bank_of(name, k):
        return banks[6 if name[:2] == "Z1" else 7 if name[0] == "O" else 6 + (st.first[name] + k) % RING]

    GE = 4
    UNITS = 4
    STEPS = UNITS * N
    CH = 2
    SPARE = 3
    SCANNED = 2 + GE
    BUILT = {"Z1": 0, "MX": 1, "Z0": 2}
    with ExitStack() as ctx:
        sb = lambda n, s, t=F32: ctx.enter_context(nc.sbuf_tensor("ssm_" + n, s, t))
        sem = lambda n: sems.take("ssm_" + n)
        ident = sb("ident", [P, P])
        w_ring = [sb(f"w_ring{i}", [P, DT, P]) for i in range(2)]
        w_out = sb("w_out", [P, ET, D])
        w_dbc = sb("w_dbc", [P, 2, ET, R + 2 * N])
        w_dt = sb("w_dt", [R, 2, E])
        neg_a = sb("neg_a", [P, 2, ET, N])
        bf_row = sb("bf_row", [P, D])
        ada = sb("ada", [P, 3, D])
        gate = sb("gate", [P, D])
        minus_half = sb("minus_half", [P, TT])
        work = sb("work", [P, 4, 4, 512])
        d_bu = [work[:, i] for i in range(2)]
        state = [work[:, 2 + i] for i in range(2)]
        skip, xs, xn = work[:, 0], work[:, 1], work[:, 2]
        x = sb("x", [P, TT, D])
        xn_t = sb("xn_t", [P, DT, T])
        z = [sb(f"z{s}", [P, ET, T]) for s in range(2)]
        delta = sb("delta", [P, ET, T])
        soft = sb("soft", [P, 2, T])
        mx = sb("mx", [P, ET, T])
        y_sum = sb("y_sum", [P, ET, T])
        acc = sb("acc", [P, TT, GE * P])
        b_rows = sb("b_rows", [P, 2, CH, T])
        dbc_t = sb("dbc_t", [R + 2 * N, T])
        dbc_tm = sb("dbc_tm", [P, TT, R + 2 * N])
        stats = sb("stats", [P, TT, 6])
        mv = sb("mv", [P, TT, 2])
        rstd = sb("rstd", [P, TT])
        stats2 = sb("stats2", [P, TT, 6])
        mv2 = sb("mv2", [P, TT, 2])
        rstd2 = sb("rstd2", [P, TT])
        cols = mod_all["ssm_cols"]
        bzc = mod_all["bzc"]

        w_loaded, const_ready, passed = sem("w_loaded"), sem("const_ready"), sem("passed")
        half_ready, w_out_loaded = sem("half_ready"), sem("w_out_loaded")
        x_loaded, x_stored, ada_loaded, gate_loaded = sem("x_loaded"), sem("x_stored"), sem("ada_loaded"), sem("gate_loaded")
        resid_stored, resid_loaded = sem("resid_stored"), sem("resid_loaded")
        ring_loaded = [sem(f"ring_loaded{i}") for i in range(2)]
        full = sem("full")
        drained = {"act": sem("act_drained"), "dve": sem("dve_drained")}
        stats_ready, mv_ready, var_ready, rstd_ready = sem("stats_ready"), sem("mv_ready"), sem("var_ready"), sem("rstd_ready")
        stats2_ready, mv2_ready, var2_ready, rstd2_ready = sem("stats2_ready"), sem("mv2_ready"), sem("var2_ready"), sem("rstd2_ready")
        xn_ready, xs_ready, xn2_ready, resid_ready = sem("xn_ready"), sem("xs_ready"), sem("xn2_ready"), sem("resid_ready")
        soft_in, soft_out, delta_ready, du_ready = sem("soft_in"), sem("soft_out"), sem("delta_ready"), sem("du_ready")
        u_used = [sem(f"u_used{s}") for s in range(2)]
        b_stored = sem("b_stored")
        b_loaded = [sem(f"b_loaded{i}") for i in range(2)]
        da_ready, dbu_ready, scanned, turned, added = sem("da_ready"), sem("dbu_ready"), sem("scanned"), sem("turned"), sem("added")
        silu_ready, gated, out_ready = sem("silu_ready"), sem("gated"), sem("out_ready")

        def wait_drained(b, name, k):
            engine, count = st.drained(b, name, k)
            return drained[engine], count

        def ring_count(b, name, i):
            return (b * 12 + (BUILT[name] * 4 + 4) + i + 1) * 16

        def batches(eng, before, body, after):
            before()
            body(0, True, False)
            with eng.Fori(1, B - 1) as b:
                body(b, False, False)
            body(B - 1, False, True)
            after()

        def absent(eng, name, by, b, first, n):
            at = [i[0] for i in plan].index(first)
            count = lambda stages: sum(k for _, k, engine in stages if by in ("pe", engine))
            if not count(plan[at:at + n]):
                return
            before = (b + 1) * count(plan) + count(plan[:at])
            if before > 0:
                eng.wait_ge(name, before)
            eng.sem_inc(name, count(plan[at:at + n]))

        def around_front(eng, name, by, norms, columns, deltas):
            absent(eng, name, by, -1, "Z10", 13)
            norms()
            absent(eng, name, by, -1, "DL1", 2)
            columns()
            deltas(-1, lambda: absent(eng, name, by, -1, "Y11", 1))

        with nc.Block() as block:

            @block.sync
            def _(sp):
                sp.dma_start(ident[:, :], d["ident"]).then_inc(w_loaded, 16)
                sp.dma_start(w_dbc[:, :, :, :], d["wdbcT"].rearrange("s (k p) n -> p s k n", p=P)).then_inc(w_loaded, 16)
                sp.dma_start(w_dt[:, :, :], d["wdtT"].rearrange("s r n -> r s n")).then_inc(w_loaded, 16)
                sp.dma_start(neg_a[:, :, :, :].rearrange("p s k n -> p (s k n)"), d["alog"]).then_inc(w_loaded, 16)
                sp.dma_start(bf_row[:, :], d["bf_row"].broadcast_to([P, D])).then_inc(w_loaded, 16)

                def load_x(b):
                    sp.dma_start(x[:, :, :], x_in[b].rearrange("(t p) n -> p t n", p=P)).then_inc(x_loaded, 16)
                    sp.dma_start(ada[:, :, :].rearrange("p r n -> p (r n)"),
                                 d["ada_d"][bass.ds(b, 1), :].broadcast_to([P, 3 * D])).then_inc(ada_loaded, 16)

                def store_resid(b):
                    sp.wait_ge(resid_ready, (b + 1) * 3)
                    sp.sem_inc(passed, 1)
                    sp.dma_start(d["resid_d"][b].rearrange("(t p) n -> p t n", p=P), x[:, :, :]
                                 ).then_inc(resid_stored, 16)

                def store_b(b, s, count):
                    sp.wait_ge(*wait_drained(b, f"DBC{s}", 0))
                    sp.sem_inc(passed, 1)
                    sp.dma_start(d["b_d"][s], dbc_t[R:R + N, :]).then_inc(b_stored, 16)
                    sp.wait_ge(b_stored, count)
                    sp.sem_inc(passed, 1)

                def unit(b, s, g, between=None):
                    def part(i):
                        for j in range(2):
                            c = i * 2 + j
                            sp.wait_ge(dbu_ready, b * STEPS + (s * 2 + g) * N + (c - 1) * CH + SPARE)
                            sp.sem_inc(passed, 1)
                            columns = slice(c * CH * T, (c + 1) * CH * T) if isinstance(c, int) else bass.ds(c * CH * T, CH * T)
                            sp.dma_start(b_rows[:, j, :, :].rearrange("p c n -> p (c n)"),
                                         d["b_flat"][s:s + 1, columns].broadcast_to([P, CH * T])
                                         ).then_inc(b_loaded[j], 16)

                    if between:
                        part(0)
                        between()
                    with sp.Fori(1 if between else 0, PARTS) as i:
                        part(i)

                def store_out(b):
                    sp.wait_ge(out_ready, (b + 1) * TT)
                    sp.sem_inc(passed, 1)
                    sp.dma_start(x_out[b].rearrange("(t p) n -> p t n", p=P), x[:, :, :]).then_inc(x_stored, 16)
                    sp.wait_ge(x_stored, (b + 1) * 16)
                    sp.sem_inc(passed, 1)

                def before():
                    load_x(0)
                    sp.dma_start(w_out[:, :, :], d["wfT"].rearrange("(k p) n -> p k n", p=P)).then_inc(w_out_loaded, 16)
                    store_resid(0)
                    store_b(-1, 0, 16)

                def body(b, first, last):
                    def turn_over():
                        if not first:
                            store_out(b - 1)
                        if not last:
                            sp.wait_ge(resid_stored, (b + 1) * 16)
                            sp.sem_inc(passed, 1)
                            load_x(b + 1)
                        sp.dma_start(gate[:, :], d["ada_d"][bass.ds(b, 1), 2 * D:3 * D].broadcast_to([P, D])
                                     ).then_inc(gate_loaded, 16)

                    unit(b, 0, 0)
                    unit(b, 0, 1, turn_over)
                    store_b(b, 1, b * 32 + 32)
                    if not last:
                        store_resid(b + 1)
                    unit(b, 1, 0)
                    sp.wait_ge(resid_stored, (b + 1 if last else b + 2) * 16)
                    sp.sem_inc(passed, 1)
                    sp.dma_start(x[:, :, :], d["resid_d"][b].rearrange("(t p) n -> p t n", p=P)).then_inc(resid_loaded, 16)
                    unit(b, 1, 1)
                    if not last:
                        store_b(b, 0, b * 32 + 48)

                batches(sp, before, body, lambda: store_out(B - 1))

            @block.gpsimd
            def _(pool):
                pool.sem_inc(dbu_ready, SPARE)
                pool.memset(minus_half[:, :], -0.5).then_inc(half_ready, 1)
                pool.wait_ge(half_ready, 1)
                pool.wait_ge(w_loaded, 5 * 16)

                def rsqrt(b, agg, out, agg_sem, var_sem, out_sem):
                    pool.wait_ge(agg_sem, (b + 1) * TT)
                    pool.sem_inc(passed, 1)
                    pool.tensor_scalar(out[:, :], agg[:, :, 1], EPS, 0.0, ALU.add, ALU.add).then_inc(var_sem, 1)
                    pool.wait_ge(var_sem, b + 1)
                    pool.tensor_tensor(out[:, :], out[:, :], minus_half[:, :], ALU.pow).then_inc(out_sem, 1)

                def norms(b):
                    rsqrt(b, mv, rstd, mv_ready, var_ready, rstd_ready)
                    rsqrt(b, mv2, rstd2, mv2_ready, var2_ready, rstd2_ready)
                    rows = lambda row: row.unsqueeze(1).broadcast_to([P, TT, D])
                    pool.tensor_tensor(skip, xs, rows(bf_row[:, :]), ALU.add).then_inc(resid_ready, 1)
                    pool.wait_ge(resid_ready, b * 3 + 1)
                    pool.tensor_tensor(skip, skip, rows(ada[:, 2, :]), ALU.mult).then_inc(resid_ready, 1)
                    pool.wait_ge(resid_ready, b * 3 + 2)
                    pool.wait_ge(xn_ready, (b + 1) * TT)
                    pool.tensor_tensor(x[:, :, :], skip, x[:, :, :], ALU.add).then_inc(resid_ready, 1)

                def direction(b, s):
                    for g in range(2):
                        for m in range(g * GE, (g + 1) * GE):
                            pool.wait_ge(delta_ready, (b * 2 + s) * ET + m + 1)
                            pool.wait_ge(u_used[s], b * ET + m + 1)
                            pool.tensor_tensor(z[s][:, m, :], z[s][:, m, :], delta[:, m, :], ALU.mult).then_inc(du_ready, 1)
                        pool.wait_ge(du_ready, (b * 2 + s) * ET + (g + 1) * GE)
                        pool.sem_inc(passed, 1)
                        with pool.Fori(0, PARTS) as i:
                            for j in range(2):
                                chunk = b * (STEPS // CH // 2) + (s * 2 + g) * PARTS + i
                                pool.wait_ge(b_loaded[j], (chunk + 1) * 16)
                                for k in range(CH):
                                    step = b * STEPS + (s * 2 + g) * N + i * 4 + (2 * j + k)
                                    pool.wait_ge(scanned, SCANNED + (step - 1) * GE)
                                    pool.tensor_tensor(d_bu[k], z[s][:, g * GE:(g + 1) * GE, :],
                                                       b_rows[:, j, k, :].unsqueeze(1).broadcast_to([P, GE, T]),
                                                       ALU.mult).then_inc(dbu_ready, 1)

                def body(b, first, last):
                    pool.wait_ge(resid_ready, (b + 1) * 3)
                    pool.wait_ge(full, st.full(b - 1, "T", DT - 1))
                    direction(b, 0)
                    if not last:
                        pool.wait_ge(x_loaded, (b + 2) * 16)
                        norms(b + 1)
                        pool.wait_ge(resid_ready, (b + 2) * 3)
                        pool.wait_ge(full, st.full(b, "T", DT - 1))
                    direction(b, 1)

                def before():
                    norms(0)

                batches(pool, before, body, lambda: None)

            @block.scalar
            def _(act):
                act.wait_ge(w_loaded, 5 * 16)
                flat = neg_a[:, :, :, :].rearrange("p s k n -> p (s k n)")
                act.activation(flat, flat, ACT.Exp).then_inc(const_ready, 1)
                act.wait_ge(const_ready, 1)
                act.activation(flat, flat, ACT.Copy, scale=-1.0).then_inc(const_ready, 1)
                act.wait_ge(const_ready, 2)

                def drain(b, name, k, out, func, bank=None, **kw):
                    act.wait_ge(full, st.full(b, name, k))
                    act.activation(out, bank_of(name, k if bank is None else bank)[:, :], func, **kw
                                   ).then_inc(drained["act"], 1)

                def load_ring(name, m, j):
                    src = {"Z0": d["wzc"][0], "Z1": d["wzc"][1], "MX": d["wxT"]}[name]
                    part = slice(m * P, (m + 1) * P) if isinstance(m, int) else bass.ds(m * P, P)
                    act.dma_start(w_ring[j][:, :, :], src[:, part].rearrange("(k p) n -> p k n", p=P)
                                  ).then_inc(ring_loaded[j], 16)

                def drain_tile(b, name, m, j, following):
                    one = (lambda t, at: t[:, at:at + 1]) if isinstance(m, int) else (lambda t, at: t[:, bass.ds(at, 1)])
                    tile = (lambda t: t[:, m, :]) if isinstance(m, int) else (
                        lambda t: t[:, bass.ds(m, 1), :].rearrange("p o n -> p (o n)"))
                    out = tile({"Z0": z[0], "Z1": z[1], "MX": mx}[name])
                    bias = one(cols, m + BX) if name == "MX" else one(bzc, m + (0 if name == "Z0" else ET))
                    if name == "Z1":
                        drain(b, f"Z1{m // 2}", j, out, ACT.Identity, bias=bias)
                    else:
                        drain(b, name, m, out, ACT.Identity, bank=j, bias=bias)
                    if not isinstance(m, int) or m + 2 < ET:
                        load_ring(name, m + 2, j)
                    elif following:
                        load_ring(following, j, j)

                def norms(b):
                    for k in range(DT):
                        drain(b, "T", k, xn_t[:, k, :], ACT.Identity, scale=cols[:, G2 + k:G2 + k + 1],
                              bias=cols[:, B2 + k:B2 + k + 1])

                def softplus(index, direct=False):
                    for m in range(ET):
                        i = index * ET + m
                        act.wait_ge(soft_in, i + 1)
                        act.activation(soft[:, m % 2, :], soft[:, m % 2, :], ACT.Exp).then_inc(soft_out, 1)
                        act.wait_ge(soft_out, 2 * i + 1)
                        act.activation(soft[:, m % 2, :], soft[:, m % 2, :], ACT.Ln, bias=1.0).then_inc(soft_out, 1)
                        if direct:
                            act.activation(y_sum[:, m, :], z[0][:, m, :], ACT.Copy,
                                           scale=cols[:, DPC + m:DPC + m + 1]).then_inc(u_used[0], 1)

                def unit(b, s, g, name, following=None):
                    def part(i):
                        for j in range(2):
                            for r in range(2):
                                n = i * 4 + (2 * j + r)
                                rate = slice(n, n + 1) if isinstance(n, int) else bass.ds(n, 1)
                                for e in range(GE):
                                    at = (b * STEPS + (s * 2 + g) * N + n) * GE + e
                                    act.wait_ge(scanned, SCANNED - 2 + at + 1)
                                    act.activation(banks[e % 2][:, :], delta[:, g * GE + e, :], ACT.Exp,
                                                   scale=neg_a[:, s, g * GE + e, rate]).then_inc(da_ready, 1)
                            if name:
                                drain_tile(b, name, i * 2 + j, j, following)

                    act.wait_ge(delta_ready, (b * 2 + s + 1) * ET)
                    if name == "Z1":
                        for p in range(PARTS):
                            part(p)
                    elif name:
                        with act.Fori(0, PARTS - 1) as i:
                            part(i)
                        part(PARTS - 1)
                    else:
                        with act.Fori(0, PARTS) as i:
                            part(i)

                def deltas(b, sums):
                    sums()
                    if not isinstance(b, int) or b >= 0:
                        act.wait_ge(gated, (b + 1) * ET)
                    act.wait_ge(*wait_drained(b, "Z0", ET - 1))
                    softplus((b + 1) * 2, direct=True)

                def before():
                    for j in range(2):
                        load_ring("Z0", j, j)
                    around_front(act, drained["act"], "act", lambda: norms(-1),
                                 lambda: [drain_tile(-1, "Z0", m, m % 2, "Z1") for m in range(ET)], deltas)

                def body(b, first, last):
                    act.wait_ge(dbu_ready, SPARE + b * STEPS)
                    unit(b, 0, 0, "Z1", "MX")
                    act.wait_ge(full, st.full(b, "Y00", 0))
                    unit(b, 0, 1, "MX", None if last else "Z0")
                    act.wait_ge(*wait_drained(b, "MX", ET - 1))
                    for m in range(ET):
                        act.activation(mx[:, m, :], mx[:, m, :], ACT.Silu).then_inc(silu_ready, 1)
                    act.preload_act_table_set("natural_log_exp_and_others")
                    if last:
                        absent(act, drained["act"], "act", b, "T", 1)
                    else:
                        norms(b)
                    softplus(b * 2 + 1)
                    unit(b, 1, 0, None)
                    if last:
                        absent(act, drained["act"], "act", b, "Z0", 1)
                        unit(b, 1, 1, None)
                    else:
                        unit(b, 1, 1, "Z0", "Z1")
                        deltas(b, lambda: None)

                act.preload_act_table_set("natural_log_exp_and_others")
                batches(act, before, body, lambda: None)

            @block.tensor
            def _(pe):
                pe.sem_inc(turned, 1)
                pe.wait_ge(w_loaded, 5 * 16)

                def wait_bank(b, name, k):
                    engine, count = st.before(b, name, k, RING)
                    pe.wait_ge(drained[engine], count)

                def products(b, name, k, pairs, rows_out=P):
                    wait_bank(b, name, k)
                    for i, (lhs_t, rhs) in enumerate(pairs):
                        last = pe.matmul(bank_of(name, k)[0:rows_out, :], lhs_t, rhs, start=(i == 0),
                                         stop=(i == len(pairs) - 1))
                    last.then_inc(full, 1)

                def norms(b):
                    pe.wait_ge(xn2_ready, (b + 2) * TT)
                    for k in range(DT):
                        wait_bank(b, "T", k)
                        for t in range(TT):
                            last = pe.transpose(bank_of("T", k)[:, t * P:(t + 1) * P], xn[:, t, k * P:(k + 1) * P], ident[:, :])
                        last.then_inc(full, 1)

                def dbc(b, s):
                    products(b, f"DBC{s}", 0, [(w_dbc[:, s, k, :], z[s][:, k, :]) for k in range(ET)], R + 2 * N)

                def dbc_turned(b, s):
                    pe.wait_ge(*wait_drained(b, f"DBC{s}", 0))
                    wait_bank(b, f"TC{s}", 0)
                    for t in range(TT):
                        last = pe.transpose(bank_of(f"TC{s}", 0)[:, t * 96:(t + 1) * 96],
                                            dbc_t[:, t * P:(t + 1) * P], ident[0:96, 0:96])
                    last.then_inc(full, 1)

                def dl(b, s):
                    for m in range(ET):
                        products(b, f"DL{s}", m, [(w_dt[:, s, m * P:(m + 1) * P], dbc_t[0:R, :])])

                def tile(b, name, i, j):
                    pe.wait_ge(ring_loaded[j], ring_count(b, name, i))
                    for k in range(DT):
                        last = pe.matmul(bank_of(f"Z1{i}" if name == "Z1" else name, j)[:, :], w_ring[j][:, k, :],
                                         xn_t[:, k, :], start=(k == 0), stop=(k == DT - 1))
                    last.then_inc(full, 1)

                def output(b, t, quarters=range(4)):
                    for k in [2 * q + i for q in quarters for i in range(2)]:
                        last = pe.matmul(bank_of(f"O{t}", 0)[:, :], mx[:, k, t * P:(t + 1) * P], w_out[:, k, :],
                                         start=(k == 0), stop=(k == ET - 1))
                    if 3 in quarters:
                        last.then_inc(full, 1)

                def unit(b, s, g, name, first=False):
                    def turn(i, j, with_output=False):
                        for r in range(2):
                            step = b * STEPS + (s * 2 + g) * N + i * 4 + (2 * j + r)
                            pe.wait_ge(scanned, SCANNED + (step + 1) * GE)
                            for t in range(TT):
                                pe.wait_ge(added, step * TT + t + 1)
                                for e in range(GE):
                                    last = pe.transpose(banks[2 + t][:, e * P:(e + 1) * P],
                                                        state[r][:, e, t * P:(t + 1) * P], ident[:, :])
                                last.then_inc(turned, 1)
                            if with_output:
                                if (i, j, r) == (0, 0, 0):
                                    pe.wait_ge(gated, b * ET)
                                elif j == r == 0:
                                    pe.wait_ge(*wait_drained(b, f"O{i - 1}", 0))
                                output(b, i, [2 * j + r])

                    if name == "Z1":
                        pe.wait_ge(*wait_drained(b - 1, "DL0", ET - 1))
                        for p in range(PARTS):
                            for j in range(2):
                                if 2 * p + j > 0:
                                    pe.wait_ge(*wait_drained(b, f"Z1{p if j else p - 1}", 1 - j))
                                tile(b, "Z1", p, j)
                                turn(p, j, not first)
                            if first:
                                absent(pe, full, "pe", b, f"O{p}", 1)
                        return
                    if name:
                        for k in range(RING):
                            wait_bank(b, name, k)
                        pe.sem_inc(passed, 1)
                        base = st.drained(b, name, 0)[1]
                    with pe.Fori(0, PARTS) as i:
                        for j in range(2):
                            if name:
                                pe.wait_ge(drained["act"], base + i * 2 + (j - 2))
                                tile(b, name, i, j)
                            turn(i, j)

                def sums(b, s, g):
                    pe.wait_ge(added, (b * STEPS + (s * 2 + g + 1) * N) * TT + TT)
                    for e in range(GE):
                        wait_bank(b, f"Y{s}{g}", e)
                        for t in range(TT):
                            last = pe.transpose(bank_of(f"Y{s}{g}", e)[:, t * P:(t + 1) * P],
                                                acc[:, t, e * P:(e + 1) * P], ident[:, :])
                        last.then_inc(full, 1)

                def first_columns():
                    pe.wait_ge(*wait_drained(-1, "T", DT - 1))
                    for m in range(ET):
                        wait_bank(-1, "Z0", m)
                        tile(-1, "Z0", m // 2, m % 2)

                def deltas(b, sums):
                    pe.wait_ge(*wait_drained(b, "Z0", ET - 1))
                    dbc(b, 0)
                    sums()
                    dbc_turned(b, 0)
                    dl(b, 0)

                def before():
                    around_front(pe, full, "pe", lambda: norms(-1), first_columns, deltas)
                    pe.wait_ge(w_out_loaded, 16)

                def body(b, first, last):
                    unit(b, 0, 0, "Z1", first)
                    sums(b, 0, 0)
                    unit(b, 0, 1, "MX")
                    pe.wait_ge(*wait_drained(b, f"Z1{PARTS - 1}", 1))
                    dbc(b, 1)
                    sums(b, 0, 1)
                    dbc_turned(b, 1)
                    if last:
                        absent(pe, full, "pe", b, "T", 1)
                        pe.wait_ge(*wait_drained(b, "TC1", 0))
                    else:
                        norms(b)
                    dl(b, 1)
                    if not last:
                        pe.wait_ge(*wait_drained(b, "T", DT - 1))
                        pe.sem_inc(passed, 1)
                    unit(b, 1, 0, None)
                    sums(b, 1, 0)
                    if last:
                        pe.wait_ge(*wait_drained(b, "Y10", GE - 1))
                        unit(b, 1, 1, None)
                        absent(pe, full, "pe", b, "Z0", 2)
                        sums(b, 1, 1)
                        absent(pe, full, "pe", b, "TC0", 2)
                    else:
                        unit(b, 1, 1, "Z0")
                        deltas(b, lambda: sums(b, 1, 1))

                def after():
                    pe.wait_ge(gated, B * ET)
                    for t in range(TT):
                        absent(pe, full, "pe", B, f"Z1{t}", 1)
                        if t > 0:
                            pe.wait_ge(*wait_drained(B, f"O{t - 1}", 0))
                        output(B, t)

                batches(pe, before, body, after)

            @block.vector
            def _(dve):
                dve.sem_inc(added, TT)
                dve.sem_inc(scanned, SCANNED)
                dve.wait_ge(w_loaded, 5 * 16)
                dve.wait_ge(const_ready, 2)

                def norms(b, between=lambda: None):
                    dve.wait_ge(x_loaded, b * 16 + 16)
                    dve.wait_ge(ada_loaded, b * 16 + 16)
                    for t in range(TT):
                        dve.bn_stats(stats[:, t, :], x[:, t, :]).then_inc(stats_ready, 1)
                    for t in range(TT):
                        dve.wait_ge(stats_ready, b * TT + t + 1)
                        dve.sem_inc(passed, 1)
                        dve.bn_aggr(mv[:, t, :], stats[:, t, :]).then_inc(mv_ready, 1)
                    dve.wait_ge(rstd_ready, b + 1)
                    for t in range(TT):
                        dve.tensor_scalar(xs[:, t, :], x[:, t, :], mv[:, t, 0:1], rstd[:, t:t + 1],
                                          ALU.subtract, ALU.mult).then_inc(xn_ready, 1)
                    for t in range(TT):
                        dve.wait_ge(xn_ready, b * TT + t + 1)
                        dve.tensor_tensor(xs[:, t, :], xs[:, t, :], ada[:, 0, :], ALU.mult).then_inc(xs_ready, 1)
                    for t in range(TT):
                        dve.wait_ge(xs_ready, b * 2 * TT + t + 1)
                        dve.tensor_tensor(xs[:, t, :], xs[:, t, :], ada[:, 1, :], ALU.add).then_inc(xs_ready, 1)
                    for t in range(TT):
                        dve.wait_ge(xs_ready, b * 2 * TT + TT + t + 1)
                        dve.bn_stats(stats2[:, t, :], xs[:, t, :]).then_inc(stats2_ready, 1)
                    for t in range(TT):
                        dve.wait_ge(stats2_ready, b * TT + t + 1)
                        dve.sem_inc(passed, 1)
                        dve.bn_aggr(mv2[:, t, :], stats2[:, t, :]).then_inc(mv2_ready, 1)
                    between()
                    dve.wait_ge(rstd2_ready, b + 1)
                    for t in range(TT):
                        dve.tensor_scalar(xn[:, t, :], xs[:, t, :], mv2[:, t, 0:1], rstd2[:, t:t + 1],
                                          ALU.subtract, ALU.mult).then_inc(xn2_ready, 1)

                def dbc(b, s, stored):
                    dve.wait_ge(full, st.full(b, f"DBC{s}", 0))
                    if stored is not None:
                        dve.wait_ge(b_stored, stored)
                    dve.tensor_copy(dbc_t[:, :], bank_of(f"DBC{s}", 0)[0:96, :]).then_inc(drained["dve"], 1)

                def dbc_turned(b, s):
                    dve.wait_ge(full, st.full(b, f"TC{s}", 0))
                    dve.tensor_copy(dbc_tm[:, :, :].rearrange("p t n -> p (t n)"),
                                    bank_of(f"TC{s}", 0)[:, 0:TT * 96]).then_inc(drained["dve"], 1)

                def direct():
                    for m in range(ET):
                        dp = cols[:, DPC + ET + m:DPC + ET + m + 1]
                        dve.scalar_tensor_tensor(y_sum[:, m, :], z[1][:, m, :], dp, y_sum[:, m, :],
                                                 ALU.mult, ALU.add).then_inc(u_used[1], 1)

                def softplus(b, s, index):
                    def finish(m):
                        dve.wait_ge(soft_out, 2 * (index * ET + m) + 2)
                        dve.tensor_tensor(delta[:, m, :], delta[:, m, :], soft[:, m % 2, :], ALU.max
                                          ).then_inc(delta_ready, 1)

                    for m in range(ET):
                        dve.wait_ge(full, st.full(b, f"DL{s}", m))
                        bias = cols[:, BDT + s * ET + m:BDT + s * ET + m + 1]
                        dve.tensor_scalar(delta[:, m, :], bank_of(f"DL{s}", m)[:, :], bias, None, ALU.add
                                          ).then_inc(drained["dve"], 1)
                        if m >= 2:
                            finish(m - 2)
                        dve.wait_ge(*wait_drained(b, f"DL{s}", m))
                        if m >= 2:
                            dve.wait_ge(delta_ready, index * ET + m - 1)
                        dve.tensor_scalar(soft[:, m % 2, :], delta[:, m, :], SP_CAP, None, ALU.min
                                          ).then_inc(soft_in, 1)
                    finish(ET - 2)
                    finish(ET - 1)

                def output(b, t):
                    if t == 0:
                        dve.wait_ge(gate_loaded, b * 16)
                        dve.wait_ge(resid_loaded, b * 16)
                    dve.wait_ge(full, st.full(b, f"O{t}", 0))
                    dve.tensor_tensor(soft[:, t % 2, :], bank_of(f"O{t}", 0)[:, :], gate[:, :], ALU.mult
                                      ).then_inc(drained["dve"], 1)
                    dve.wait_ge(*wait_drained(b, f"O{t}", 0))
                    dve.tensor_tensor(x[:, t, :], x[:, t, :], soft[:, t % 2, :], ALU.add).then_inc(out_ready, 1)

                def unit(b, s, g, first=False):
                    order = slice(None, None, -1 if s else 1)

                    def scan(step, j):
                        dve.wait_ge(dbu_ready, SPARE + step + 1)
                        for e in range(GE):
                            dve.wait_ge(da_ready, step * GE + e + 1)
                            dve.tensor_tensor_scan(state[j][:, e, order], banks[e % 2][:, order],
                                                   d_bu[j][:, e, order], 0.0, ALU.mult, ALU.add
                                                   ).then_inc(scanned, 1)

                    def add(step, n):
                        start = isinstance(n, int) and n == 0
                        for t in range(TT):
                            dve.wait_ge(turned, 1 + step * TT + t + 1)
                            at = slice(n + R + N, n + R + N + 1) if isinstance(n, int) else bass.ds(n + (R + N), 1)
                            c = dbc_tm[:, t, at]
                            if start:
                                ins = dve.tensor_scalar(acc[:, t, :], banks[2 + t][:, :], c, None, ALU.mult)
                            else:
                                dve.wait_ge(added, step * TT + t + 1)
                                ins = dve.scalar_tensor_tensor(acc[:, t, :], banks[2 + t][:, :], c, acc[:, t, :],
                                                               ALU.mult, ALU.add)
                            ins.then_inc(added, 1)

                    base = b * STEPS + (s * 2 + g) * N
                    scan(base, 0)
                    scan(base + 1, 1)
                    add(base, 0)
                    if (s, g) == (0, 0):
                        for n in range(2, N, 2):
                            scan(base + n, 0)
                            add(base + n - 1, n - 1)
                            scan(base + n + 1, 1)
                            if n % 4 == 0 and not first:
                                output(b, n // 4 - 1)
                            elif n % 4 == 0:
                                absent(dve, drained["dve"], "dve", b, f"O{n // 4 - 1}", 1)
                            add(base + n, n)
                    else:
                        with dve.Fori(1, N // 2) as pair:
                            n = pair * 2
                            scan(base + n, 0)
                            add(base + n - 1, n - 1)
                            scan(base + n + 1, 1)
                            add(base + n, n)
                    add(base + N - 1, N - 1)
                    if (s, g) == (0, 0) and not first:
                        output(b, PARTS - 1)
                    elif (s, g) == (0, 0):
                        absent(dve, drained["dve"], "dve", b, f"O{PARTS - 1}", 1)

                def sums(b, s, g):
                    for e in range(GE):
                        dve.wait_ge(full, st.full(b, f"Y{s}{g}", e))
                        dve.tensor_tensor(y_sum[:, g * GE + e, :], bank_of(f"Y{s}{g}", e)[:, :],
                                          y_sum[:, g * GE + e, :], ALU.add).then_inc(drained["dve"], 1)

                def gating(b, g):
                    dve.wait_ge(*wait_drained(b, f"Y1{g}", GE - 1))
                    for m in range(g * GE, (g + 1) * GE):
                        dve.wait_ge(silu_ready, b * ET + m + 1)
                        dve.tensor_tensor(mx[:, m, :], y_sum[:, m, :], mx[:, m, :], ALU.mult).then_inc(gated, 1)

                def deltas(b, sums):
                    dbc(b, 0, None if isinstance(b, int) and b < 0 else b * 32 + 32)
                    sums()
                    dbc_turned(b, 0)
                    softplus(b, 0, (b + 1) * 2)
                    dve.wait_ge(*wait_drained(b, "TC0", 0))

                def last_sums(b):
                    sums(b, 1, 1)
                    gating(b, 1)

                def before():
                    around_front(dve, drained["dve"], "dve", lambda: norms(0), lambda: None, deltas)

                def body(b, first, last):
                    unit(b, 0, 0, first)
                    dve.wait_ge(u_used[0], (b + 1) * ET)
                    sums(b, 0, 0)
                    unit(b, 0, 1)

                    def between():
                        dbc(b, 1, b * 32 + 16)
                        sums(b, 0, 1)

                    if last:
                        between()
                    else:
                        norms(b + 1, between)
                    dve.wait_ge(*wait_drained(b, "Y01", GE - 1))
                    dve.wait_ge(*wait_drained(b, "DBC1", 0))
                    dve.wait_ge(drained["act"], st.drained(b, f"Z1{PARTS - 1}", 1)[1])
                    direct()
                    dbc_turned(b, 1)
                    softplus(b, 1, b * 2 + 1)
                    dve.wait_ge(*wait_drained(b, "TC1", 0))
                    dve.wait_ge(u_used[1], (b + 1) * ET)
                    unit(b, 1, 0)
                    sums(b, 1, 0)
                    unit(b, 1, 1)
                    gating(b, 0)
                    if last:
                        absent(dve, drained["dve"], "dve", b, "DBC0", 1)
                        last_sums(b)
                        absent(dve, drained["dve"], "dve", b, "TC0", 2)
                    else:
                        deltas(b, lambda: last_sums(b))

                def after():
                    for t in range(TT):
                        output(B, t)

                batches(dve, before, body, after)


def program(nc, d, out):
    with ExitStack() as ctx:
        banks = [ctx.enter_context(nc.psum_tensor(f"bank{i}", [P, 512], F32)) for i in range(8)]
        sb = lambda n, s: ctx.enter_context(nc.sbuf_tensor(n, s, F32))
        mod_all = {"gain": sb("gain", [P, 3, DT, B]), "shift": sb("shift", [P, 3, DT, B]),
                   "ssm_cols": sb("ssm_cols", [P, 72]), "bzc": sb("bzc", [P, 16])}
        d = dict(d)
        for name, shape in (("wzc", [2, D, E]), ("ada_d", [B, 3 * D]), ("b_d", [2, N, T]),
                            ("x1", [B, T, D]), ("x2", [B, T, D]), ("x3", [B, T, D]),
                            ("resid_d", [B, T, D])):
            d[name] = nc.dram_tensor(name, shape, F32, kind="Internal").ap()
        d["b_flat"] = d["b_d"].rearrange("s n t -> s (n t)")
        cols_loaded = ctx.enter_context(nc.semaphore("cols_loaded"))
        with nc.Block() as block:

            @block.sync
            def _(sp):
                sp.dma_start(mod_all["ssm_cols"][:, :], d["ssm_cols"]).then_inc(cols_loaded, 16)
                sp.wait_ge(cols_loaded, 16)

        sems = LayerSemaphores(nc)
        prologue(nc, sems, d, mod_all, banks)
        sems.clear()
        attention_layer(nc, sems, d, mod_all, banks, 0, d["x"], d["x1"])
        sems.clear()
        attention_layer(nc, sems, d, mod_all, banks, 1, d["x1"], d["x2"])
        sems.clear()
        attention_layer(nc, sems, d, mod_all, banks, 2, d["x2"], d["x3"])
        sems.clear()
        ssm_layer(nc, sems, d, mod_all, banks, d["x3"], out)


def kernel(**inputs):
    import numpy as np
    import concourse.bacc as bacc
    from concourse.bass_utils import run_bass_kernel_spmd

    v = {k: np.asarray(a) for k, a in inputs.items()}
    col = lambda a: a.reshape(-1, P).T
    layers = [
        dict(n="L0_cond_", nw="norm_scale", nb="norm_bias", wq="Wq", wk="Wk", wv="Wv", wo="film_out_W", bq="bq",
             bk="bk", bv="bv", bo="film_out_b", mw="film_emb_W", mb="film_emb_b", n2w="film_norm_scale",
             n2b="film_norm_bias"),
        dict(n="L1_cond_", nw="ln_w", nb="ln_b", wq="Wq", wk="Wk", wv="Wv", wo="W_out", bq="bq", bk="bk", bv="bv",
             bo="b_out", mw="W_emb", mb="b_emb", n2w="ln2_w", n2b="ln2_b"),
        dict(n="L2_cond_", nw="norm_w", nb="norm_b", wq="q_w", wk="k_w", wv="v_w", wo="out_w", bq="q_b", bk="k_b",
             bv="v_b", bo="out_b", mw="emb_w", mb="emb_b", n2w="sb_norm_w", n2b="sb_norm_b"),
    ]
    g = lambda l, key: v[l["n"] + l[key]]
    s = lambda key: v["L3_cond_" + key]
    arrays = {
        "x": v["x"],
        "cond": v["cond_2048"],
        "ident": np.eye(P, dtype=np.float32),
        "block_masks": np.stack([np.kron(np.eye(P // w), np.ones((w, w))) for w in (32, 64)], 1).astype(np.float32),
        "att_w": np.stack([np.stack([g(l, k) for k in ("wq", "wk", "wv", "wo")]) for l in layers]),
        "mod_w": np.stack([g(l, "mw") for l in layers]),
        "att_cols": np.stack([np.concatenate([col(a) for a in (g(l, "nw"), g(l, "nb"), g(l, "bq"), g(l, "bk"),
                                                               g(l, "mb")[:D], g(l, "mb")[D:], g(l, "n2w"),
                                                               g(l, "n2b"))], 1) for l in layers], 1),
        "att_rows": np.stack([np.concatenate([g(l, "bq"), g(l, "bv"), g(l, "bo")]) for l in layers]),
        "ada_wT": s("Wada").T,
        "ada_rows": np.concatenate([s("norm1_g"), s("norm1_b"), s("bada")])[None],
        "wz": s("Wz"),
        "wcT": np.stack([s("Wc1").T, s("Wc2").T]),
        "wxT": s("Wx").T,
        "wfT": s("Wf").T,
        "wdbcT": np.stack([s("Wdbc1").T, s("Wdbc2").T]),
        "wdtT": np.stack([s("Wdt1").T, s("Wdt2").T]),
        "alog": np.stack([s("Alog1"), s("Alog2")]).reshape(2, ET, P, N).transpose(2, 0, 1, 3).reshape(P, -1),
        "ssm_cols": np.concatenate([col(s(k)) for k in ("norm2_g", "norm2_b", "bx", "bc1", "bc2", "bz", "bdt1",
                                                        "bdt2", "Dp1", "Dp2")], 1),
        "bf_row": s("bf")[None],
    }
    for i, key in enumerate(("mask_BxS_ik0", "mask_BxSx1_fk1", "mask_BxS_ff1")):
        m = v[key].reshape(B, T)
        arrays[f"mask{i}"] = m[:, None]
        arrays[f"mask{i}_t"] = m.reshape(B * TT, P).T
    nc = bacc.Bacc("TRN2", target_bir_lowering=False, num_devices=1)
    maps, d = {}, {}
    for name, a in arrays.items():
        a = np.ascontiguousarray(a)
        maps["in_" + name] = a
        d[name] = nc.dram_tensor("in_" + name, a.shape, mybir.dt.from_np(a.dtype), kind="ExternalInput").ap()
    out = nc.dram_tensor("out_0", (B, T, D), F32, kind="ExternalOutput").ap()
    program(nc, d, out)
    r = run_bass_kernel_spmd(nc, [maps], core_ids=[0])
    return r.results[0]["out_0"]
```

```python
import concourse.bass as bass
from concourse import mybir
from contextlib import ExitStack

F32 = mybir.dt.float32
I32 = mybir.dt.int32
ALU = mybir.AluOpType
ACT = mybir.ActivationFunctionType
AX = mybir.AxisListType

P = 128
B = 8
T = 512
D = 512
E = 1024
N = 16
R = 64
TT = T // P
DT = D // P
ET = E // P
EPS = 1e-5
NEG = -1.0e30
SP_CAP = 40.0

NW, NB, BQ, BK, FS, FH, N2W, N2B = range(8)
G2, B2, BX, BC, BZ, BDT, DPC = 0, 4, 8, 16, 32, 40, 56


class Stages:

    def __init__(self, plan):
        self.plan, self.first, self.by, self.per = plan, {}, [], {}
        for name, n, engine in plan:
            self.first[name] = len(self.by)
            self.by += [engine] * n
        for engine in set(self.by):
            self.per[engine] = self.by.count(engine)
        self.n = len(self.by)

    def full(self, b, name, k=0):
        return (b + 1) * self.n + self.first[name] + k + 1

    def drained(self, b, name, k=0):
        at = self.first[name] + k
        engine = self.by[at]
        return engine, (b + 1) * self.per[engine] + self.by[: at + 1].count(engine)

    def before(self, b, name, k, ring):
        at = self.first[name] + k - ring
        if at >= 0:
            engine = self.by[at]
            return engine, (b + 1) * self.per[engine] + self.by[: at + 1].count(engine)
        engine = self.by[at + self.n]
        return engine, b * self.per[engine] + self.by[: at + self.n + 1].count(engine)


def absent(stages, eng, semaphore, by, b, first, n=1):
    plan = stages.plan
    at = [i[0] for i in plan].index(first)
    count = lambda part: sum(k for _, k, engine in part if by in ("pe", engine))
    if not count(plan[at:at + n]):
        return
    before = (b + 1) * count(plan) + count(plan[:at])
    if not isinstance(before, int) or before > 0:
        eng.wait_ge(semaphore, before)
    eng.sem_inc(semaphore, count(plan[at:at + n]))


class LayerSemaphores:

    def __init__(self, nc):
        self.nc, self.held = nc, []

    def take(self, name):
        self.held.append(self.nc.alloc_semaphore(name=name))
        return self.held[-1]

    def clear(self):
        self.nc.clear_and_free_semaphores(self.held)
        self.held = []
        self.nc.all_engine_barrier()


def prologue(nc, sems, d, mod_all, banks):
    with ExitStack() as ctx:
        sb = lambda n, s, t=F32: ctx.enter_context(nc.sbuf_tensor("pro_" + n, s, t))
        sem = lambda n: sems.take("pro_" + n)
        cond = sb("cond", [B, E])
        ident = sb("ident", [P, P])
        silu_t = sb("silu_t", [P, ET, B])
        w_mod = [sb(f"w_mod{i}", [P, ET, 512]) for i in range(2)]
        cols = sb("cols", [P, 3, 8 * DT])
        raw = sb("raw", [P, 2 * DT, B])
        ada_bias = sb("ada_bias", [B, 5, D])
        ada = sb("ada", [B, 3, D])
        wz = sb("wz", [P, ET, D])
        wc = [sb(f"wc{s}", [P, ET, E]) for s in range(2)]
        rows = [sb(f"rows{i}", [B, 512]) for i in range(2)]
        bias_row = sb("bias_row", [1, 2, E])
        fused = [sb(f"fused{i}", [P, D]) for i in range(2)]

        loaded, stored = sem("loaded"), [sem(f"stored{i}") for i in range(2)]
        w_loaded = [sem(f"w_loaded{i}") for i in range(2)]
        wc_loaded = [sem(f"wc_loaded{s}") for s in range(2)]
        silu_ready, silu_t_full, silu_t_ready = sem("silu"), sem("silu_t_full"), sem("silu_t")
        full, drained, mod_step, ada_ready = sem("full"), sem("drained"), sem("mod_step"), sem("ada_ready")
        fused_full, fused_ready = sem("fused_full"), sem("fused_ready")
        cols_full, cols_read = sem("cols_full"), sem("cols_read")
        bias_full, bias_ready, bias_cols = sem("bias_full"), sem("bias_ready"), sem("bias_cols")
        pieces = [(d["mod_w"][l], 512 * h) for l in range(3) for h in range(2)]
        pieces += [(d["ada_wT"], 512 * h) for h in range(3)]
        with nc.Block() as block:

            @block.sync
            def _(sp):
                sp.dma_start(cond[:, :], d["cond"]).then_inc(loaded, 16)
                sp.dma_start(ident[:, :], d["ident"]).then_inc(loaded, 16)
                sp.dma_start(cols[:, :, :], d["att_cols"]).then_inc(loaded, 16)
                sp.dma_start(ada_bias[:, :, :].rearrange("b r n -> b (r n)"),
                             d["ada_rows"].broadcast_to([B, 5 * D])).then_inc(loaded, 16)
                sp.dma_start(wz[:, :, :], d["wz"].rearrange("(k p) n -> p k n", p=P)).then_inc(loaded, 16)
                for i, (w, c0) in enumerate(pieces):
                    if i >= 2:
                        sp.wait_ge(full, i - 1)
                    sp.dma_start(w_mod[i % 2][:, :, :], w[:, c0:c0 + 512].rearrange("(k p) n -> p k n", p=P)
                                 ).then_inc(w_loaded[i % 2], 16)
                for s in range(2):
                    sp.dma_start(wc[s][:, :, :], d["wcT"][s].rearrange("(k p) n -> p k n", p=P)
                                 ).then_inc(wc_loaded[s], 16)
                for s in range(2):
                    for m in range(DT * 2):
                        i = s * 8 + m
                        sp.wait_ge(fused_ready, i + 1)
                        sp.dma_start(d["wzc"][s, (m // 2) * P:(m // 2 + 1) * P, (m % 2) * 512:(m % 2 + 1) * 512],
                                     fused[i % 2][:, :]).then_inc(stored[i % 2], 16)
                sp.wait_ge(ada_ready, 1)
                sp.dma_start(d["ada_d"], ada[:, :, :].rearrange("b r n -> b (r n)")).then_inc(loaded, 16)
                sp.wait_ge(loaded, 96)
                for i in range(2):
                    sp.wait_ge(stored[i], 128)

            @block.scalar
            def _(act):
                act.wait_ge(loaded, 80)
                act.activation(cond[:, :], cond[:, :], ACT.Silu).then_inc(silu_ready, 1)

            @block.tensor
            def _(pe):
                pe.wait_ge(silu_ready, 1)
                for k in range(ET):
                    last = pe.transpose(banks[0][:, k * B:(k + 1) * B], cond[:, k * P:(k + 1) * P], ident[0:B, 0:B])
                last.then_inc(silu_t_full, 1)
                pe.wait_ge(silu_t_ready, 1)
                for i in range(9):
                    pe.wait_ge(w_loaded[i % 2], 16 * (i // 2 + 1))
                    if i >= 2:
                        pe.wait_ge(drained, i - 1)
                    for k in range(ET):
                        last = pe.matmul(banks[1 + i % 2][0:B, :], silu_t[:, k, :], w_mod[i % 2][:, k, :],
                                         start=(k == 0), stop=(k == ET - 1))
                    last.then_inc(full, 1)
                    if 1 <= i <= 6:
                        pe.wait_ge(drained, i)
                        if i >= 3:
                            pe.wait_ge(cols_read, i - 2)
                        for m in range(4):
                            last = pe.transpose(banks[6 + (i - 1) % 2][:, m * B:(m + 1) * B],
                                                rows[(i - 1) % 2][:, m * P:(m + 1) * P], ident[0:B, 0:B])
                        last.then_inc(cols_full, 1)
                for s in range(2):
                    pe.wait_ge(wc_loaded[s], 16)
                    for m in range(8):
                        i = s * 8 + m
                        if i >= 2:
                            pe.wait_ge(fused_ready, i - 1)
                        for k in range(ET):
                            last = pe.matmul(banks[3 + i % 2][:, :], wz[:, k, (m // 2) * P:(m // 2 + 1) * P],
                                             wc[s][:, k, (m % 2) * 512:(m % 2 + 1) * 512],
                                             start=(k == 0), stop=(k == ET - 1))
                        last.then_inc(fused_full, 1)
                    for h in range(2):
                        if s == 1:
                            pe.wait_ge(bias_ready, h + 1)
                        for k in range(ET):
                            last = pe.matmul(banks[1 + h][0:1, :], mod_all["ssm_cols"][:, BZ + k:BZ + k + 1],
                                             wc[s][:, k, h * 512:(h + 1) * 512], start=(k == 0), stop=(k == ET - 1))
                        last.then_inc(bias_full, 1)
                pe.wait_ge(bias_ready, 4)
                for s in range(2):
                    for m in range(ET):
                        last = pe.transpose(banks[5][:, s * ET + m:s * ET + m + 1],
                                            bias_row[:, s, m * P:(m + 1) * P], ident[0:1, 0:1])
                last.then_inc(bias_cols, 1)

            @block.vector
            def _(dve):
                steps = [0]

                def step(ins):
                    ins.then_inc(mod_step, 1)
                    steps[0] += 1
                    dve.wait_ge(mod_step, steps[0])

                dve.wait_ge(silu_t_full, 1)
                dve.tensor_copy(silu_t[:, :, :].rearrange("p k b -> p (k b)"), banks[0][:, 0:ET * B]
                                ).then_inc(silu_t_ready, 1)
                dve.wait_ge(loaded, 80)
                col = lambda l, v: cols[:, l, v * DT:(v + 1) * DT].unsqueeze(2).broadcast_to([P, DT, B])

                def modulation(i):
                    l, h = i // 2, i % 2
                    dve.wait_ge(cols_full, i + 1)
                    dve.tensor_tensor(raw[:, h * DT:(h + 1) * DT, :],
                                      banks[6 + i % 2][:, 0:DT * B].rearrange("p (m b) -> p m b", b=B),
                                      col(l, (FS, FH)[h]), ALU.add).then_inc(cols_read, 1)
                    dve.wait_ge(cols_read, i + 1)
                    if h == 0:
                        return
                    gain, shift = mod_all["gain"][:, l, :, :], mod_all["shift"][:, l, :, :]
                    step(dve.tensor_scalar(raw[:, 0:DT, :], raw[:, 0:DT, :], 1.0, None, ALU.add))
                    step(dve.tensor_tensor(gain, raw[:, 0:DT, :], col(l, N2W), ALU.mult))
                    step(dve.tensor_tensor(shift, raw[:, 0:DT, :], col(l, N2B), ALU.mult))
                    step(dve.tensor_tensor(shift, shift, raw[:, DT:2 * DT, :], ALU.add))

                for i in range(9):
                    dve.wait_ge(full, i + 1)
                    if i < 6:
                        if i >= 2:
                            dve.wait_ge(cols_full, i - 1)
                        dve.tensor_copy(rows[i % 2][:, :], banks[1 + i % 2][0:B, :]).then_inc(drained, 1)
                    else:
                        dve.tensor_tensor(ada[:, i - 6, :], banks[1 + i % 2][0:B, :], ada_bias[:, i - 4, :], ALU.add
                                          ).then_inc(drained, 1)
                    if 1 <= i <= 6:
                        modulation(i - 1)
                dve.wait_ge(drained, 9)
                step(dve.tensor_scalar(ada[:, 1, :], ada[:, 1, :], 1.0, None, ALU.add))
                step(dve.tensor_tensor(ada_bias[:, 1, :], ada_bias[:, 1, :], ada[:, 1, :], ALU.mult))
                step(dve.tensor_tensor(ada_bias[:, 1, :], ada_bias[:, 1, :], ada[:, 0, :], ALU.add))
                step(dve.tensor_tensor(ada[:, 0, :], ada[:, 1, :], ada_bias[:, 0, :], ALU.mult))
                step(dve.tensor_copy(ada[:, 1, :], ada_bias[:, 1, :]))
                dve.sem_inc(ada_ready, 1)
                for s in range(2):
                    for m in range(8):
                        i = s * 8 + m
                        dve.wait_ge(fused_full, i + 1)
                        if i >= 2:
                            dve.wait_ge(stored[i % 2], 16 * (i // 2))
                        dve.tensor_copy(fused[i % 2][:, :], banks[3 + i % 2][:, :]).then_inc(fused_ready, 1)
                    for h in range(2):
                        dve.wait_ge(bias_full, s * 2 + h + 1)
                        dve.tensor_copy(bias_row[:, s, h * 512:(h + 1) * 512], banks[1 + h][0:1, :]
                                        ).then_inc(bias_ready, 1)
                dve.wait_ge(bias_cols, 1)
                dve.tensor_tensor(mod_all["bzc"][:, :], banks[5][:, 0:16], mod_all["ssm_cols"][:, BC:BC + 16], ALU.add)


def attention_layer(nc, sems, d, mod_all, banks, layer, x_in, x_out):
    H = (16, 8, 16)[layer]
    dh = D // H
    linear = layer < 2
    if linear:
        plan = [("V", 4, "dve"), ("TK", 4, "act"), ("TQ", 4, "act"), ("A", 4, "dve"), ("Y", 4, "dve"),
                ("T", 4, "act"), ("K", 4, "dve"), ("TY", 4, "act"), ("Q", 4, "dve"), ("O", 4, "dve")]
    else:
        plan = [("V", 4, "dve"), ("YT", 4, "dve"), ("T", 4, "act"), ("K", 4, "act"),
                ("TY", 4, "act"), ("Q", 4, "act"), ("O", 4, "dve")]
    st = Stages(plan)

    def bank_of(name, k):
        if linear:
            return banks[(st.first[name] + k) % 8]
        return banks[(4 if name in ("V", "YT", "K", "Q") else 0) + k]

    pre = f"l{layer}_"
    HG = 4
    NG = H // HG
    UNITS = TT * H

    with ExitStack() as ctx:
        sb = lambda n, s, t=F32: ctx.enter_context(nc.sbuf_tensor(pre + n, s, t))
        sem = lambda n: sems.take(pre + n)
        w = [sb(f"w{i}", [P, DT, D]) for i in range(4)]
        cols = sb("cols", [P, 8 * DT])
        rows = sb("rows", [P, 3, D])
        ident = sb("ident", [P, P])
        block_mask = sb("block_mask", [P, P])
        minus_half = sb("minus_half", [P, TT])
        keep_in = sb("keep_in", [P, B * TT], I32 if layer == 0 else F32)
        keep = sb("keep", [P, B * TT])
        mask_in = [sb(f"mask_in{j}", [P, T], I32 if layer == 0 else F32) for j in range(2)]
        mask_add = sb("mask_add", [P, T])
        x = [sb(f"x{j}", [P, TT, D]) for j in range(2)]
        out = [sb(f"out{j}", [P, TT, D]) for j in range(2)]
        xn = sb("xn", [P, TT, D])
        xn_t = sb("xn_t", [P, DT, T])
        k_t = sb("k_t", [P, DT, T])
        v_tm = sb("v_tm", [P, TT, D])
        q_t = sb("q_t", [P, DT, T])
        stats = sb("stats", [P, TT, 6])
        mv = sb("mv", [P, TT, 2])
        rstd = sb("rstd", [P, TT])
        y_stats = sb("y_stats", [P, TT, 6])
        y_mv = sb("y_mv", [P, TT, 2])
        y_rstd = sb("y_rstd", [P, TT])
        k_max = sb("k_max", [P, DT])
        k_sum = sb("k_sum", [P, DT])
        q_max = sb("q_max", [P, TT, H])
        q_sum = sb("q_sum", [P, TT, H])
        if linear:
            k_tm, q_tm, y = (sb(n, [P, TT, D]) for n in ("k_tm", "q_tm", "y"))
            h_t = sb("h_t", [P, DT, T])
            attn = sb("attn", [P, DT, P])
        else:
            prob = sb("prob", [P, 2 * HG, T])
            prob_t = sb("prob_t", [P, 2, HG, TT, T])
            y_t = sb("y_t", [P, DT, T])
            y, h_t = prob[:, 0:TT, :], prob[:, TT:2 * TT, :]
            s_max = sb("s_max", [P, TT * H])

        const_loaded, const_ready, passed = sem("const_loaded"), sem("const_ready"), sem("passed")
        half_ready = sem("half_ready")
        w_ready = [sem(f"w_ready{i}") for i in range(4)]
        x_loaded = [sem(f"x_loaded{j}") for j in range(2)]
        mask_loaded = [sem(f"mask_loaded{j}") for j in range(2)]
        x_stored = [sem(f"x_stored{j}") for j in range(2)]
        psum_full = sem("psum_full")
        drained = {"act": sem("act_drained"), "dve": sem("dve_drained")}
        mask_ready, stats_ready, mv_ready = sem("mask_ready"), sem("stats_ready"), sem("mv_ready")
        var_ready, rstd_ready, xn_ready, xb_ready = sem("var_ready"), sem("rstd_ready"), sem("xn_ready"), sem("xb_ready")
        k_max_ready, k_exp_ready, rk_ready = sem("k_max_ready"), sem("k_exp_ready"), sem("rk_ready")
        k_norm_ready = sem("k_norm_ready")
        q_max_ready, q_sub_ready, q_exp_ready = sem("q_max_ready"), sem("q_sub_ready"), sem("q_exp_ready")
        q_sum_ready, v_ready, out_ready = sem("q_sum_ready"), sem("v_ready"), sem("out_ready")
        y_stats_ready, y_mv_ready, y_var_ready = sem("y_stats_ready"), sem("y_mv_ready"), sem("y_var_ready")
        y_rstd_ready, yn_ready = sem("y_rstd_ready"), sem("yn_ready")
        s_full, s_drained, p_ready = sem("s_full"), sem("s_drained"), sem("p_ready")
        pt_full, pt_ready, pv_done, y_drained = sem("pt_full"), sem("pt_ready"), sem("pv_done"), sem("y_drained")

        def wait_bank(pe, b, name, k):
            if linear:
                engine, count = st.before(b, name, k, 8)
                pe.wait_ge(drained[engine], count)
            elif name in ("K", "TY", "Q", "O"):
                pe.wait_ge(*wait_drained(b, {"K": "YT", "TY": "T", "Q": "K", "O": "TY"}[name], k))
            elif name == "V":
                pe.wait_ge(*wait_drained(b - 1, "Q", k))

        def batches(eng, body):
            with eng.Fori(0, B // 2 - 1) as pair:
                for j in range(2):
                    body(pair * 2 + j, pair, j, False)
            body(B - 2, B // 2 - 1, 0, False)
            body(B - 1, B // 2 - 1, 1, True)

        def wait_drained(b, name, k):
            engine, count = st.drained(b, name, k)
            return drained[engine], count

        def transposes(pe, b, name, src):
            for k in range(4):
                wait_bank(pe, b, name, k)
                for i in range(4):
                    last = pe.transpose(bank_of(name, k)[:, i * P:(i + 1) * P], src[:, i, k * P:(k + 1) * P],
                                        ident[:, :])
                last.then_inc(psum_full, 1)

        def project_t(pe, b, name, weight):
            for m in range(DT):
                wait_bank(pe, b, name, m)
                for k in range(DT):
                    last = pe.matmul(bank_of(name, m)[:, :], weight[:, k, m * P:(m + 1) * P], xn_t[:, k, :],
                                     start=(k == 0), stop=(k == DT - 1))
                last.then_inc(psum_full, 1)

        def project(pe, b, name, src_t, weight):
            for t in range(TT):
                wait_bank(pe, b, name, t)
                for k in range(DT):
                    last = pe.matmul(bank_of(name, t)[:, :], src_t[:, k, t * P:(t + 1) * P], weight[:, k, :],
                                     start=(k == 0), stop=(k == DT - 1))
                last.then_inc(psum_full, 1)

        def attention_pe(pe, b):
            pe.wait_ge(*wait_drained(b - 1, "Q", DT - 1))
            pe.wait_ge(*wait_drained(b - 1, "O", TT - 1))

            def scores(g):
                quad, t = g // TT, g % TT
                for i in range(HG):
                    if g > 0:
                        pe.wait_ge(s_drained, b * UNITS + g * HG + i - HG + 1)
                    head = slice(dh * i, dh * (i + 1))
                    pe.matmul(banks[i][:, :], q_t[head, quad, t * P:(t + 1) * P], k_t[head, quad, :],
                              start=True, stop=True).then_inc(s_full, 1)

            def transpose_p(u):
                pe.wait_ge(p_ready, b * UNITS + u + 1)
                if u >= 2:
                    pe.wait_ge(pt_ready, b * UNITS + u - 1)
                for m in range(TT):
                    last = pe.transpose(banks[4 + u % 2][:, m * P:(m + 1) * P],
                                        prob[:, u % (2 * HG), m * P:(m + 1) * P], ident[:, :])
                last.then_inc(pt_full, 1)

            def values(quad):
                pe.wait_ge(pt_ready, b * UNITS + (quad + 1) * TT * HG)
                if quad >= 2:
                    pe.wait_ge(y_drained, b * DT + quad - 1)
                for m in range(TT):
                    for i in range(HG):
                        h = quad * HG + i
                        last = pe.matmul(banks[6 + quad % 2][dh * i:dh * (i + 1), :], v_tm[:, m, h * dh:(h + 1) * dh],
                                         prob_t[:, quad % 2, i, m, :], start=(m == 0), stop=(m == TT - 1))
                last.then_inc(pv_done, 1)

            scores(0)
            pe.wait_ge(v_ready, (b + 1) * TT)
            for g in range(TT * NG):
                if g + 1 < TT * NG:
                    scores(g + 1)
                for i in range(HG):
                    transpose_p(g * HG + i)
                if g % TT == 0 and g > 0:
                    values(g // TT - 1)
            values(NG - 1)
            pe.wait_ge(s_drained, (b + 1) * UNITS)
            pe.wait_ge(y_drained, (b + 1) * DT)
            transposes(pe, b, "YT", y_t)

        def attention_act(act, b):
            def exps(g):
                for i in range(HG):
                    u = g * HG + i
                    act.wait_ge(s_drained, b * UNITS + u + 1)
                    h = (g // TT) * HG + i
                    act.activation(prob[:, u % (2 * HG), :], prob[:, u % (2 * HG), :], ACT.Exp, scale=-1.0,
                                   bias=s_max[:, u:u + 1],
                                   accum_out=q_sum[:, g % TT, h:h + 1]).then_inc(p_ready, 1)

            for g in range(TT * NG):
                exps(g)

        def attention_dve(dve, b):
            def scores(g):
                for i in range(HG):
                    u = g * HG + i
                    dve.wait_ge(s_full, b * UNITS + u + 1)
                    if u >= 2 * HG:
                        dve.wait_ge(pt_full, b * UNITS + u - 2 * HG + 1)
                    dve.sem_inc(passed, 1)
                    dve.tensor_tensor_reduce(out=prob[:, u % (2 * HG), :], in0=banks[i][:, :],
                                             in1=mask_add[:, :], op0=ALU.add, op1=ALU.min, scale=-1.0,
                                             scalar=3.0e38, accum_out=s_max[:, u:u + 1]).then_inc(s_drained, 1)

            def y_copy(quad):
                dve.wait_ge(pv_done, b * NG + quad + 1)
                dve.tensor_copy(y_t[:, quad, :], banks[6 + quad % 2][:, :]).then_inc(y_drained, 1)

            scores(0)
            for g in range(TT * NG):
                if g + 1 < TT * NG:
                    scores(g + 1)
                for i in range(HG):
                    u = g * HG + i
                    dve.wait_ge(pt_full, b * UNITS + u + 1)
                    if g >= 2 * TT and g % TT == 0 and i == 0:
                        dve.wait_ge(pv_done, b * NG + g // TT - 1)
                    dve.tensor_copy(prob_t[:, (g // TT) % 2, i, :, (g % TT) * P:(g % TT + 1) * P],
                                    banks[4 + u % 2][:, :].rearrange("p (m n) -> p m n", m=TT)).then_inc(pt_ready, 1)
                if g % TT == 1 and g > TT:
                    y_copy(g // TT - 1)
            y_copy(NG - 1)
            dve.wait_ge(p_ready, (b + 1) * UNITS)
            dve.reciprocal(q_sum[:, :, :], q_sum[:, :, :]).then_inc(q_sum_ready, 1)
            dve.wait_ge(q_sum_ready, b + 1)
            for t in range(TT):
                dve.wait_ge(psum_full, st.full(b, "YT", t))
                dve.tensor_tensor(y[:, t, :].rearrange("p (h e) -> p h e", e=dh),
                                  bank_of("YT", t)[:, :].rearrange("p (h e) -> p h e", e=dh),
                                  q_sum[:, t, :].unsqueeze(2).broadcast_to([P, H, dh]), ALU.mult
                                  ).then_inc(drained["dve"], 1)
            dve.wait_ge(*wait_drained(b, "YT", TT - 1))

        with nc.Block() as block:

            @block.sync
            def _(sp):
                for j in range(2):
                    sp.sem_inc(x_stored[j], 16)
                sp.dma_start(cols[:, :], d["att_cols"][:, layer, :]).then_inc(const_loaded, 16)
                sp.dma_start(rows[:, :, :].rearrange("p r n -> p (r n)"),
                             d["att_rows"][layer:layer + 1, :].broadcast_to([P, 3 * D])).then_inc(const_loaded, 16)
                sp.dma_start(ident[:, :], d["ident"]).then_inc(const_loaded, 16)
                sp.dma_start(block_mask[:, :], d["block_masks"][:, 1 if dh == 64 else 0, :]).then_inc(const_loaded, 16)
                sp.dma_start(keep_in[:, :], d[f"mask{layer}_t"]).then_inc(const_loaded, 16)

                def load(b, j):
                    sp.dma_start(x[j][:, :, :], x_in[b].rearrange("(t p) n -> p t n", p=P)).then_inc(x_loaded[j], 16)
                    sp.dma_start(mask_in[j][:, :], d[f"mask{layer}"][b].broadcast_to([P, T])).then_inc(mask_loaded[j], 16)

                load(0, 0)
                for i in (1, 0, 2, 3):
                    sp.dma_start(w[i][:, :, :], d["att_w"][layer, i].rearrange("(k p) n -> p k n", p=P)
                                 ).then_inc(w_ready[i], 16)
                load(1, 1)

                def body(b, pair, j, more):
                    if more:
                        sp.wait_ge(xb_ready, b + 1)
                        sp.sem_inc(passed, 1)
                        sp.wait_ge(mask_ready, b + 2)
                        sp.sem_inc(passed, 1)
                        load(b + 2, j)
                    sp.wait_ge(out_ready, (b + 1) * TT)
                    sp.sem_inc(passed, 1)
                    sp.dma_start(x_out[b].rearrange("(t p) n -> p t n", p=P), out[j][:, :, :]
                                 ).then_inc(x_stored[j], 16)

                with sp.Fori(0, B // 2 - 1) as pair:
                    for j in range(2):
                        body(pair * 2 + j, pair, j, True)
                for j in range(2):
                    body(B - 2 + j, B // 2 - 1, j, False)
                for j in range(2):
                    sp.wait_ge(x_stored[j], B // 2 * 16 + 16)

            @block.gpsimd
            def _(pool):
                pool.memset(minus_half[:, :], -0.5).then_inc(half_ready, 1)
                pool.wait_ge(half_ready, 1)
                pool.wait_ge(const_loaded, 5 * 16)

                def norms(b, pair, j):
                    pool.wait_ge(mv_ready, (b + 1) * TT)
                    pool.sem_inc(passed, 1)
                    pool.tensor_scalar(rstd[:, :], mv[:, :, 1], EPS, 0.0, ALU.add, ALU.add).then_inc(var_ready, 1)
                    pool.wait_ge(var_ready, b + 1)
                    pool.tensor_tensor(rstd[:, :], rstd[:, :], minus_half[:, :], ALU.pow).then_inc(rstd_ready, 1)
                    pool.wait_ge(x_stored[j], pair * 16 + 16)
                    pool.sem_inc(passed, 1)
                    pool.wait_ge(xn_ready, (b + 1) * TT)
                    pool.tensor_tensor(out[j][:, :, :], x[j][:, :, :],
                                       rows[:, 2, :].unsqueeze(1).broadcast_to([P, TT, D]), ALU.add
                                       ).then_inc(xb_ready, 1)

                def body(b, pair, j, last):
                    if not last:
                        norms(b + 1, pair + j, 1 - j)
                    pool.wait_ge(y_mv_ready, (b + 1) * TT)
                    pool.sem_inc(passed, 1)
                    pool.tensor_scalar(y_rstd[:, :], y_mv[:, :, 1], EPS, 0.0, ALU.add, ALU.add).then_inc(y_var_ready, 1)
                    pool.wait_ge(y_var_ready, b + 1)
                    pool.tensor_tensor(y_rstd[:, :], y_rstd[:, :], minus_half[:, :], ALU.pow).then_inc(y_rstd_ready, 1)

                norms(0, 0, 0)
                batches(pool, body)

            @block.scalar
            def _(act):
                act.wait_ge(const_loaded, 5 * 16)
                col = lambda v, k: cols[:, v * DT + k:v * DT + k + 1]

                def drain(b, name, k, out, func, **kw):
                    act.wait_ge(psum_full, st.full(b, name, k))
                    act.activation(out, bank_of(name, k)[:, :], func, **kw).then_inc(drained["act"], 1)

                def next_norms(b):
                    for k in range(DT):
                        drain(b, "T", k, xn_t[:, k, :], ACT.Identity, scale=col(NW, k), bias=col(NB, k))

                def next_k(b):
                    for k in range(DT):
                        drain(b, "K", k, k_t[:, k, :], ACT.Identity, bias=col(BK, k))

                def next_q(b):
                    for k in range(DT):
                        drain(b, "Q", k, q_t[:, k, :], ACT.Identity, bias=col(BQ, k))

                def next_exps(b):
                    act.wait_ge(k_max_ready, 2 * (b + 2))
                    for k in range(DT):
                        act.activation(k_t[:, k, :], k_t[:, k, :], ACT.Exp, bias=k_max[:, k:k + 1],
                                       accum_out=k_sum[:, k:k + 1]).then_inc(k_exp_ready, 1)
                    for t in range(TT):
                        act.wait_ge(q_sub_ready, (b + 1) * TT + t + 1)
                        act.activation(q_tm[:, t, :], q_tm[:, t, :], ACT.Exp).then_inc(q_exp_ready, 1)

                def body(b, pair, j, last):
                    if linear:
                        for t in range(TT):
                            drain(b, "TK", t, k_tm[:, t, :], ACT.Copy)
                        for k in range(DT):
                            drain(b, "TQ", k, q_t[:, k, :], ACT.Copy)
                    else:
                        attention_act(act, b)
                    if last:
                        absent(st, act, drained["act"], "act", b, "T", 2)
                    else:
                        next_norms(b)
                        if not linear:
                            next_k(b)
                    for k in range(DT):
                        drain(b, "TY", k, h_t[:, k, :], ACT.Silu,
                              scale=mod_all["gain"][:, layer, k, bass.ds(b, 1)],
                              bias=mod_all["shift"][:, layer, k, bass.ds(b, 1)])
                    if last:
                        absent(st, act, drained["act"], "act", b, "Q", 1)
                    elif linear:
                        next_exps(b)
                    else:
                        next_q(b)

                first = [i[0] for i in plan].index("T")
                absent(st, act, drained["act"], "act", -1, plan[0][0], first)
                next_norms(-1)
                if not linear:
                    next_k(-1)
                absent(st, act, drained["act"], "act", -1, "TY", 1)
                if linear:
                    next_exps(-1)
                else:
                    next_q(-1)
                batches(act, body)

            @block.tensor
            def _(pe):
                pe.wait_ge(const_loaded, 5 * 16)
                wq, wk, wv, wo = w

                def next_k(b):
                    pe.wait_ge(xn_ready, (b + 2) * TT)
                    transposes(pe, b, "T", xn)
                    pe.wait_ge(*wait_drained(b, "T", DT - 1))
                    if isinstance(b, int) and b < 0:
                        pe.wait_ge(w_ready[1], 16)
                    project_t(pe, b, "K", wk)

                def next_q(b):
                    if linear:
                        project(pe, b, "Q", xn_t, wq)
                    else:
                        project_t(pe, b, "Q", wq)

                def body(b, pair, j, last):
                    project(pe, b, "V", xn_t, wv)
                    if linear:
                        pe.wait_ge(k_norm_ready if layer == 0 else k_exp_ready, (b + 1) * DT)
                        transposes(pe, b, "TK", k_t)
                        pe.wait_ge(q_exp_ready, (b + 1) * TT)
                        transposes(pe, b, "TQ", q_tm)
                        pe.wait_ge(v_ready, (b + 1) * TT)
                        pe.wait_ge(*wait_drained(b, "TK", TT - 1))
                        for g in range(DT):
                            wait_bank(pe, b, "A", g)
                            for t in range(TT):
                                k_part, v_part = (i[:, t, g * P:(g + 1) * P] for i in (k_tm, v_tm))
                                lhs_t, rhs = (v_part, k_part) if layer == 0 else (k_part, v_part)
                                last_ins = pe.matmul(bank_of("A", g)[:, 0:P], lhs_t, rhs, start=(t == 0),
                                                     stop=(t == TT - 1))
                            last_ins.then_inc(psum_full, 1)
                        pe.wait_ge(*wait_drained(b, "A", DT - 1))
                        pe.wait_ge(*wait_drained(b, "TQ", DT - 1))
                        for t in range(TT):
                            wait_bank(pe, b, "Y", t)
                            for g in range(DT):
                                last_ins = pe.matmul(bank_of("Y", t)[:, g * P:(g + 1) * P],
                                                     q_t[:, g, t * P:(t + 1) * P], attn[:, g, :],
                                                     start=True, stop=True)
                            last_ins.then_inc(psum_full, 1)
                    else:
                        attention_pe(pe, b)
                    if last:
                        absent(st, pe, psum_full, "pe", b, "T", 2)
                    else:
                        next_k(b)
                    pe.wait_ge(yn_ready, (b + 1) * TT)
                    transposes(pe, b, "TY", y)
                    if last:
                        absent(st, pe, psum_full, "pe", b, "Q", 1)
                    else:
                        next_q(b)
                    pe.wait_ge(*wait_drained(b, "TY", DT - 1))
                    project(pe, b, "O", h_t, wo)

                first = [i[0] for i in plan].index("T")
                absent(st, pe, psum_full, "pe", -1, plan[0][0], first)
                next_k(-1)
                absent(st, pe, psum_full, "pe", -1, "TY", 1)
                pe.wait_ge(w_ready[0], 16)
                next_q(-1)
                absent(st, pe, psum_full, "pe", -1, "O", 1)
                for i in (2, 3):
                    pe.wait_ge(w_ready[i], 16)
                batches(pe, body)

            @block.vector
            def _(dve):
                dve.sem_inc(mask_ready, 1)
                dve.wait_ge(const_loaded, 5 * 16)
                if layer == 0:
                    dve.tensor_scalar(keep[:, :], keep_in[:, :], 1.0, None, ALU.not_equal).then_inc(const_ready, 1)
                else:
                    dve.tensor_copy(keep[:, :], keep_in[:, :]).then_inc(const_ready, 1)
                dve.wait_ge(const_ready, 1)
                col = lambda v, k: cols[:, v * DT + k:v * DT + k + 1]

                def norm_stats(b, src, out, agg, stats_sem, agg_sem):
                    for t in range(TT):
                        dve.bn_stats(out[:, t, :], src[:, t, :]).then_inc(stats_sem, 1)
                    for t in range(TT):
                        dve.wait_ge(stats_sem, b * TT + t + 1)
                        dve.sem_inc(passed, 1)
                        dve.bn_aggr(agg[:, t, :], out[:, t, :]).then_inc(agg_sem, 1)

                def mask(b, pair, j):
                    dve.wait_ge(mask_loaded[j], pair * 16 + 16)
                    if layer == 0:
                        dve.tensor_scalar(mask_add[:, :], mask_in[j][:, :], 1.0, NEG, ALU.is_equal, ALU.mult
                                          ).then_inc(mask_ready, 1)
                    else:
                        dve.tensor_scalar(mask_add[:, :], mask_in[j][:, :], 1.0, 1.0e6, ALU.subtract, ALU.mult
                                          ).then_inc(mask_ready, 1)

                def norms(b, pair, j):
                    if linear:
                        mask(b, pair, j)
                    dve.wait_ge(x_loaded[j], pair * 16 + 16)
                    norm_stats(b, x[j], stats, mv, stats_ready, mv_ready)
                    dve.wait_ge(rstd_ready, b + 1)
                    if not isinstance(b, int) or b > 0:
                        dve.wait_ge(psum_full, st.full(b - 2, "T", DT - 1))
                    for t in range(TT):
                        dve.tensor_scalar(xn[:, t, :], x[j][:, t, :], mv[:, t, 0:1], rstd[:, t:t + 1],
                                          ALU.subtract, ALU.mult).then_inc(xn_ready, 1)

                def next_k(b):
                    dve.wait_ge(mask_ready, b + 3)
                    for k in range(DT):
                        dve.wait_ge(psum_full, st.full(b, "K", k))
                        dve.scalar_tensor_tensor(k_t[:, k, :], bank_of("K", k)[:, :], col(BK, k), mask_add[:, :],
                                                 ALU.add, ALU.add).then_inc(drained["dve"], 1)
                        dve.wait_ge(*wait_drained(b, "K", k))
                        last = dve.reduce_max(k_max[:, k:k + 1], k_t[:, k, :], AX.X)
                    last.then_inc(k_max_ready, 1)
                    dve.wait_ge(k_max_ready, 2 * b + 3)
                    dve.tensor_scalar(k_max[:, :], k_max[:, :], -1.0, None, ALU.mult).then_inc(k_max_ready, 1)

                def next_q(b):
                    for t in range(TT):
                        dve.wait_ge(psum_full, st.full(b, "Q", t))
                        dve.tensor_tensor(q_tm[:, t, :], bank_of("Q", t)[:, :], rows[:, 0, :], ALU.add
                                          ).then_inc(drained["dve"], 1)
                        dve.wait_ge(*wait_drained(b, "Q", t))
                        heads = q_tm[:, t, :].rearrange("p (h e) -> p h e", e=dh)
                        dve.tensor_reduce(q_max[:, t, :], heads, AX.X, ALU.max).then_inc(q_max_ready, 1)
                        dve.wait_ge(q_max_ready, (b + 1) * TT + t + 1)
                        dve.tensor_tensor(heads, heads, q_max[:, t, :].unsqueeze(2).broadcast_to([P, H, dh]),
                                          ALU.subtract).then_inc(q_sub_ready, 1)

                def body(b, pair, j, last):
                    if not linear:
                        mask(b, pair, j)
                    if not last:
                        norms(b + 1, pair + j, 1 - j)
                    if linear:
                        dve.wait_ge(k_exp_ready, (b + 1) * DT)
                        dve.reciprocal(k_sum[:, :], k_sum[:, :]).then_inc(rk_ready, 1)
                        dve.wait_ge(rk_ready, b + 1)
                        if layer == 0:
                            for k in range(DT):
                                dve.tensor_scalar(k_t[:, k, :], k_t[:, k, :], k_sum[:, k:k + 1], None, ALU.mult
                                                  ).then_inc(k_norm_ready, 1)
                    for t in range(TT):
                        dve.wait_ge(psum_full, st.full(b, "V", t))
                        dve.tensor_tensor(v_tm[:, t, :], bank_of("V", t)[:, :], rows[:, 1, :], ALU.add
                                          ).then_inc(drained["dve"], 1)
                        dve.wait_ge(*wait_drained(b, "V", t))
                        dve.tensor_scalar(v_tm[:, t, :], v_tm[:, t, :], keep[:, bass.ds(b * TT + t, 1)], None, ALU.mult
                                          ).then_inc(v_ready, 1)
                    if linear:
                        for t in range(TT):
                            dve.wait_ge(q_exp_ready, b * TT + t + 1)
                            last_ins = dve.reduce_sum(q_sum[:, t, :], q_tm[:, t, :].rearrange("p (h e) -> p h e", e=dh),
                                                      AX.X)
                        last_ins.then_inc(q_sum_ready, 1)
                        dve.wait_ge(q_sum_ready, 2 * b + 1)
                        dve.reciprocal(q_sum[:, :, :], q_sum[:, :, :]).then_inc(q_sum_ready, 1)
                        for g in range(DT):
                            dve.wait_ge(psum_full, st.full(b, "A", g))
                            if layer == 0:
                                ins = dve.tensor_tensor(attn[:, g, :], bank_of("A", g)[:, 0:P], block_mask[:, :],
                                                        ALU.mult)
                            else:
                                ins = dve.scalar_tensor_tensor(attn[:, g, :], bank_of("A", g)[:, 0:P],
                                                               k_sum[:, g:g + 1], block_mask[:, :], ALU.mult, ALU.mult)
                            ins.then_inc(drained["dve"], 1)
                        dve.wait_ge(q_sum_ready, 2 * b + 2)
                        for t in range(TT):
                            dve.wait_ge(psum_full, st.full(b, "Y", t))
                            dve.tensor_tensor(y[:, t, :].rearrange("p (h e) -> p h e", e=dh),
                                              bank_of("Y", t)[:, :].rearrange("p (h e) -> p h e", e=dh),
                                              q_sum[:, t, :].unsqueeze(2).broadcast_to([P, H, dh]), ALU.mult
                                              ).then_inc(drained["dve"], 1)
                        dve.wait_ge(*wait_drained(b, "Y", TT - 1))
                    else:
                        dve.wait_ge(mask_ready, b + 2)
                        attention_dve(dve, b)
                    norm_stats(b, y, y_stats, y_mv, y_stats_ready, y_mv_ready)
                    dve.wait_ge(y_rstd_ready, b + 1)
                    for t in range(TT):
                        dve.tensor_scalar(y[:, t, :], y[:, t, :], y_mv[:, t, 0:1], y_rstd[:, t:t + 1],
                                          ALU.subtract, ALU.mult).then_inc(yn_ready, 1)
                    if last:
                        absent(st, dve, drained["dve"], "dve", b, "T", 2)
                        absent(st, dve, drained["dve"], "dve", b, "Q", 1)
                    elif linear:
                        next_k(b)
                        next_q(b)
                    dve.wait_ge(xb_ready, b + 1)
                    for t in range(TT):
                        dve.wait_ge(psum_full, st.full(b, "O", t))
                        dve.tensor_tensor(out[j][:, t, :], bank_of("O", t)[:, :], out[j][:, t, :], ALU.add
                                          ).then_inc(drained["dve"], 1)
                    dve.wait_ge(*wait_drained(b, "O", TT - 1))
                    dve.sem_inc(out_ready, TT)

                first = [i[0] for i in plan].index("T")
                absent(st, dve, drained["dve"], "dve", -1, plan[0][0], first)
                norms(0, 0, 0)
                if linear:
                    next_k(-1)
                    next_q(-1)
                absent(st, dve, drained["dve"], "dve", -1, "O", 1)
                batches(dve, body)


def ssm_layer(nc, sems, d, mod_all, banks, x_in, x_out):
    PARTS = 4
    plan = []
    for p in range(PARTS):
        plan += [(f"Z1{p}", 2, "act"), (f"O{p}", 1, "dve")]
    plan += [("Y00", 4, "dve"), ("MX", ET, "act"), ("DBC1", 1, "dve"), ("Y01", 4, "dve"), ("TC1", 1, "dve"),
             ("T", DT, "act"), ("DL1", ET, "dve"), ("Y10", 4, "dve"), ("Z0", ET, "act"),
             ("DBC0", 1, "dve"), ("Y11", 4, "dve"), ("TC0", 1, "dve"), ("DL0", ET, "dve")]
    st = Stages(plan)
    RING = 2

    def bank_of(name, k):
        return banks[6 if name[:2] == "Z1" else 7 if name[0] == "O" else 6 + (st.first[name] + k) % RING]

    GE = 4
    UNITS = 4
    STEPS = UNITS * N
    CH = 2
    SPARE = 3
    SCANNED = 2 + GE
    BUILT = {"Z1": 0, "MX": 1, "Z0": 2}
    with ExitStack() as ctx:
        sb = lambda n, s, t=F32: ctx.enter_context(nc.sbuf_tensor("ssm_" + n, s, t))
        sem = lambda n: sems.take("ssm_" + n)
        ident = sb("ident", [P, P])
        w_ring = [sb(f"w_ring{i}", [P, DT, P]) for i in range(2)]
        w_out = sb("w_out", [P, ET, D])
        w_dbc = sb("w_dbc", [P, 2, ET, R + 2 * N])
        w_dt = sb("w_dt", [R, 2, E])
        neg_a = sb("neg_a", [P, 2, ET, N])
        bf_row = sb("bf_row", [P, D])
        ada = sb("ada", [P, 3, D])
        gate = sb("gate", [P, D])
        minus_half = sb("minus_half", [P, TT])
        work = sb("work", [P, 4, 4, 512])
        d_bu = [work[:, i] for i in range(2)]
        state = [work[:, 2 + i] for i in range(2)]
        skip, xs, xn = work[:, 0], work[:, 1], work[:, 2]
        x = sb("x", [P, TT, D])
        xn_t = sb("xn_t", [P, DT, T])
        z = [sb(f"z{s}", [P, ET, T]) for s in range(2)]
        delta = sb("delta", [P, ET, T])
        soft = sb("soft", [P, 2, T])
        decay = [banks[e] if e < 2 else sb(f"decay{e}", [P, T]) for e in range(GE)]
        mx = sb("mx", [P, ET, T])
        y_sum = sb("y_sum", [P, ET, T])
        acc = sb("acc", [P, TT, GE * P])
        b_rows = sb("b_rows", [P, 2, CH, T])
        dbc_t = sb("dbc_t", [R + 2 * N, T])
        dbc_tm = sb("dbc_tm", [P, TT, R + 2 * N])
        stats = sb("stats", [P, TT, 6])
        mv = sb("mv", [P, TT, 2])
        rstd = sb("rstd", [P, TT])
        stats2 = sb("stats2", [P, TT, 6])
        mv2 = sb("mv2", [P, TT, 2])
        rstd2 = sb("rstd2", [P, TT])
        cols = mod_all["ssm_cols"]
        bzc = mod_all["bzc"]

        w_loaded, const_ready, passed = sem("w_loaded"), sem("const_ready"), sem("passed")
        half_ready, w_out_loaded = sem("half_ready"), sem("w_out_loaded")
        x_loaded, x_stored, ada_loaded, gate_loaded = sem("x_loaded"), sem("x_stored"), sem("ada_loaded"), sem("gate_loaded")
        resid_stored, resid_loaded = sem("resid_stored"), sem("resid_loaded")
        ring_loaded = [sem(f"ring_loaded{i}") for i in range(2)]
        full = sem("full")
        drained = {"act": sem("act_drained"), "dve": sem("dve_drained")}
        stats_ready, mv_ready, var_ready, rstd_ready = sem("stats_ready"), sem("mv_ready"), sem("var_ready"), sem("rstd_ready")
        stats2_ready, mv2_ready, var2_ready, rstd2_ready = sem("stats2_ready"), sem("mv2_ready"), sem("var2_ready"), sem("rstd2_ready")
        xn_ready, xs_ready, xn2_ready, resid_ready = sem("xn_ready"), sem("xs_ready"), sem("xn2_ready"), sem("resid_ready")
        soft_in, soft_out, delta_ready, du_ready = sem("soft_in"), sem("soft_out"), sem("delta_ready"), sem("du_ready")
        u_used = [sem(f"u_used{s}") for s in range(2)]
        b_stored = sem("b_stored")
        b_loaded = [sem(f"b_loaded{i}") for i in range(2)]
        da_ready, dbu_ready, scanned, turned, added = sem("da_ready"), sem("dbu_ready"), sem("scanned"), sem("turned"), sem("added")
        silu_ready, gated, out_ready = sem("silu_ready"), sem("gated"), sem("out_ready")

        def wait_drained(b, name, k):
            engine, count = st.drained(b, name, k)
            return drained[engine], count

        def ring_count(b, name, i):
            return (b * 12 + (BUILT[name] * 4 + 4) + i + 1) * 16

        def batches(eng, before, body, after):
            before()
            body(0, True, False)
            with eng.Fori(1, B - 1) as b:
                body(b, False, False)
            body(B - 1, False, True)
            after()

        def around_front(eng, name, by, norms, columns, deltas):
            absent(st, eng, name, by, -1, "Z10", 13)
            norms()
            absent(st, eng, name, by, -1, "DL1", 2)
            columns()
            deltas(-1, lambda: absent(st, eng, name, by, -1, "Y11", 1))

        with nc.Block() as block:

            @block.sync
            def _(sp):
                sp.dma_start(ident[:, :], d["ident"]).then_inc(w_loaded, 16)
                sp.dma_start(w_dbc[:, :, :, :], d["wdbcT"].rearrange("s (k p) n -> p s k n", p=P)).then_inc(w_loaded, 16)
                sp.dma_start(w_dt[:, :, :], d["wdtT"].rearrange("s r n -> r s n")).then_inc(w_loaded, 16)
                sp.dma_start(neg_a[:, :, :, :].rearrange("p s k n -> p (s k n)"), d["alog"]).then_inc(w_loaded, 16)
                sp.dma_start(bf_row[:, :], d["bf_row"].broadcast_to([P, D])).then_inc(w_loaded, 16)

                def load_x(b):
                    sp.dma_start(x[:, :, :], x_in[b].rearrange("(t p) n -> p t n", p=P)).then_inc(x_loaded, 16)
                    sp.dma_start(ada[:, :, :].rearrange("p r n -> p (r n)"),
                                 d["ada_d"][bass.ds(b, 1), :].broadcast_to([P, 3 * D])).then_inc(ada_loaded, 16)

                def store_resid(b):
                    sp.wait_ge(resid_ready, (b + 1) * 3)
                    sp.sem_inc(passed, 1)
                    sp.dma_start(d["resid_d"][b].rearrange("(t p) n -> p t n", p=P), x[:, :, :]
                                 ).then_inc(resid_stored, 16)

                def store_b(b, s, count):
                    sp.wait_ge(*wait_drained(b, f"DBC{s}", 0))
                    sp.sem_inc(passed, 1)
                    sp.dma_start(d["b_d"][s], dbc_t[R:R + N, :]).then_inc(b_stored, 16)
                    sp.wait_ge(b_stored, count)
                    sp.sem_inc(passed, 1)

                def unit(b, s, g, between=None):
                    def part(i):
                        for j in range(2):
                            c = i * 2 + j
                            sp.wait_ge(dbu_ready, b * STEPS + (s * 2 + g) * N + (c - 1) * CH + SPARE)
                            sp.sem_inc(passed, 1)
                            columns = slice(c * CH * T, (c + 1) * CH * T) if isinstance(c, int) else bass.ds(c * CH * T, CH * T)
                            sp.dma_start(b_rows[:, j, :, :].rearrange("p c n -> p (c n)"),
                                         d["b_flat"][s:s + 1, columns].broadcast_to([P, CH * T])
                                         ).then_inc(b_loaded[j], 16)

                    if between:
                        part(0)
                        between()
                    with sp.Fori(1 if between else 0, PARTS) as i:
                        part(i)

                def store_out(b):
                    sp.wait_ge(out_ready, (b + 1) * TT)
                    sp.sem_inc(passed, 1)
                    sp.dma_start(x_out[b].rearrange("(t p) n -> p t n", p=P), x[:, :, :]).then_inc(x_stored, 16)
                    sp.wait_ge(x_stored, (b + 1) * 16)
                    sp.sem_inc(passed, 1)

                def before():
                    load_x(0)
                    sp.dma_start(w_out[:, :, :], d["wfT"].rearrange("(k p) n -> p k n", p=P)).then_inc(w_out_loaded, 16)
                    store_resid(0)
                    store_b(-1, 0, 16)

                def body(b, first, last):
                    def turn_over():
                        if not first:
                            store_out(b - 1)
                        if not last:
                            sp.wait_ge(resid_stored, (b + 1) * 16)
                            sp.sem_inc(passed, 1)
                            load_x(b + 1)
                        sp.dma_start(gate[:, :], d["ada_d"][bass.ds(b, 1), 2 * D:3 * D].broadcast_to([P, D])
                                     ).then_inc(gate_loaded, 16)

                    unit(b, 0, 0)
                    unit(b, 0, 1, turn_over)
                    store_b(b, 1, b * 32 + 32)
                    if not last:
                        store_resid(b + 1)
                    unit(b, 1, 0)
                    sp.wait_ge(resid_stored, (b + 1 if last else b + 2) * 16)
                    sp.sem_inc(passed, 1)
                    sp.dma_start(x[:, :, :], d["resid_d"][b].rearrange("(t p) n -> p t n", p=P)).then_inc(resid_loaded, 16)
                    unit(b, 1, 1)
                    if not last:
                        store_b(b, 0, b * 32 + 48)

                batches(sp, before, body, lambda: store_out(B - 1))

            @block.gpsimd
            def _(pool):
                pool.sem_inc(dbu_ready, SPARE)
                pool.memset(minus_half[:, :], -0.5).then_inc(half_ready, 1)
                pool.wait_ge(half_ready, 1)
                pool.wait_ge(w_loaded, 5 * 16)

                def rsqrt(b, agg, out, agg_sem, var_sem, out_sem):
                    pool.wait_ge(agg_sem, (b + 1) * TT)
                    pool.sem_inc(passed, 1)
                    pool.tensor_scalar(out[:, :], agg[:, :, 1], EPS, 0.0, ALU.add, ALU.add).then_inc(var_sem, 1)
                    pool.wait_ge(var_sem, b + 1)
                    pool.tensor_tensor(out[:, :], out[:, :], minus_half[:, :], ALU.pow).then_inc(out_sem, 1)

                def norms(b):
                    rsqrt(b, mv, rstd, mv_ready, var_ready, rstd_ready)
                    rsqrt(b, mv2, rstd2, mv2_ready, var2_ready, rstd2_ready)
                    rows = lambda row: row.unsqueeze(1).broadcast_to([P, TT, D])
                    pool.tensor_tensor(skip, xs, rows(bf_row[:, :]), ALU.add).then_inc(resid_ready, 1)
                    pool.wait_ge(resid_ready, b * 3 + 1)
                    pool.tensor_tensor(skip, skip, rows(ada[:, 2, :]), ALU.mult).then_inc(resid_ready, 1)
                    pool.wait_ge(resid_ready, b * 3 + 2)
                    pool.wait_ge(xn_ready, (b + 1) * TT)
                    pool.tensor_tensor(x[:, :, :], skip, x[:, :, :], ALU.add).then_inc(resid_ready, 1)

                def direction(b, s):
                    for g in range(2):
                        for m in range(g * GE, (g + 1) * GE):
                            pool.wait_ge(delta_ready, (b * 2 + s) * ET + m + 1)
                            pool.wait_ge(u_used[s], b * ET + m + 1)
                            pool.tensor_tensor(z[s][:, m, :], z[s][:, m, :], delta[:, m, :], ALU.mult).then_inc(du_ready, 1)
                        pool.wait_ge(du_ready, (b * 2 + s) * ET + (g + 1) * GE)
                        pool.sem_inc(passed, 1)
                        with pool.Fori(0, PARTS) as i:
                            for j in range(2):
                                chunk = b * (STEPS // CH // 2) + (s * 2 + g) * PARTS + i
                                pool.wait_ge(b_loaded[j], (chunk + 1) * 16)
                                for k in range(CH):
                                    step = b * STEPS + (s * 2 + g) * N + i * 4 + (2 * j + k)
                                    pool.wait_ge(scanned, SCANNED + (step - 1) * GE)
                                    pool.tensor_tensor(d_bu[k], z[s][:, g * GE:(g + 1) * GE, :],
                                                       b_rows[:, j, k, :].unsqueeze(1).broadcast_to([P, GE, T]),
                                                       ALU.mult).then_inc(dbu_ready, 1)

                def body(b, first, last):
                    pool.wait_ge(resid_ready, (b + 1) * 3)
                    pool.wait_ge(full, st.full(b - 1, "T", DT - 1))
                    direction(b, 0)
                    if not last:
                        pool.wait_ge(x_loaded, (b + 2) * 16)
                        norms(b + 1)
                        pool.wait_ge(resid_ready, (b + 2) * 3)
                        pool.wait_ge(full, st.full(b, "T", DT - 1))
                    direction(b, 1)

                def before():
                    norms(0)

                batches(pool, before, body, lambda: None)

            @block.scalar
            def _(act):
                act.wait_ge(w_loaded, 5 * 16)
                flat = neg_a[:, :, :, :].rearrange("p s k n -> p (s k n)")
                act.activation(flat, flat, ACT.Exp).then_inc(const_ready, 1)
                act.wait_ge(const_ready, 1)
                act.activation(flat, flat, ACT.Copy, scale=-1.0).then_inc(const_ready, 1)
                act.wait_ge(const_ready, 2)

                def drain(b, name, k, out, func, bank=None, **kw):
                    act.wait_ge(full, st.full(b, name, k))
                    act.activation(out, bank_of(name, k if bank is None else bank)[:, :], func, **kw
                                   ).then_inc(drained["act"], 1)

                def load_ring(name, m, j):
                    src = {"Z0": d["wzc"][0], "Z1": d["wzc"][1], "MX": d["wxT"]}[name]
                    part = slice(m * P, (m + 1) * P) if isinstance(m, int) else bass.ds(m * P, P)
                    act.dma_start(w_ring[j][:, :, :], src[:, part].rearrange("(k p) n -> p k n", p=P)
                                  ).then_inc(ring_loaded[j], 16)

                def drain_tile(b, name, m, j, following):
                    one = (lambda t, at: t[:, at:at + 1]) if isinstance(m, int) else (lambda t, at: t[:, bass.ds(at, 1)])
                    tile = (lambda t: t[:, m, :]) if isinstance(m, int) else (
                        lambda t: t[:, bass.ds(m, 1), :].rearrange("p o n -> p (o n)"))
                    out = tile({"Z0": z[0], "Z1": z[1], "MX": mx}[name])
                    bias = one(cols, m + BX) if name == "MX" else one(bzc, m + (0 if name == "Z0" else ET))
                    if name == "Z1":
                        drain(b, f"Z1{m // 2}", j, out, ACT.Identity, bias=bias)
                    else:
                        drain(b, name, m, out, ACT.Identity, bank=j, bias=bias)
                    if not isinstance(m, int) or m + 2 < ET:
                        load_ring(name, m + 2, j)
                    elif following:
                        load_ring(following, j, j)

                def norms(b):
                    for k in range(DT):
                        drain(b, "T", k, xn_t[:, k, :], ACT.Identity, scale=cols[:, G2 + k:G2 + k + 1],
                              bias=cols[:, B2 + k:B2 + k + 1])

                def softplus(index, direct=False):
                    for m in range(ET):
                        i = index * ET + m
                        act.wait_ge(soft_in, i + 1)
                        act.activation(soft[:, m % 2, :], soft[:, m % 2, :], ACT.Exp).then_inc(soft_out, 1)
                        act.wait_ge(soft_out, 2 * i + 1)
                        act.activation(soft[:, m % 2, :], soft[:, m % 2, :], ACT.Ln, bias=1.0).then_inc(soft_out, 1)
                        if direct:
                            act.activation(y_sum[:, m, :], z[0][:, m, :], ACT.Copy,
                                           scale=cols[:, DPC + m:DPC + m + 1]).then_inc(u_used[0], 1)

                def unit(b, s, g, name, following=None):
                    def part(i):
                        for j in range(2):
                            for r in range(2):
                                n = i * 4 + (2 * j + r)
                                rate = slice(n, n + 1) if isinstance(n, int) else bass.ds(n, 1)
                                for e in range(GE):
                                    at = (b * STEPS + (s * 2 + g) * N + n) * GE + e
                                    act.wait_ge(scanned, SCANNED - GE + at + 1)
                                    act.activation(decay[e][:, :], delta[:, g * GE + e, :], ACT.Exp,
                                                   scale=neg_a[:, s, g * GE + e, rate]).then_inc(da_ready, 1)
                            if name:
                                drain_tile(b, name, i * 2 + j, j, following)

                    act.wait_ge(delta_ready, (b * 2 + s + 1) * ET)
                    if name == "Z1":
                        for p in range(PARTS):
                            part(p)
                    elif name:
                        with act.Fori(0, PARTS - 1) as i:
                            part(i)
                        part(PARTS - 1)
                    else:
                        with act.Fori(0, PARTS) as i:
                            part(i)

                def deltas(b, sums):
                    sums()
                    if not isinstance(b, int) or b >= 0:
                        act.wait_ge(gated, (b + 1) * ET)
                    act.wait_ge(*wait_drained(b, "Z0", ET - 1))
                    softplus((b + 1) * 2, direct=True)

                def before():
                    for j in range(2):
                        load_ring("Z0", j, j)
                    around_front(act, drained["act"], "act", lambda: norms(-1),
                                 lambda: [drain_tile(-1, "Z0", m, m % 2, "Z1") for m in range(ET)], deltas)

                def body(b, first, last):
                    act.wait_ge(dbu_ready, SPARE + b * STEPS)
                    unit(b, 0, 0, "Z1", "MX")
                    act.wait_ge(full, st.full(b, "Y00", 0))
                    unit(b, 0, 1, "MX", None if last else "Z0")
                    act.wait_ge(*wait_drained(b, "MX", ET - 1))
                    for m in range(ET):
                        act.activation(mx[:, m, :], mx[:, m, :], ACT.Silu).then_inc(silu_ready, 1)
                    act.preload_act_table_set("natural_log_exp_and_others")
                    if last:
                        absent(st, act, drained["act"], "act", b, "T", 1)
                    else:
                        norms(b)
                    softplus(b * 2 + 1)
                    unit(b, 1, 0, None)
                    if last:
                        absent(st, act, drained["act"], "act", b, "Z0", 1)
                        unit(b, 1, 1, None)
                    else:
                        unit(b, 1, 1, "Z0", "Z1")
                        deltas(b, lambda: None)

                act.preload_act_table_set("natural_log_exp_and_others")
                batches(act, before, body, lambda: None)

            @block.tensor
            def _(pe):
                pe.sem_inc(turned, 1)
                pe.wait_ge(w_loaded, 5 * 16)

                def wait_bank(b, name, k):
                    engine, count = st.before(b, name, k, RING)
                    pe.wait_ge(drained[engine], count)

                def products(b, name, k, pairs, rows_out=P):
                    wait_bank(b, name, k)
                    for i, (lhs_t, rhs) in enumerate(pairs):
                        last = pe.matmul(bank_of(name, k)[0:rows_out, :], lhs_t, rhs, start=(i == 0),
                                         stop=(i == len(pairs) - 1))
                    last.then_inc(full, 1)

                def norms(b):
                    pe.wait_ge(xn2_ready, (b + 2) * TT)
                    for k in range(DT):
                        wait_bank(b, "T", k)
                        for t in range(TT):
                            last = pe.transpose(bank_of("T", k)[:, t * P:(t + 1) * P], xn[:, t, k * P:(k + 1) * P], ident[:, :])
                        last.then_inc(full, 1)

                def dbc(b, s):
                    products(b, f"DBC{s}", 0, [(w_dbc[:, s, k, :], z[s][:, k, :]) for k in range(ET)], R + 2 * N)

                def dbc_turned(b, s):
                    pe.wait_ge(*wait_drained(b, f"DBC{s}", 0))
                    wait_bank(b, f"TC{s}", 0)
                    for t in range(TT):
                        last = pe.transpose(bank_of(f"TC{s}", 0)[:, t * 96:(t + 1) * 96],
                                            dbc_t[:, t * P:(t + 1) * P], ident[0:96, 0:96])
                    last.then_inc(full, 1)

                def dl(b, s):
                    for m in range(ET):
                        products(b, f"DL{s}", m, [(w_dt[:, s, m * P:(m + 1) * P], dbc_t[0:R, :])])

                def tile(b, name, i, j):
                    pe.wait_ge(ring_loaded[j], ring_count(b, name, i))
                    for k in range(DT):
                        last = pe.matmul(bank_of(f"Z1{i}" if name == "Z1" else name, j)[:, :], w_ring[j][:, k, :],
                                         xn_t[:, k, :], start=(k == 0), stop=(k == DT - 1))
                    last.then_inc(full, 1)

                def output(b, t, quarters=range(4)):
                    for k in [2 * q + i for q in quarters for i in range(2)]:
                        last = pe.matmul(bank_of(f"O{t}", 0)[:, :], mx[:, k, t * P:(t + 1) * P], w_out[:, k, :],
                                         start=(k == 0), stop=(k == ET - 1))
                    if 3 in quarters:
                        last.then_inc(full, 1)

                def unit(b, s, g, name, first=False):
                    def turn(i, j, with_output=False):
                        for r in range(2):
                            step = b * STEPS + (s * 2 + g) * N + i * 4 + (2 * j + r)
                            pe.wait_ge(scanned, SCANNED + (step + 1) * GE)
                            for t in range(TT):
                                pe.wait_ge(added, step * TT + t + 1)
                                for e in range(GE):
                                    last = pe.transpose(banks[2 + t][:, e * P:(e + 1) * P],
                                                        state[r][:, e, t * P:(t + 1) * P], ident[:, :])
                                last.then_inc(turned, 1)
                            if with_output:
                                if (i, j, r) == (0, 0, 0):
                                    pe.wait_ge(gated, b * ET)
                                elif j == r == 0:
                                    pe.wait_ge(*wait_drained(b, f"O{i - 1}", 0))
                                output(b, i, [2 * j + r])

                    if name == "Z1":
                        pe.wait_ge(*wait_drained(b - 1, "DL0", ET - 1))
                        for p in range(PARTS):
                            for j in range(2):
                                if 2 * p + j > 0:
                                    pe.wait_ge(*wait_drained(b, f"Z1{p if j else p - 1}", 1 - j))
                                tile(b, "Z1", p, j)
                                turn(p, j, not first)
                            if first:
                                absent(st, pe, full, "pe", b, f"O{p}", 1)
                        return
                    if name:
                        for k in range(RING):
                            wait_bank(b, name, k)
                        pe.sem_inc(passed, 1)
                        base = st.drained(b, name, 0)[1]
                    with pe.Fori(0, PARTS) as i:
                        for j in range(2):
                            if name:
                                pe.wait_ge(drained["act"], base + i * 2 + (j - 2))
                                tile(b, name, i, j)
                            turn(i, j)

                def sums(b, s, g):
                    pe.wait_ge(added, (b * STEPS + (s * 2 + g + 1) * N) * TT + TT)
                    for e in range(GE):
                        wait_bank(b, f"Y{s}{g}", e)
                        for t in range(TT):
                            last = pe.transpose(bank_of(f"Y{s}{g}", e)[:, t * P:(t + 1) * P],
                                                acc[:, t, e * P:(e + 1) * P], ident[:, :])
                        last.then_inc(full, 1)

                def first_columns():
                    pe.wait_ge(*wait_drained(-1, "T", DT - 1))
                    for m in range(ET):
                        wait_bank(-1, "Z0", m)
                        tile(-1, "Z0", m // 2, m % 2)

                def deltas(b, sums):
                    pe.wait_ge(*wait_drained(b, "Z0", ET - 1))
                    dbc(b, 0)
                    sums()
                    dbc_turned(b, 0)
                    dl(b, 0)

                def before():
                    around_front(pe, full, "pe", lambda: norms(-1), first_columns, deltas)
                    pe.wait_ge(w_out_loaded, 16)

                def body(b, first, last):
                    unit(b, 0, 0, "Z1", first)
                    sums(b, 0, 0)
                    unit(b, 0, 1, "MX")
                    pe.wait_ge(*wait_drained(b, f"Z1{PARTS - 1}", 1))
                    dbc(b, 1)
                    sums(b, 0, 1)
                    dbc_turned(b, 1)
                    if last:
                        absent(st, pe, full, "pe", b, "T", 1)
                        pe.wait_ge(*wait_drained(b, "TC1", 0))
                    else:
                        norms(b)
                    dl(b, 1)
                    if not last:
                        pe.wait_ge(*wait_drained(b, "T", DT - 1))
                        pe.sem_inc(passed, 1)
                    unit(b, 1, 0, None)
                    sums(b, 1, 0)
                    if last:
                        pe.wait_ge(*wait_drained(b, "Y10", GE - 1))
                        unit(b, 1, 1, None)
                        absent(st, pe, full, "pe", b, "Z0", 2)
                        sums(b, 1, 1)
                        absent(st, pe, full, "pe", b, "TC0", 2)
                    else:
                        unit(b, 1, 1, "Z0")
                        deltas(b, lambda: sums(b, 1, 1))

                def after():
                    pe.wait_ge(gated, B * ET)
                    for t in range(TT):
                        absent(st, pe, full, "pe", B, f"Z1{t}", 1)
                        if t > 0:
                            pe.wait_ge(*wait_drained(B, f"O{t - 1}", 0))
                        output(B, t)

                batches(pe, before, body, after)

            @block.vector
            def _(dve):
                dve.sem_inc(added, TT)
                dve.sem_inc(scanned, SCANNED)
                dve.wait_ge(w_loaded, 5 * 16)
                dve.wait_ge(const_ready, 2)

                def norms(b, between=lambda: None):
                    dve.wait_ge(x_loaded, b * 16 + 16)
                    dve.wait_ge(ada_loaded, b * 16 + 16)
                    for t in range(TT):
                        dve.bn_stats(stats[:, t, :], x[:, t, :]).then_inc(stats_ready, 1)
                    for t in range(TT):
                        dve.wait_ge(stats_ready, b * TT + t + 1)
                        dve.sem_inc(passed, 1)
                        dve.bn_aggr(mv[:, t, :], stats[:, t, :]).then_inc(mv_ready, 1)
                    dve.wait_ge(rstd_ready, b + 1)
                    for t in range(TT):
                        dve.tensor_scalar(xs[:, t, :], x[:, t, :], mv[:, t, 0:1], rstd[:, t:t + 1],
                                          ALU.subtract, ALU.mult).then_inc(xn_ready, 1)
                    for t in range(TT):
                        dve.wait_ge(xn_ready, b * TT + t + 1)
                        dve.tensor_tensor(xs[:, t, :], xs[:, t, :], ada[:, 0, :], ALU.mult).then_inc(xs_ready, 1)
                    for t in range(TT):
                        dve.wait_ge(xs_ready, b * 2 * TT + t + 1)
                        dve.tensor_tensor(xs[:, t, :], xs[:, t, :], ada[:, 1, :], ALU.add).then_inc(xs_ready, 1)
                    for t in range(TT):
                        dve.wait_ge(xs_ready, b * 2 * TT + TT + t + 1)
                        dve.bn_stats(stats2[:, t, :], xs[:, t, :]).then_inc(stats2_ready, 1)
                    for t in range(TT):
                        dve.wait_ge(stats2_ready, b * TT + t + 1)
                        dve.sem_inc(passed, 1)
                        dve.bn_aggr(mv2[:, t, :], stats2[:, t, :]).then_inc(mv2_ready, 1)
                    between()
                    dve.wait_ge(rstd2_ready, b + 1)
                    for t in range(TT):
                        dve.tensor_scalar(xn[:, t, :], xs[:, t, :], mv2[:, t, 0:1], rstd2[:, t:t + 1],
                                          ALU.subtract, ALU.mult).then_inc(xn2_ready, 1)

                def dbc(b, s, stored):
                    dve.wait_ge(full, st.full(b, f"DBC{s}", 0))
                    if stored is not None:
                        dve.wait_ge(b_stored, stored)
                    dve.tensor_copy(dbc_t[:, :], bank_of(f"DBC{s}", 0)[0:96, :]).then_inc(drained["dve"], 1)

                def dbc_turned(b, s):
                    dve.wait_ge(full, st.full(b, f"TC{s}", 0))
                    dve.tensor_copy(dbc_tm[:, :, :].rearrange("p t n -> p (t n)"),
                                    bank_of(f"TC{s}", 0)[:, 0:TT * 96]).then_inc(drained["dve"], 1)

                def direct():
                    for m in range(ET):
                        dp = cols[:, DPC + ET + m:DPC + ET + m + 1]
                        dve.scalar_tensor_tensor(y_sum[:, m, :], z[1][:, m, :], dp, y_sum[:, m, :],
                                                 ALU.mult, ALU.add).then_inc(u_used[1], 1)

                def softplus(b, s, index):
                    def finish(m):
                        dve.wait_ge(soft_out, 2 * (index * ET + m) + 2)
                        dve.tensor_tensor(delta[:, m, :], delta[:, m, :], soft[:, m % 2, :], ALU.max
                                          ).then_inc(delta_ready, 1)

                    for m in range(ET):
                        dve.wait_ge(full, st.full(b, f"DL{s}", m))
                        bias = cols[:, BDT + s * ET + m:BDT + s * ET + m + 1]
                        dve.tensor_scalar(delta[:, m, :], bank_of(f"DL{s}", m)[:, :], bias, None, ALU.add
                                          ).then_inc(drained["dve"], 1)
                        if m >= 2:
                            finish(m - 2)
                        dve.wait_ge(*wait_drained(b, f"DL{s}", m))
                        if m >= 2:
                            dve.wait_ge(delta_ready, index * ET + m - 1)
                        dve.tensor_scalar(soft[:, m % 2, :], delta[:, m, :], SP_CAP, None, ALU.min
                                          ).then_inc(soft_in, 1)
                    finish(ET - 2)
                    finish(ET - 1)

                def output(b, t):
                    if t == 0:
                        dve.wait_ge(gate_loaded, b * 16)
                        dve.wait_ge(resid_loaded, b * 16)
                    dve.wait_ge(full, st.full(b, f"O{t}", 0))
                    dve.tensor_tensor(soft[:, t % 2, :], bank_of(f"O{t}", 0)[:, :], gate[:, :], ALU.mult
                                      ).then_inc(drained["dve"], 1)
                    dve.wait_ge(*wait_drained(b, f"O{t}", 0))
                    dve.tensor_tensor(x[:, t, :], x[:, t, :], soft[:, t % 2, :], ALU.add).then_inc(out_ready, 1)

                def unit(b, s, g, first=False):
                    order = slice(None, None, -1 if s else 1)

                    def scan(step, j):
                        dve.wait_ge(dbu_ready, SPARE + step + 1)
                        for e in range(GE):
                            dve.wait_ge(da_ready, step * GE + e + 1)
                            dve.tensor_tensor_scan(state[j][:, e, order], decay[e][:, order],
                                                   d_bu[j][:, e, order], 0.0, ALU.mult, ALU.add
                                                   ).then_inc(scanned, 1)

                    def add(step, n):
                        start = isinstance(n, int) and n == 0
                        for t in range(TT):
                            dve.wait_ge(turned, 1 + step * TT + t + 1)
                            at = slice(n + R + N, n + R + N + 1) if isinstance(n, int) else bass.ds(n + (R + N), 1)
                            c = dbc_tm[:, t, at]
                            if start:
                                ins = dve.tensor_scalar(acc[:, t, :], banks[2 + t][:, :], c, None, ALU.mult)
                            else:
                                dve.wait_ge(added, step * TT + t + 1)
                                ins = dve.scalar_tensor_tensor(acc[:, t, :], banks[2 + t][:, :], c, acc[:, t, :],
                                                               ALU.mult, ALU.add)
                            ins.then_inc(added, 1)

                    base = b * STEPS + (s * 2 + g) * N
                    scan(base, 0)
                    scan(base + 1, 1)
                    add(base, 0)
                    if (s, g) == (0, 0):
                        for n in range(2, N, 2):
                            scan(base + n, 0)
                            add(base + n - 1, n - 1)
                            scan(base + n + 1, 1)
                            if n % 4 == 0 and not first:
                                output(b, n // 4 - 1)
                            elif n % 4 == 0:
                                absent(st, dve, drained["dve"], "dve", b, f"O{n // 4 - 1}", 1)
                            add(base + n, n)
                    else:
                        with dve.Fori(1, N // 2) as pair:
                            n = pair * 2
                            scan(base + n, 0)
                            add(base + n - 1, n - 1)
                            scan(base + n + 1, 1)
                            add(base + n, n)
                    add(base + N - 1, N - 1)
                    if (s, g) == (0, 0) and not first:
                        output(b, PARTS - 1)
                    elif (s, g) == (0, 0):
                        absent(st, dve, drained["dve"], "dve", b, f"O{PARTS - 1}", 1)

                def sums(b, s, g):
                    for e in range(GE):
                        dve.wait_ge(full, st.full(b, f"Y{s}{g}", e))
                        dve.tensor_tensor(y_sum[:, g * GE + e, :], bank_of(f"Y{s}{g}", e)[:, :],
                                          y_sum[:, g * GE + e, :], ALU.add).then_inc(drained["dve"], 1)

                def gating(b, g):
                    dve.wait_ge(*wait_drained(b, f"Y1{g}", GE - 1))
                    for m in range(g * GE, (g + 1) * GE):
                        dve.wait_ge(silu_ready, b * ET + m + 1)
                        dve.tensor_tensor(mx[:, m, :], y_sum[:, m, :], mx[:, m, :], ALU.mult).then_inc(gated, 1)

                def deltas(b, sums):
                    dbc(b, 0, None if isinstance(b, int) and b < 0 else b * 32 + 32)
                    sums()
                    dbc_turned(b, 0)
                    softplus(b, 0, (b + 1) * 2)
                    dve.wait_ge(*wait_drained(b, "TC0", 0))

                def last_sums(b):
                    sums(b, 1, 1)
                    gating(b, 1)

                def before():
                    around_front(dve, drained["dve"], "dve", lambda: norms(0), lambda: None, deltas)

                def body(b, first, last):
                    unit(b, 0, 0, first)
                    dve.wait_ge(u_used[0], (b + 1) * ET)
                    sums(b, 0, 0)
                    unit(b, 0, 1)

                    def between():
                        dbc(b, 1, b * 32 + 16)
                        sums(b, 0, 1)

                    if last:
                        between()
                    else:
                        norms(b + 1, between)
                    dve.wait_ge(*wait_drained(b, "Y01", GE - 1))
                    dve.wait_ge(*wait_drained(b, "DBC1", 0))
                    dve.wait_ge(drained["act"], st.drained(b, f"Z1{PARTS - 1}", 1)[1])
                    direct()
                    dbc_turned(b, 1)
                    softplus(b, 1, b * 2 + 1)
                    dve.wait_ge(*wait_drained(b, "TC1", 0))
                    dve.wait_ge(u_used[1], (b + 1) * ET)
                    unit(b, 1, 0)
                    sums(b, 1, 0)
                    unit(b, 1, 1)
                    gating(b, 0)
                    if last:
                        absent(st, dve, drained["dve"], "dve", b, "DBC0", 1)
                        last_sums(b)
                        absent(st, dve, drained["dve"], "dve", b, "TC0", 2)
                    else:
                        deltas(b, lambda: last_sums(b))

                def after():
                    for t in range(TT):
                        output(B, t)

                batches(dve, before, body, after)


def program(nc, d, out):
    with ExitStack() as ctx:
        banks = [ctx.enter_context(nc.psum_tensor(f"bank{i}", [P, 512], F32)) for i in range(8)]
        sb = lambda n, s: ctx.enter_context(nc.sbuf_tensor(n, s, F32))
        mod_all = {"gain": sb("gain", [P, 3, DT, B]), "shift": sb("shift", [P, 3, DT, B]),
                   "ssm_cols": sb("ssm_cols", [P, 72]), "bzc": sb("bzc", [P, 16])}
        d = dict(d)
        for name, shape in (("wzc", [2, D, E]), ("ada_d", [B, 3 * D]), ("b_d", [2, N, T]),
                            ("x1", [B, T, D]), ("x2", [B, T, D]), ("x3", [B, T, D]),
                            ("resid_d", [B, T, D])):
            d[name] = nc.dram_tensor(name, shape, F32, kind="Internal").ap()
        d["b_flat"] = d["b_d"].rearrange("s n t -> s (n t)")
        cols_loaded = ctx.enter_context(nc.semaphore("cols_loaded"))
        with nc.Block() as block:

            @block.sync
            def _(sp):
                sp.dma_start(mod_all["ssm_cols"][:, :], d["ssm_cols"]).then_inc(cols_loaded, 16)
                sp.wait_ge(cols_loaded, 16)

        sems = LayerSemaphores(nc)
        prologue(nc, sems, d, mod_all, banks)
        sems.clear()
        attention_layer(nc, sems, d, mod_all, banks, 0, d["x"], d["x1"])
        sems.clear()
        attention_layer(nc, sems, d, mod_all, banks, 1, d["x1"], d["x2"])
        sems.clear()
        attention_layer(nc, sems, d, mod_all, banks, 2, d["x2"], d["x3"])
        sems.clear()
        ssm_layer(nc, sems, d, mod_all, banks, d["x3"], out)


def kernel(**inputs):
    import numpy as np
    import concourse.bacc as bacc
    from concourse.bass_utils import run_bass_kernel_spmd

    v = {k: np.asarray(a) for k, a in inputs.items()}
    col = lambda a: a.reshape(-1, P).T
    layers = [
        dict(n="L0_cond_", nw="norm_scale", nb="norm_bias", wq="Wq", wk="Wk", wv="Wv", wo="film_out_W", bq="bq",
             bk="bk", bv="bv", bo="film_out_b", mw="film_emb_W", mb="film_emb_b", n2w="film_norm_scale",
             n2b="film_norm_bias"),
        dict(n="L1_cond_", nw="ln_w", nb="ln_b", wq="Wq", wk="Wk", wv="Wv", wo="W_out", bq="bq", bk="bk", bv="bv",
             bo="b_out", mw="W_emb", mb="b_emb", n2w="ln2_w", n2b="ln2_b"),
        dict(n="L2_cond_", nw="norm_w", nb="norm_b", wq="q_w", wk="k_w", wv="v_w", wo="out_w", bq="q_b", bk="k_b",
             bv="v_b", bo="out_b", mw="emb_w", mb="emb_b", n2w="sb_norm_w", n2b="sb_norm_b"),
    ]
    g = lambda l, key: v[l["n"] + l[key]]
    s = lambda key: v["L3_cond_" + key]
    arrays = {
        "x": v["x"],
        "cond": v["cond_2048"],
        "ident": np.eye(P, dtype=np.float32),
        "block_masks": np.stack([np.kron(np.eye(P // w), np.ones((w, w))) for w in (32, 64)], 1).astype(np.float32),
        "att_w": np.stack([np.stack([g(l, k) for k in ("wq", "wk", "wv", "wo")]) for l in layers]),
        "mod_w": np.stack([g(l, "mw") for l in layers]),
        "att_cols": np.stack([np.concatenate([col(a) for a in (g(l, "nw"), g(l, "nb"), g(l, "bq"), g(l, "bk"),
                                                               g(l, "mb")[:D], g(l, "mb")[D:], g(l, "n2w"),
                                                               g(l, "n2b"))], 1) for l in layers], 1),
        "att_rows": np.stack([np.concatenate([g(l, "bq"), g(l, "bv"), g(l, "bo")]) for l in layers]),
        "ada_wT": s("Wada").T,
        "ada_rows": np.concatenate([s("norm1_g"), s("norm1_b"), s("bada")])[None],
        "wz": s("Wz"),
        "wcT": np.stack([s("Wc1").T, s("Wc2").T]),
        "wxT": s("Wx").T,
        "wfT": s("Wf").T,
        "wdbcT": np.stack([s("Wdbc1").T, s("Wdbc2").T]),
        "wdtT": np.stack([s("Wdt1").T, s("Wdt2").T]),
        "alog": np.stack([s("Alog1"), s("Alog2")]).reshape(2, ET, P, N).transpose(2, 0, 1, 3).reshape(P, -1),
        "ssm_cols": np.concatenate([col(s(k)) for k in ("norm2_g", "norm2_b", "bx", "bc1", "bc2", "bz", "bdt1",
                                                        "bdt2", "Dp1", "Dp2")], 1),
        "bf_row": s("bf")[None],
    }
    for i, key in enumerate(("mask_BxS_ik0", "mask_BxSx1_fk1", "mask_BxS_ff1")):
        m = v[key].reshape(B, T)
        arrays[f"mask{i}"] = m[:, None]
        arrays[f"mask{i}_t"] = m.reshape(B * TT, P).T
    nc = bacc.Bacc("TRN2", target_bir_lowering=False, num_devices=1)
    maps, d = {}, {}
    for name, a in arrays.items():
        a = np.ascontiguousarray(a)
        maps["in_" + name] = a
        d[name] = nc.dram_tensor("in_" + name, a.shape, mybir.dt.from_np(a.dtype), kind="ExternalInput").ap()
    out = nc.dram_tensor("out_0", (B, T, D), F32, kind="ExternalOutput").ap()
    program(nc, d, out)
    r = run_bass_kernel_spmd(nc, [maps], core_ids=[0])
    return r.results[0]["out_0"]
```
